# Optimizing a Trainium2 kernel written in Bass

```python
import numpy as np
import jax
import jax.numpy as jnp

def _softmax(x, axis=-1):
    return jax.nn.softmax(x, axis=axis)

def _gelu(x):
    return jax.nn.gelu(x, approximate=True)

def _silu(x):
    return jax.nn.silu(x)

def _sigmoid(x):
    return jax.nn.sigmoid(x)

def _layernorm(x, axis=-1, eps=1e-05):
    m = jnp.mean(x, axis=axis, keepdims=True)
    v = jnp.var(x, axis=axis, keepdims=True)
    return (x - m) / jnp.sqrt(v + eps)

def _scatter_add(tgt, idx, src, axis=0):
    return tgt.at[idx].add(src)

def _segment_sum(src, seg, n):
    return jax.ops.segment_sum(src, seg, n)
kernel_name = 'mk_audio_tower_d1_tok_aud1d768_r4_ac8391'

def setup_inputs(seed: int=0):
    np.random.seed(seed)
    _w = jnp.asarray

    def _rec_inputs():
        import jax
        import jax.numpy as jnp
        _rk = jax.random.key(seed)
        x = -6.41493e-05 + 1.00002 * jax.random.normal(jax.random.fold_in(_rk, 1), (64, 40000), jnp.float32)
        return x
    x = _rec_inputs()

    def _L0_tok_setup():
        import jax, jax.numpy as jnp
        import numpy as np
        import math
        SR = 4000
        FRAME_LEN = 100
        FRAME_STEP = 160
        N_FILTERS = 40
        N_MFCC = 13
        EMBED = 192
        BATCH = 64
        AUDIO_LEN = 40000
        N_FFT_BINS = FRAME_LEN // 2 + 1

        def _mel_filterbank():
            low_mel = 2595.0 * math.log10(1.0 + 0.0 / 700.0)
            high_mel = 2595.0 * math.log10(1.0 + SR // 2 / 700.0)
            mel_points = np.linspace(low_mel, high_mel, N_FILTERS + 2)
            hz_points = 700.0 * (10.0 ** (mel_points / 2595.0) - 1.0)
            bin_points = np.floor((FRAME_LEN + 1) * hz_points / SR)
            filt = np.zeros((N_FILTERS, N_FFT_BINS), dtype=np.float32)
            for i in range(1, N_FILTERS + 1):
                l, c, r = (bin_points[i - 1], bin_points[i], bin_points[i + 1])
                for j in range(int(l), int(c)):
                    filt[i - 1, j] = (j - l) / (c - l)
                for j in range(int(c), int(r)):
                    filt[i - 1, j] = (r - j) / (r - c)
            return jnp.asarray(filt)

        def _dct_matrix():
            k = np.arange(N_MFCC)[:, None]
            j = np.arange(N_FILTERS)[None, :]
            m = np.cos(np.pi * k * (2 * j + 1) / (2 * N_FILTERS)) * math.sqrt(2.0 / N_FILTERS)
            return jnp.asarray(m.astype(np.float32))
        key = jax.random.key(seed)
        kx, kw = jax.random.split(key)
        x = jax.random.normal(kx, (BATCH, AUDIO_LEN), dtype=jnp.float32)
        bound = 1.0 / math.sqrt(N_MFCC)
        w_proj = jax.random.uniform(kw, (N_MFCC, EMBED), minval=-bound, maxval=bound, dtype=jnp.float32)
        b_proj = jnp.zeros((EMBED,), dtype=jnp.float32)
        return {'x': x, 'mel_filters': _mel_filterbank(), 'dct': _dct_matrix(), 'w_proj': w_proj, 'b_proj': b_proj}
    _L0_tok_all = _L0_tok_setup()
    _L0_tok_in = {k: v for k, v in _L0_tok_all.items() if k in ('mel_filters', 'dct', 'w_proj', 'b_proj')}
    del _L0_tok_all

    def _L0_attn_setup():
        import jax, jax.numpy as jnp
        import numpy as np
        EPS = 1e-06
        H = 12

        def _phi(x):
            return jax.nn.elu(x) + 1.0
        key = jax.random.key(seed)
        k1, k2, k3 = jax.random.split(key, 3)
        B, N, D = (32, 256, 192)
        x = jax.random.normal(k1, (B, N, D), dtype=jnp.float32)
        W_qkv = jax.random.normal(k2, (D, 3 * D), dtype=jnp.float32) * D ** (-0.5)
        W_out = jax.random.normal(k3, (D, D), dtype=jnp.float32) * D ** (-0.5)
        b_out = jnp.zeros((D,), dtype=jnp.float32)
        return {'x': x, 'W_qkv': W_qkv, 'W_out': W_out, 'b_out': b_out}
    _L0_attn_all = _L0_attn_setup()
    _L0_attn_in = {k: v for k, v in _L0_attn_all.items() if k in ('W_qkv', 'W_out', 'b_out')}
    del _L0_attn_all

    def _L0_ffn_setup():
        import math
        import jax, jax.numpy as jnp
        import numpy as np
        B, L, D = (8, 1024, 192)
        E = 16
        TOP_K = 2
        F_EXP = 4 * D
        F_SH = F_EXP * 2 // 4
        key = jax.random.key(seed)
        ks = jax.random.split(key, 8)
        s = lambda fan_in: 1.0 / math.sqrt(fan_in)
        return {'hidden_states': jax.random.normal(ks[0], (B, L, D), jnp.float32), 'gate_weight': jax.random.uniform(ks[1], (E, D), jnp.float32, -s(D), s(D)), 'Wg': jax.random.uniform(ks[2], (E, F_EXP, D), jnp.float32, -s(D), s(D)), 'Wu': jax.random.uniform(ks[3], (E, F_EXP, D), jnp.float32, -s(D), s(D)), 'Wd': jax.random.uniform(ks[4], (E, D, F_EXP), jnp.float32, -s(F_EXP), s(F_EXP)), 'Ws_g': jax.random.uniform(ks[5], (F_SH, D), jnp.float32, -s(D), s(D)), 'Ws_u': jax.random.uniform(ks[6], (F_SH, D), jnp.float32, -s(D), s(D)), 'Ws_d': jax.random.uniform(ks[7], (D, F_SH), jnp.float32, -s(F_SH), s(F_SH))}
    _L0_ffn_all = _L0_ffn_setup()
    _L0_ffn_in = {k: v for k, v in _L0_ffn_all.items() if k in ('gate_weight', 'Wg', 'Wu', 'Wd', 'Ws_g', 'Ws_u', 'Ws_d')}
    del _L0_ffn_all
    return {'x': x, 'L0_tok_mel_filters': _L0_tok_in['mel_filters'], 'L0_tok_dct': _L0_tok_in['dct'], 'L0_tok_w_proj': _L0_tok_in['w_proj'], 'L0_tok_b_proj': _L0_tok_in['b_proj'], 'L0_attn_W_qkv': _L0_attn_in['W_qkv'], 'L0_attn_W_out': _L0_attn_in['W_out'], 'L0_attn_b_out': _L0_attn_in['b_out'], 'L0_ffn_gate_weight': _L0_ffn_in['gate_weight'], 'L0_ffn_Wg': _L0_ffn_in['Wg'], 'L0_ffn_Wu': _L0_ffn_in['Wu'], 'L0_ffn_Wd': _L0_ffn_in['Wd'], 'L0_ffn_Ws_g': _L0_ffn_in['Ws_g'], 'L0_ffn_Ws_u': _L0_ffn_in['Ws_u'], 'L0_ffn_Ws_d': _L0_ffn_in['Ws_d']}

def reference(x, L0_tok_mel_filters, L0_tok_dct, L0_tok_w_proj, L0_tok_b_proj, L0_attn_W_qkv, L0_attn_W_out, L0_attn_b_out, L0_ffn_gate_weight, L0_ffn_Wg, L0_ffn_Wu, L0_ffn_Wd, L0_ffn_Ws_g, L0_ffn_Ws_u, L0_ffn_Ws_d):
    import jax
    import jax.numpy as jnp

    def _L0_tok_ref(x, mel_filters, dct, w_proj, b_proj):
        import jax, jax.numpy as jnp
        import numpy as np
        import math
        SR = 4000
        FRAME_LEN = 100
        FRAME_STEP = 160
        N_FILTERS = 40
        N_MFCC = 13
        EMBED = 192
        BATCH = 64
        AUDIO_LEN = 40000
        N_FFT_BINS = FRAME_LEN // 2 + 1

        def _mel_filterbank():
            low_mel = 2595.0 * math.log10(1.0 + 0.0 / 700.0)
            high_mel = 2595.0 * math.log10(1.0 + SR // 2 / 700.0)
            mel_points = np.linspace(low_mel, high_mel, N_FILTERS + 2)
            hz_points = 700.0 * (10.0 ** (mel_points / 2595.0) - 1.0)
            bin_points = np.floor((FRAME_LEN + 1) * hz_points / SR)
            filt = np.zeros((N_FILTERS, N_FFT_BINS), dtype=np.float32)
            for i in range(1, N_FILTERS + 1):
                l, c, r = (bin_points[i - 1], bin_points[i], bin_points[i + 1])
                for j in range(int(l), int(c)):
                    filt[i - 1, j] = (j - l) / (c - l)
                for j in range(int(c), int(r)):
                    filt[i - 1, j] = (r - j) / (r - c)
            return jnp.asarray(filt)

        def _dct_matrix():
            k = np.arange(N_MFCC)[:, None]
            j = np.arange(N_FILTERS)[None, :]
            m = np.cos(np.pi * k * (2 * j + 1) / (2 * N_FILTERS)) * math.sqrt(2.0 / N_FILTERS)
            return jnp.asarray(m.astype(np.float32))
        B, T = x.shape
        n_frames = 1 + (T - FRAME_LEN) // FRAME_STEP
        idx = jnp.arange(n_frames)[:, None] * FRAME_STEP + jnp.arange(FRAME_LEN)[None, :]
        frames = x[:, idx]
        window = 0.54 - 0.46 * jnp.cos(2.0 * jnp.pi * jnp.arange(FRAME_LEN, dtype=jnp.float32) / (FRAME_LEN - 1))
        windowed = frames * window
        fft = jnp.fft.rfft(windowed, axis=-1)
        power = fft.real ** 2 + fft.imag ** 2
        mel_energies = jnp.einsum('bnf,mf->bnm', power, mel_filters)
        log_energies = jnp.log(mel_energies + 1e-06)
        mfcc = jnp.einsum('bnm,km->bnk', log_energies, dct)
        out = mfcc @ w_proj + b_proj
        return out

    def _L0_attn_ref(x, W_qkv, W_out, b_out):
        import jax, jax.numpy as jnp
        import numpy as np
        EPS = 1e-06
        H = 12

        def _phi(x):
            return jax.nn.elu(x) + 1.0
        B, N, D = x.shape
        d = D // H
        x_ = jnp.pad(x, ((0, 0), (0, 1), (0, 0)))
        qkv = x_ @ W_qkv
        q, k, v = jnp.split(qkv, 3, axis=-1)
        q = q.reshape(B, N + 1, H, d)
        k = k.reshape(B, N + 1, H, d)
        v = v.reshape(B, N + 1, H, d)
        q = _phi(q)
        k = _phi(k)
        kv = jnp.einsum('bshd,bshm->bhdm', k, v)
        z = 1.0 / (jnp.einsum('blhd,bhd->blh', q, k.sum(axis=1)) + EPS)
        out = jnp.einsum('blhd,bhdm,blh->blhm', q, kv, z)
        out = out.reshape(B, N + 1, D)
        out = out @ W_out + b_out
        return out[:, :-1, :]

    def _L0_ffn_ref(hidden_states, gate_weight, Wg, Wu, Wd, Ws_g, Ws_u, Ws_d):
        import math
        import jax, jax.numpy as jnp
        import numpy as np
        B, L, D = (8, 1024, 192)
        E = 16
        TOP_K = 2
        F_EXP = 4 * D
        F_SH = F_EXP * 2 // 4
        b, l, d = hidden_states.shape
        n = b * l
        x = hidden_states.reshape(n, d)
        scores = jax.nn.sigmoid(x @ gate_weight.T)
        capacity = math.ceil(n / E * TOP_K)
        topk_score, topk_ids = jax.lax.top_k(scores.T, capacity)
        xg = x[topk_ids]
        gate = jax.nn.silu(jnp.einsum('ecd,efd->ecf', xg, Wg))
        up = jnp.einsum('ecd,efd->ecf', xg, Wu)
        out = jnp.einsum('ecf,edf->ecd', gate * up, Wd)
        out = out * topk_score[..., None]
        y = jnp.zeros((n, d), x.dtype).at[topk_ids.reshape(-1)].add(out.reshape(-1, d))
        y = y.reshape(b, l, d)
        shared = jax.nn.silu(hidden_states @ Ws_g.T) * (hidden_states @ Ws_u.T) @ Ws_d.T
        return y + shared
    h = _L0_tok_ref(x, L0_tok_mel_filters, L0_tok_dct, L0_tok_w_proj, L0_tok_b_proj)
    h = h + _L0_attn_ref(_layernorm(h, axis=-1), L0_attn_W_qkv, L0_attn_W_out, L0_attn_b_out)
    h = h + _L0_ffn_ref(_layernorm(h, axis=-1), L0_ffn_gate_weight, L0_ffn_Wg, L0_ffn_Wu, L0_ffn_Wd, L0_ffn_Ws_g, L0_ffn_Ws_u, L0_ffn_Ws_d)
    return h

_drawn_inputs = setup_inputs


def setup_inputs(seed=0):
    import zlib

    import numpy as np

    out = dict(_drawn_inputs(seed))
    spreads = {'L0_tok_b_proj': (0.0, 0.326), 'L0_attn_b_out': (0.0, 0.335)}
    factors = {'L0_ffn_gate_weight': 2.821}
    for name, (base, spread) in spreads.items():
        noise = np.random.default_rng([zlib.crc32(name.encode()), seed]).standard_normal(out[name].shape)
        drawn = base * np.exp(spread * noise) if base else spread * noise
        out[name] = jnp.asarray(drawn.astype(out[name].dtype))
    for name, factor in factors.items():
        out[name] = (out[name] * factor).astype(out[name].dtype)
    return out
```

```python
from collections import namedtuple
from contextlib import ExitStack

import concourse.bass as bass
from concourse import mybir

F32 = mybir.dt.float32
F32R = mybir.dt.float32r
BF16 = mybir.dt.bfloat16
I32 = mybir.dt.int32
U32 = mybir.dt.uint32
ALU = mybir.AluOpType
ACT = mybir.ActivationFunctionType

BATCH, FRAMES, FRAME = 64, 250, 100
BINS = 2 * (FRAME // 2 + 1)
MEL = 40
D = 192
DA, DB = 128, 64
HEADS, DH = 12, 16
EXPERTS = 16
FE, FS = 768, 384
TOKENS = BATCH * FRAMES
CAP = 2000
P = 125
TILES = TOKENS // P
GT = 4
G = GT * P
GROUPS = TOKENS // G
ROW = D + EXPERTS
CHUNKS = 128 // EXPERTS
CT = TILES // CHUNKS
CLEN = CT * P
EPS_LOG, EPS_LN, EPS_ATT = 1e-6, 1e-5, 1e-6
ROUND = float(3 << 22)

Group = namedtuple("Group", "n half par known")


def wait(eng, sem, per, g, off=0, less=0):
    if g.known and per * (g.n - less) + off <= 0:
        return
    eng.wait_ge(sem, (g.n - less) * per + off)


def apart(eng):
    eng.nop(nofuse=True)


def skewed(eng, step):
    def groups(n, half, par, known):
        out = []
        for s in range(3):
            gpar = (par - s) % 2
            gh = half + (par - s - gpar) // 2
            out.append(Group(n - s, gh, gpar, known) if not known or 0 <= n - s < GROUPS else None)
        return out

    for it in range(4):
        step(groups(it, it // 2, it % 2, True))
    with eng.Fori(0, (GROUPS - 4) // 2) as i:
        for par in range(2):
            step(groups(i * 2 + (4 + par), i + 2, par, False))
    for it in range(GROUPS, GROUPS + 2):
        step(groups(it, it // 2, it % 2, True))


def tower_phase(nc, io, resident):
    scores_tm, ident = resident["scores_tm"], resident["ident"]
    with ExitStack() as ctx:
        def sb(name, shape, dt=F32):
            return ctx.enter_context(nc.sbuf_tensor(name, shape, dt))

        def sem(name):
            return ctx.enter_context(nc.semaphore(name))

        bank = [ctx.enter_context(nc.psum_tensor(f"bank{i}", [128, 512], F32)) for i in range(8)]

        dft = sb("dft", [FRAME, BINS])
        mel = sb("mel", [BINS, MEL])
        dctT = sb("dctT", [13, MEL])
        wproj = sb("wproj", [13, D])
        cproj = sb("cproj", [MEL + 1, D])
        wqkv_a, wqkv_b = sb("wqkv_a", [DA, 3 * D]), sb("wqkv_b", [DB, 3 * D])
        wout_a, wout_b = sb("wout_a", [DA, D]), sb("wout_b", [DB + 1, D])
        gate_a, gate_b = sb("gate_a", [DA, EXPERTS]), sb("gate_b", [DB, EXPERTS])
        wsg_a, wsg_b = sb("wsg_a", [DA, FS]), sb("wsg_b", [DB, FS])
        wsu_a, wsu_b = sb("wsu_a", [DA, FS]), sb("wsu_b", [DB, FS])
        wsd = sb("wsd", [128, FS // 128, D])
        same_a, same_b = sb("same_a", [DA, D]), sb("same_b", [DB, D])
        head_a, head_b = sb("head_a", [DA, HEADS]), sb("head_b", [DB, HEADS])
        eps_log, eps_ln = sb("eps_log", [MEL, 1]), sb("eps_ln", [P, 1])

        frames = [sb(f"frames{i}", [FRAME, G]) for i in range(2)]
        power = sb("power", [BINS, G])
        logmel = sb("logmel", [MEL + 1, G])
        h = [sb(f"h{i}", [P, GT, D]) for i in range(2)]
        stats = sb("stats", [P, GT, 6])
        mv = sb("mv", [P, GT, 2])
        lnv, rstd = sb("lnv", [P, GT]), sb("rstd", [P, GT])
        stats2 = sb("stats2", [P, GT, 6])
        mv2 = sb("mv2", [P, GT, 2])
        lnv2, rstd2 = sb("lnv2", [P, GT]), sb("rstd2", [P, GT])
        xn = sb("xn", [P, GT, D])
        xT_a, xT_b = sb("xT_a", [DA, G]), sb("xT_b", [DB, G])
        expq_a, expq_b = sb("expq_a", [DA, G]), sb("expq_b", [DB, G])
        expk = sb("expk", [P, GT, D])
        q_a = [sb(f"q_a{i}", [DA, G]) for i in range(2)]
        q_b = [sb(f"q_b{i}", [DB, G]) for i in range(2)]
        k = [sb(f"k{i}", [P, GT, D]) for i in range(2)]
        v = [sb(f"v{i}", [P, GT, D + 1]) for i in range(2)]
        kv_a, kv_b = sb("kv_a", [DA, 2, D + HEADS]), sb("kv_b", [DB, 2, D + HEADS])
        ks_a, ks_b = sb("ks_a", [DA, 2]), sb("ks_b", [DB, 2])
        den, z = sb("den", [P, GT, HEADS]), sb("z", [P, GT, HEADS])
        o = sb("o", [P, GT, D])
        oT_a, oT_b = sb("oT_a", [DA, G]), sb("oT_b", [DB + 1, G])
        h1 = [sb(f"h1_{i}", [P, GT, D]) for i in range(2)]
        row = [sb(f"row{i}", [P, GT, ROW]) for i in range(2)]
        x2T_a, x2T_b = sb("x2T_a", [DA, G]), sb("x2T_b", [DB, G])
        exps, sig = sb("exps", [P, GT, EXPERTS]), sb("sig", [P, GT, EXPERTS])
        silu = [sb(f"silu{i}", [128, G]) for i in range(2)]
        hs = sb("hs", [128, FS // 128, G])
        y = [sb(f"y{i}", [P, GT, D]) for i in range(2)]

        consts_in, consts_set, cproj_mm, cproj_set = sem("consts_in"), sem("consts_set"), sem("cproj_mm"), sem("cproj_set")
        frames_in = [sem(f"frames_in{i}") for i in range(2)]
        dft_done, power_ready, mel_done, logmel_ready, proj_done = (sem(n) for n in (
            "dft_done", "power_ready", "mel_done", "logmel_ready", "proj_done"))
        h_ready, stats_ready, mv_ready, lnv_ready, rstd_ready, xn_ready = (sem(n) for n in (
            "h_ready", "stats_ready", "mv_ready", "lnv_ready", "rstd_ready", "xn_ready"))
        xT_done, xTa_ready, xTb_ready = sem("xT_done"), sem("xTa_ready"), sem("xTb_ready")
        q_done, kv_done, expq_ready, expk_ready = sem("q_done"), sem("kv_done"), sem("expq_ready"), sem("expk_ready")
        minq_ready, mink_ready, q_ready, k_ready, v_ready = (sem(n) for n in (
            "minq_ready", "mink_ready", "q_ready", "k_ready", "v_ready"))
        ktv_done, ks_ready, kvm_ready = sem("ktv_done"), sem("ks_ready"), sem("kvm_ready")
        att_done, den_ready, z_ready, o_ready = sem("att_done"), sem("den_ready"), sem("z_ready"), sem("o_ready")
        oT_done, oTa_ready, oTb_ready, wo_done = sem("oT_done"), sem("oTa_ready"), sem("oTb_ready"), sem("wo_done")
        h1_ready, stats2_ready, mv2_ready, lnv2_ready, rstd2_ready, x2_ready = (sem(n) for n in (
            "h1_ready", "stats2_ready", "mv2_ready", "lnv2_ready", "rstd2_ready", "x2_ready"))
        x2T_done, x2Ta_ready, x2Tb_ready = sem("x2T_done"), sem("x2Ta_ready"), sem("x2Tb_ready")
        router_done, exps_ready, sig1_ready, sig_ready, scores_ready = (sem(n) for n in (
            "router_done", "exps_ready", "sig1_ready", "sig_ready", "scores_ready"))
        gu_done, silu_ready, hs_ready, down_done, y_ready = (sem(n) for n in (
            "gu_done", "silu_ready", "hs_ready", "down_done", "y_ready"))
        rows_out = [sem(f"rows_out{i}") for i in range(2)]
        y_out = [sem(f"y_out{i}") for i in range(2)]

        loads = [
            (dft, io["dft"]), (mel, io["mel"]), (dctT, io["dct"]), (wproj, io["w_proj"]),
            (cproj[MEL:MEL + 1, :], io["b_proj"]),
            (wqkv_a, io["wqkv"][0:DA, :]), (wqkv_b, io["wqkv"][DA:D, :]),
            (wout_a, io["wout"][0:DA, :]), (wout_b[0:DB, :], io["wout"][DA:D, :]),
            (wout_b[DB:DB + 1, :], io["b_out"]),
            (gate_a, io["gateT"][0:DA, :]), (gate_b, io["gateT"][DA:D, :]),
            (wsg_a, io["wsgT"][0:DA, :]), (wsg_b, io["wsgT"][DA:D, :]),
            (wsu_a, io["wsuT"][0:DA, :]), (wsu_b, io["wsuT"][DA:D, :]),
            (wsd, io["wsdT"].rearrange("(c p) n -> p c n", p=128)),
            (same_a, io["same_head"][0:DA, :]), (same_b, io["same_head"][DA:D, :]),
            (head_a, io["head_of"][0:DA, :]), (head_b, io["head_of"][DA:D, :]),
            (ident, io["ident"]),
        ]
        block = ctx.enter_context(nc.Block())

        @block.sync
        def _(sp):
            for dst, src in loads:
                sp.dma_start(dst if isinstance(dst, bass.AP) else dst[tuple(slice(None) for _ in dst.shape)], src).then_inc(consts_in, 16)

            def step(gs):
                g, _, g3 = gs
                if g:
                    wait(sp, dft_done, 1, g, less=1)
                    sp.dma_start(frames[g.par][:, :], io["framesT"][:, bass.ds(g.n * G, G)]).then_inc(frames_in[g.par], 16)
                if g3:
                    wait(sp, scores_ready, 1, g3, 1)
                    sp.dma_start(io["rows"][bass.ds(g3.n * G, G), :].rearrange("(j p) c -> p j c", p=P),
                                 row[g3.par][:, :, :]).then_inc(rows_out[g3.par], 16)
                    wait(sp, y_ready, 1, g3, 1)
                    sp.dma_start(io["out"][bass.ds(g3.n * G, G), :].rearrange("(j p) c -> p j c", p=P),
                                 y[g3.par][:, :, :]).then_inc(y_out[g3.par], 16)

            skewed(sp, step)
            for i in range(2):
                sp.wait_ge(rows_out[i], 16 * (GROUPS // 2))
                sp.wait_ge(y_out[i], 16 * (GROUPS // 2))

        @block.tensor
        def _(pe):
            pe.wait_ge(consts_in, 16 * len(loads))
            nc.tensor.matmul(bank[0][0:MEL, 0:D], dctT[:, :], wproj[:, :], start=True, stop=True).then_inc(cproj_mm, 1)
            pe.wait_ge(cproj_set, 1)
            pe.wait_ge(consts_set, 6)

            def spectrum(g):
                pe.wait_ge(frames_in[g.par], (g.half + 1) * 16)
                wait(pe, v_ready, 4, g)
                wait(pe, k_ready, 4, g)
                nc.tensor.matmul(bank[0][0:BINS, 0:G], dft[:, :], frames[g.par][:, :], start=True, stop=True).then_inc(dft_done, 1)

            def filterbank(g):
                wait(pe, power_ready, 1, g, 1)
                nc.tensor.matmul(bank[1][0:MEL, 0:G], mel[:, :], power[:, :], start=True, stop=True).then_inc(mel_done, 1)

            def project(g):
                wait(pe, logmel_ready, 1, g, 1)
                for j in range(GT):
                    last = nc.tensor.matmul(bank[0 if j < 2 else 2][0:P, (j % 2) * D:(j % 2 + 1) * D],
                                            logmel[:, j * P:(j + 1) * P], cproj[:, :], start=True, stop=True)
                last.then_inc(proj_done, 1)

            def transpose(src, to_a, to_b, done):
                for j in range(GT):
                    nc.tensor.transpose(to_a[0:DA, j * P:(j + 1) * P], src[:, j, 0:DA], ident[0:P, 0:P])
                for j in range(GT):
                    last = nc.tensor.transpose(to_b[0:DB, j * P:(j + 1) * P], src[:, j, DA:D], ident[0:P, 0:P])
                last.then_inc(done, 1)

            def qkv(g):
                wait(pe, xTa_ready, 1, g, 1)
                wait(pe, xTb_ready, 1, g, 1)
                for to, c0, m in ((bank[2], 0, DA), (bank[0], DA, DB)):
                    nc.tensor.matmul(to[0:m, 0:G], wqkv_a[:, c0:c0 + m], xT_a[:, :], start=True, stop=False)
                    nc.tensor.matmul(to[0:m, 0:G], wqkv_b[:, c0:c0 + m], xT_b[:, :], start=False, stop=True).then_inc(q_done, 1)
                for j, to in enumerate((1, 2, 0, 1)):
                    if j in (1, 2):
                        wait(pe, q_ready, 2, g, j)
                    if j == 3:
                        wait(pe, k_ready, 4, g, 1)
                        wait(pe, v_ready, 4, g, 1)
                    cols = slice(j * P, (j + 1) * P)
                    nc.tensor.matmul(bank[to][0:P, 0:2 * D], xT_a[:, cols], wqkv_a[:, D:3 * D], start=True, stop=False)
                    nc.tensor.matmul(bank[to][0:P, 0:2 * D], xT_b[:, cols], wqkv_b[:, D:3 * D], start=False, stop=True).then_inc(kv_done, 1)

            def keys_values(g):
                wait(pe, k_ready, 4, g, 4)
                wait(pe, v_ready, 4, g, 4)
                wait(pe, h1_ready, 1, g)
                for b in range(2):
                    for j in (2 * b, 2 * b + 1):
                        nc.tensor.matmul(bank[3][0:DA, b * (D + 1):(b + 1) * (D + 1)], k[g.par][:, j, 0:DA],
                                         v[g.par][:, j, :], start=(j % 2 == 0), stop=(j % 2 == 1))
                    for j in (2 * b, 2 * b + 1):
                        last = nc.tensor.matmul(bank[4][0:DB, b * (D + 1):(b + 1) * (D + 1)], k[g.par][:, j, DA:D],
                                                v[g.par][:, j, :], start=(j % 2 == 0), stop=(j % 2 == 1))
                last.then_inc(ktv_done, 1)

            def attend(g):
                wait(pe, kvm_ready, 1, g, 1)
                wait(pe, q_ready, 2, g, 2)
                for j in range(GT):
                    to = bank[3 + j // 2][0:P, (j % 2) * (D + HEADS):(j % 2 + 1) * (D + HEADS)]
                    cols = slice(j * P, (j + 1) * P)
                    nc.tensor.matmul(to, q_a[g.par][:, cols], kv_a[:, j // 2, :], start=True, stop=False)
                    last = nc.tensor.matmul(to, q_b[g.par][:, cols], kv_b[:, j // 2, :], start=False, stop=True)
                last.then_inc(att_done, 1)

            def out_proj(g):
                wait(pe, oTa_ready, 1, g, 1)
                wait(pe, oTb_ready, 1, g, 1)
                for j in range(GT):
                    to = bank[3 + j // 2][0:P, (j % 2) * D:(j % 2 + 1) * D]
                    cols = slice(j * P, (j + 1) * P)
                    nc.tensor.matmul(to, oT_a[:, cols], wout_a[:, :], start=True, stop=False)
                    last = nc.tensor.matmul(to, oT_b[:, cols], wout_b[:, :], start=False, stop=True)
                last.then_inc(wo_done, 1)

            def router(g):
                wait(pe, x2Ta_ready, 1, g, 1)
                wait(pe, x2Tb_ready, 1, g, 1)
                for j in range(GT):
                    to = bank[7][0:P, j * EXPERTS:(j + 1) * EXPERTS]
                    cols = slice(j * P, (j + 1) * P)
                    nc.tensor.matmul(to, x2T_a[:, cols], gate_a[:, :], start=True, stop=False)
                    last = nc.tensor.matmul(to, x2T_b[:, cols], gate_b[:, :], start=False, stop=True)
                last.then_inc(router_done, 1)

            def shared_up(g, f):
                for which, (wa, wb) in enumerate(((wsg_a, wsg_b), (wsu_a, wsu_b))):
                    to = bank[(5, 6, 7, 5, 6, 7)[2 * f + which]]
                    if (f, which) == (1, 0):
                        wait(pe, exps_ready, 1, g, 1)
                    if (f, which) == (1, 1):
                        wait(pe, silu_ready, 3, g, 1)
                    if (f, which) == (2, 0):
                        wait(pe, hs_ready, 3, g, 1)
                    if (f, which) == (2, 1):
                        wait(pe, silu_ready, 3, g, 2)
                    cols = slice(f * 128, (f + 1) * 128)
                    nc.tensor.matmul(to[:, 0:G], wa[:, cols], x2T_a[:, :], start=True, stop=False)
                    nc.tensor.matmul(to[:, 0:G], wb[:, cols], x2T_b[:, :], start=False, stop=True).then_inc(gu_done, 1)

            def shared_down(g):
                wait(pe, hs_ready, 3, g, 3)
                for j in range(GT):
                    to = bank[5 + j // 2][0:P, (j % 2) * D:(j % 2 + 1) * D]
                    for f in range(FS // 128):
                        last = nc.tensor.matmul(to, hs[:, f, j * P:(j + 1) * P], wsd[:, f, :],
                                                start=(f == 0), stop=(f == FS // 128 - 1))
                last.then_inc(down_done, 1)

            def step(gs):
                g1, g2, g3 = gs
                if g1:
                    spectrum(g1)
                if g2:
                    keys_values(g2)
                if g3:
                    wait(pe, x2_ready, 1, g3, 1)
                    wait(pe, y_ready, 1, g3)
                    transpose(row[g3.par], bank[5], bank[6], x2T_done)
                if g1:
                    filterbank(g1)
                if g2:
                    attend(g2)
                if g3:
                    router(g3)
                    shared_up(g3, 0)
                if g1:
                    project(g1)
                if g3:
                    shared_up(g3, 1)
                if g2:
                    wait(pe, o_ready, 1, g2, 1)
                    transpose(o, bank[3], bank[4], oT_done)
                if g3:
                    shared_up(g3, 2)
                if g1:
                    wait(pe, xn_ready, 1, g1, 1)
                    transpose(xn, bank[1], bank[0], xT_done)
                if g2:
                    out_proj(g2)
                if g1:
                    qkv(g1)
                if g3:
                    shared_down(g3)

            skewed(pe, step)

        @block.scalar
        def _(act):
            act.wait_ge(consts_set, 6)

            def inv_std(g, mvx, lnx, rx, mv_sem, ln_sem, r_sem):
                wait(act, mv_sem, 1, g, 1)
                nc.scalar.activation(lnx[:, :], mvx[:, :, 1], ACT.Ln, bias=eps_ln[:, :]).then_inc(ln_sem, 1)
                wait(act, ln_sem, 1, g, 1)
                nc.scalar.activation(rx[:, :], lnx[:, :], ACT.Exp, scale=-0.5).then_inc(r_sem, 1)

            def gate(g, f):
                wait(act, gu_done, 6, g, 2 * f + 1)
                wait(act, hs_ready, 3, g, (0, 0, 1)[f])
                nc.scalar.activation(silu[f % 2][:, :], bank[(5, 7, 6)[f]][:, 0:G], ACT.Silu).then_inc(silu_ready, 1)

            def step(gs):
                g1, g2, g3 = gs
                if g1:
                    wait(act, dft_done, 1, g1, 1)
                    wait(act, mel_done, 1, g1)
                    nc.scalar.activation(power[:, :], bank[0][0:BINS, 0:G], ACT.Square).then_inc(power_ready, 1)
                if g3:
                    wait(act, x2T_done, 1, g3, 1)
                    wait(act, gu_done, 6, g3)
                    nc.scalar.copy(x2T_a[:, :], bank[5][:, 0:G]).then_inc(x2Ta_ready, 1)
                if g1:
                    wait(act, mel_done, 1, g1, 1)
                    wait(act, proj_done, 1, g1)
                    nc.scalar.activation(logmel[0:MEL, :], bank[1][0:MEL, 0:G], ACT.Ln, bias=eps_log[:, :]).then_inc(logmel_ready, 1)
                if g3:
                    wait(act, router_done, 1, g3, 1)
                    wait(act, sig1_ready, 1, g3)
                    nc.scalar.activation(exps[:, :, :], bank[7][0:P, 0:GT * EXPERTS].rearrange("p (j e) -> p j e", e=EXPERTS),
                                         ACT.Exp, scale=-1.0).then_inc(exps_ready, 1)
                if g3:
                    gate(g3, 0)
                if g1:
                    wait(act, proj_done, 1, g1, 1)
                    wait(act, h1_ready, 1, g1, less=1)
                    for b in range(2):
                        last = nc.scalar.copy(h[g1.par][:, 2 * b:2 * b + 2, :],
                                              bank[2 * b][0:P, 0:2 * D].rearrange("p (j c) -> p j c", c=D))
                    last.then_inc(h_ready, 1)
                    inv_std(g1, mv, lnv, rstd, mv_ready, lnv_ready, rstd_ready)
                if g2:
                    wait(act, oT_done, 1, g2, 1)
                    wait(act, wo_done, 1, g2)
                    nc.scalar.copy(oT_a[:, :], bank[3][:, 0:G]).then_inc(oTa_ready, 1)
                if g3:
                    gate(g3, 1)
                    gate(g3, 2)
                if g1:
                    wait(act, xT_done, 1, g1, 1)
                    wait(act, kv_done, 4, g1)
                    nc.scalar.copy(xT_a[:, :], bank[1][:, 0:G]).then_inc(xTa_ready, 1)
                    for n, (e, b, m) in enumerate(((expq_a, bank[2], DA), (expq_b, bank[0], DB))):
                        wait(act, q_done, 2, g1, n + 1)
                        wait(act, q_ready, 2, g1)
                        nc.scalar.activation(e[:, :], b[0:m, 0:G], ACT.Exp).then_inc(expq_ready, 1)
                    for j, b in enumerate((1, 2, 0, 1)):
                        wait(act, kv_done, 4, g1, j + 1)
                        wait(act, k_ready, 4, g1)
                        nc.scalar.activation(expk[:, j, :], bank[b][0:P, 0:D], ACT.Exp).then_inc(expk_ready, 1)
                        wait(act, ktv_done, 1, g1, less=1)
                        nc.scalar.copy(v[g1.par][:, j, 0:D], bank[b][0:P, D:2 * D]).then_inc(v_ready, 1)
                if g2:
                    inv_std(g2, mv2, lnv2, rstd2, mv2_ready, lnv2_ready, rstd2_ready)

            skewed(act, step)

        @block.vector
        def _(dve):
            nc.vector.memset(eps_log[:, :], EPS_LOG).then_inc(consts_set, 1)
            nc.vector.memset(eps_ln[:, :], EPS_LN).then_inc(consts_set, 1)
            nc.vector.memset(logmel[:, :], 1.0).then_inc(consts_set, 1)
            nc.vector.memset(oT_b[DB:DB + 1, :], 1.0).then_inc(consts_set, 1)
            for i in range(2):
                nc.vector.memset(v[i][:, :, D:D + 1], 1.0).then_inc(consts_set, 1)
            dve.wait_ge(cproj_mm, 1)
            nc.vector.tensor_copy(cproj[0:MEL, :], bank[0][0:MEL, 0:D]).then_inc(cproj_set, 1)

            def moments(g, src, st, mvx, st_sem, mv_sem):
                for j in range(GT):
                    last = nc.vector.bn_stats(st[:, j, :], src(j))
                last.then_inc(st_sem, 1)
                wait(dve, st_sem, 1, g, 1)
                apart(dve)
                for j in range(GT):
                    last = nc.vector.bn_aggr(mvx[:, j, :], st[:, j, :])
                last.then_inc(mv_sem, 1)

            def relu_plus(g, to, src, e, exp_sem, per, off, min_sem, done):
                wait(dve, exp_sem, per, g, off)
                nc.vector.tensor_scalar(e, e, 1.0, None, ALU.min).then_inc(min_sem, 1)
                wait(dve, min_sem, per, g, off)
                nc.vector.scalar_tensor_tensor(out=to, in0=src, scalar=0.0, in1=e, op0=ALU.max, op1=ALU.add).then_inc(done, 1)

            def step(gs):
                g1, g2, g3 = gs
                if g2:
                    wait(dve, ktv_done, 1, g2, 1)
                    wait(dve, att_done, 1, g2)
                    for kvx, ksx, b, m, same in ((kv_a, ks_a, bank[3], DA, same_a), (kv_b, ks_b, bank[4], DB, same_b)):
                        both = b[0:m, 0:2 * (D + 1)].rearrange("p (b c) -> p b c", b=2)
                        nc.vector.tensor_tensor(kvx[:, :, 0:D], both[:, :, 0:D],
                                                same[:, None, :].to_broadcast([m, 2, D]), ALU.mult)
                        last = nc.vector.tensor_scalar(ksx[:, :], both[:, :, D], 1.0, None, ALU.add)
                    last.then_inc(ks_ready, 1)
                    wait(dve, ks_ready, 1, g2, 1)
                    for kvx, ksx, head in ((kv_a, ks_a, head_a), (kv_b, ks_b, head_b)):
                        for b in range(2):
                            last = nc.vector.tensor_scalar(kvx[:, b, D:D + HEADS], head[:, :], ksx[:, b:b + 1], None, ALU.mult)
                    last.then_inc(kvm_ready, 1)
                if g3:
                    wait(dve, x2T_done, 1, g3, 1)
                    wait(dve, gu_done, 6, g3)
                    nc.vector.tensor_copy(x2T_b[:, :], bank[6][0:DB, 0:G]).then_inc(x2Tb_ready, 1)
                if g2:
                    wait(dve, att_done, 1, g2, 1)
                    for b in range(2):
                        both = bank[3 + b][0:P, 0:2 * (D + HEADS)].rearrange("p (j c) -> p j c", j=2)
                        last = nc.vector.tensor_scalar(den[:, 2 * b:2 * b + 2, :], both[:, :, D:D + HEADS], EPS_ATT, None, ALU.add)
                    last.then_inc(den_ready, 1)
                    wait(dve, den_ready, 1, g2, 1)
                    nc.vector.reciprocal(z[:, :, :], den[:, :, :]).then_inc(z_ready, 1)
                    wait(dve, z_ready, 1, g2, 1)
                    for j in range(GT):
                        c0 = (j % 2) * (D + HEADS)
                        last = nc.vector.tensor_tensor(
                            o[:, j, :].rearrange("p (h d) -> p h d", d=DH),
                            bank[3 + j // 2][0:P, c0:c0 + D].rearrange("p (h d) -> p h d", d=DH),
                            z[:, j, :, None].to_broadcast([P, HEADS, DH]), ALU.mult)
                    last.then_inc(o_ready, 1)
                if g3:
                    wait(dve, exps_ready, 1, g3, 1)
                    nc.vector.tensor_scalar(sig[:, :, :], exps[:, :, :], 1.0, None, ALU.add).then_inc(sig1_ready, 1)
                    wait(dve, sig1_ready, 1, g3, 1)
                    nc.vector.reciprocal(row[g3.par][:, :, D:ROW], sig[:, :, :]).then_inc(sig_ready, 1)
                    wait(dve, sig_ready, 1, g3, 1)
                    apart(dve)
                    nc.vector.tensor_copy(scores_tm[:, bass.ds(g3.n * GT, GT), :], row[g3.par][:, :, D:ROW]).then_inc(scores_ready, 1)
                if g1:
                    wait(dve, h_ready, 1, g1, 1)
                    moments(g1, lambda j: h[g1.par][:, j, :], stats, mv, stats_ready, mv_ready)
                    wait(dve, rstd_ready, 1, g1, 1)
                    for j in range(GT):
                        last = nc.vector.tensor_scalar(xn[:, j, :], h[g1.par][:, j, :], mv[:, j, 0:1], rstd[:, j:j + 1],
                                                       ALU.subtract, ALU.mult)
                    last.then_inc(xn_ready, 1)
                if g2:
                    wait(dve, oT_done, 1, g2, 1)
                    nc.vector.tensor_copy(oT_b[0:DB, :], bank[4][0:DB, 0:G]).then_inc(oTb_ready, 1)
                if g3:
                    wait(dve, down_done, 1, g3)
                    for f in range(3):
                        wait(dve, silu_ready, 3, g3, f + 1)
                        wait(dve, gu_done, 6, g3, 2 * f + 2)
                        nc.vector.tensor_tensor(hs[:, f, :], silu[f % 2][:, :], bank[(6, 5, 7)[f]][:, 0:G], ALU.mult).then_inc(hs_ready, 1)
                if g1:
                    wait(dve, xT_done, 1, g1, 1)
                    nc.vector.tensor_copy(xT_b[:, :], bank[0][0:DB, 0:G]).then_inc(xTb_ready, 1)
                if g2:
                    wait(dve, wo_done, 1, g2, 1)
                    for b in range(2):
                        last = nc.vector.tensor_tensor(h1[g2.par][:, 2 * b:2 * b + 2, :], h[g2.par][:, 2 * b:2 * b + 2, :],
                                                       bank[3 + b][0:P, 0:2 * D].rearrange("p (j c) -> p j c", c=D), ALU.add)
                    last.then_inc(h1_ready, 1)
                    wait(dve, h1_ready, 1, g2, 1)
                    moments(g2, lambda j: h1[g2.par][:, j, :], stats2, mv2, stats2_ready, mv2_ready)
                if g1:
                    for n, (to, b, e, m) in enumerate(((q_a, bank[2], expq_a, DA), (q_b, bank[0], expq_b, DB))):
                        relu_plus(g1, to[g1.par][:, :], b[0:m, 0:G], e[:, :], expq_ready, 2, n + 1, minq_ready, q_ready)
                    for j, b in enumerate((1, 2, 0, 1)):
                        wait(dve, v_ready, 4, g1, j + 1)
                        relu_plus(g1, k[g1.par][:, j, :], bank[b][0:P, 0:D], expk[:, j, :], expk_ready, 4, j + 1, mink_ready, k_ready)
                if g2:
                    wait(dve, rstd2_ready, 1, g2, 1)
                    if not g2.known or g2.n >= 2:
                        dve.wait_ge(rows_out[g2.par], g2.half * 16)
                    for j in range(GT):
                        last = nc.vector.tensor_scalar(row[g2.par][:, j, 0:D], h1[g2.par][:, j, :], mv2[:, j, 0:1],
                                                       rstd2[:, j:j + 1], ALU.subtract, ALU.mult)
                    last.then_inc(x2_ready, 1)
                if g3:
                    wait(dve, down_done, 1, g3, 1)
                    if not g3.known or g3.n >= 2:
                        dve.wait_ge(y_out[g3.par], g3.half * 16)
                    for b in range(2):
                        last = nc.vector.tensor_tensor(y[g3.par][:, 2 * b:2 * b + 2, :], h1[g3.par][:, 2 * b:2 * b + 2, :],
                                                       bank[5 + b][0:P, 0:2 * D].rearrange("p (j c) -> p j c", c=D), ALU.add)
                    last.then_inc(y_ready, 1)

            skewed(dve, step)



def select_phase(nc, io, resident):
    scores_tm, ident = resident["scores_tm"], resident["ident"]
    with ExitStack() as ctx:
        def sb(name, shape, dt=F32):
            return ctx.enter_context(nc.sbuf_tensor(name, shape, dt))

        def sem(name):
            return ctx.enter_context(nc.semaphore(name))

        bank = [ctx.enter_context(nc.psum_tensor(f"sel_bank{i}", [128, 512], F32)) for i in range(8)]
        same, before = sb("same", [128, 128]), sb("before", [128, 128])
        s = sb("s", [128, CLEN])
        mark = sb("mark", [128, CLEN], BF16)
        above, equal, ties, chosen, slot, slot_q, slot_p = (sb(n, [128, CLEN]) for n in (
            "above", "equal", "ties", "chosen", "slot", "quot", "rest"))
        zero = sb("zero", [128, 1])
        gathered = sb("by_piece", [P, CT * 128])
        gather_ready = sem("by_piece_ready")
        bit_f, count = sb("bit_f", [128, 1]), sb("count", [128, 1])
        bit, thr, cand, keep = (sb(n, [128, 1], I32) for n in ("bit", "thr", "cand", "keep"))
        room, offset = sb("room", [128, 1]), sb("offset", [128, 1])

        mats_in, s_done, s_ready, init_set = sem("mats_in"), sem("s_done"), sem("s_ready"), sem("init_set")
        cand_ready, count_ready, total_done, keep_ready, thr_ready, bit_ready = (sem(n) for n in (
            "cand_ready", "count_ready", "total_done", "keep_ready", "thr_ready", "bit_ready"))
        above_ready, ties_ready, offsets_done, chosen_ready, slots_ready = (sem(n) for n in (
            "above_ready", "ties_ready", "offsets_done", "chosen_ready", "slots_ready"))
        link, maps_done, maps_read = sem("link"), sem("maps_done"), sem("maps_read")
        BITS = 30
        block = ctx.enter_context(nc.Block())

        @block.sync
        def _(sp):
            sp.dma_start(same[:, :], io["same_expert"]).then_inc(mats_in, 16)
            sp.dma_start(before[:, :], io["before"]).then_inc(mats_in, 16)

        @block.tensor
        def _(pe):
            pe.wait_ge(gather_ready, 1)
            for b in range(CT):
                nc.tensor.transpose(bank[b // 4][:, (b % 4) * P:(b % 4 + 1) * P], gathered[:, b * 128:(b + 1) * 128],
                                    ident[0:P, 0:P]).then_inc(s_done, 1)
            pe.wait_ge(mats_in, 32)
            with pe.Fori(0, BITS) as i:
                pe.wait_ge(count_ready, i + 1)
                nc.tensor.matmul(bank[4][:, 0:1], same[:, :], count[:, :], start=True, stop=True).then_inc(total_done, 1)
            pe.wait_ge(ties_ready, 1)
            nc.tensor.matmul(bank[5][:, 0:1], same[:, :], count[:, :], start=True, stop=True)
            nc.tensor.matmul(bank[5][:, 1:2], before[:, :], ties[:, CLEN - 1:CLEN], start=True, stop=True).then_inc(offsets_done, 1)
            pe.wait_ge(chosen_ready, 1)
            nc.tensor.matmul(bank[5][:, 2:3], before[:, :], slot[:, CLEN - 1:CLEN], start=True, stop=True).then_inc(offsets_done, 1)
            pe.wait_ge(slots_ready, 1)
            for n, src in enumerate((slot_q, slot_p)):
                for b in range(CT):
                    if n and b % 4 == 0:
                        pe.wait_ge(maps_read, b // 4 + 1)
                    last = nc.tensor.transpose(bank[b // 4][0:P, (b % 4) * 128:(b % 4 + 1) * 128], src[:, b * P:(b + 1) * P], ident[:, :])
                    if b % 4 == 3:
                        last.then_inc(maps_done, 1)

        @block.vector
        def _(dve):
            links = [0]

            def then(instruction):
                links[0] += 1
                instruction.then_inc(link, 1)
                dve.wait_ge(link, links[0])

            nc.vector.tensor_copy(gathered[:, :].rearrange("p (b c e) -> p c b e", b=CT, c=CHUNKS),
                                  scores_tm[:, :, :].rearrange("p (c b) e -> p c b e", b=CT)).then_inc(gather_ready, 1)
            nc.vector.memset(zero[:, :], 0.0)
            nc.vector.memset(bit_f[:, :], float(2 ** (BITS - 1)))
            nc.vector.memset(thr[:, :], 0).then_inc(init_set, 1)
            dve.wait_ge(init_set, 1)
            nc.vector.tensor_copy(bit[:, :], bit_f[:, :]).then_inc(bit_ready, 1)
            for n in range(4):
                dve.wait_ge(s_done, 4 * n + 4)
                last = nc.vector.tensor_copy(s[:, n * 4 * P:(n + 1) * 4 * P], bank[n][:, 0:4 * P])
            last.then_inc(s_ready, 1)
            dve.wait_ge(s_ready, 1)
            with dve.Fori(0, BITS) as i:
                dve.wait_ge(bit_ready, i + 1)
                nc.vector.tensor_tensor(cand[:, :], thr[:, :], bit[:, :], ALU.bitwise_or).then_inc(cand_ready, 1)
                dve.wait_ge(cand_ready, i + 1)
                nc.vector.tensor_scalar(mark[:, :], s[:, :], cand[:, :].bitcast(F32), None, ALU.is_ge, ALU.add,
                                        accum_out=count[:, :]).then_inc(count_ready, 1)
                dve.wait_ge(total_done, i + 1)
                nc.vector.tensor_scalar(keep[:, :], bank[4][:, 0:1], float(CAP), bit_f[:, :], ALU.is_ge, ALU.mult).then_inc(keep_ready, 1)
                dve.wait_ge(keep_ready, i + 1)
                nc.vector.tensor_scalar(bit_f[:, :], bit_f[:, :], 0.5, None, ALU.mult)
                nc.vector.tensor_tensor(thr[:, :], thr[:, :], keep[:, :], ALU.bitwise_or).then_inc(thr_ready, 1)
                dve.wait_ge(thr_ready, i + 1)
                nc.vector.tensor_copy(bit[:, :], bit_f[:, :]).then_inc(bit_ready, 1)
            best = thr[:, :].bitcast(F32)
            nc.vector.tensor_scalar(above[:, :], s[:, :], best, None, ALU.is_gt, ALU.add, accum_out=count[:, :])
            then(nc.vector.tensor_scalar(equal[:, :], s[:, :], best, None, ALU.is_equal))
            nc.vector.tensor_tensor_scan(ties[:, :], equal[:, :], zero[:, :].to_broadcast([128, CLEN]), 0.0,
                                         ALU.add, ALU.add).then_inc(ties_ready, 1)
            dve.wait_ge(offsets_done, 1)
            then(nc.vector.tensor_scalar(room[:, :], bank[5][:, 0:1], -1.0, float(CAP), ALU.mult, ALU.add))
            then(nc.vector.tensor_tensor(room[:, :], room[:, :], bank[5][:, 1:2], ALU.subtract))
            then(nc.vector.scalar_tensor_tensor(out=chosen[:, :], in0=ties[:, :], scalar=room[:, :], in1=equal[:, :],
                                                op0=ALU.is_le, op1=ALU.mult))
            then(nc.vector.tensor_tensor(chosen[:, :], chosen[:, :], above[:, :], ALU.add))
            nc.vector.tensor_tensor_scan(slot[:, :], chosen[:, :], zero[:, :].to_broadcast([128, CLEN]), 0.0,
                                         ALU.add, ALU.add).then_inc(chosen_ready, 1)
            dve.wait_ge(offsets_done, 2)
            then(nc.vector.tensor_copy(offset[:, :], bank[5][:, 2:3]))
            then(nc.vector.scalar_tensor_tensor(out=slot[:, :], in0=slot[:, :], scalar=offset[:, :], in1=chosen[:, :],
                                                op0=ALU.add, op1=ALU.mult))
            then(nc.vector.tensor_scalar(slot_q[:, :], slot[:, :], 1.0 / P, -(P // 2 + 1) / P, ALU.mult, ALU.add))
            then(nc.vector.tensor_scalar(slot_q[:, :], slot_q[:, :], ROUND, ROUND, ALU.add, ALU.subtract))
            nc.vector.scalar_tensor_tensor(out=slot_p[:, :], in0=slot_q[:, :], scalar=float(-P), in1=slot[:, :],
                                           op0=ALU.mult, op1=ALU.add).then_inc(slots_ready, 1)
            for n, to in enumerate((resident["slot_q"], resident["slot_p"])):
                view = to[:, :, :].rearrange("p e (c b) -> p b c e", b=CT)
                for b in range(0, CT, 4):
                    dve.wait_ge(maps_done, 4 * n + b // 4 + 1)
                    nc.vector.tensor_copy(view[:, b:b + 4], bank[b // 4][0:P, :].rearrange(
                        "p (b c e) -> p b c e", b=4, c=CHUNKS)).then_inc(maps_read, 1)


def experts_phase(nc, io, resident):
    ident = resident["ident"]
    NF = FE // 128
    NG = CAP // G
    OHT = 16
    NCH = TILES // OHT
    AT = {(g, f): c for c, (g, f) in enumerate([(g, f) for g in range(NG - 1) for f in (2, 3, 4)][:NCH])}
    NLOAD = 7
    with ExitStack() as ctx:
        def sb(name, shape, dt=F32):
            return ctx.enter_context(nc.sbuf_tensor(name, shape, dt))

        def sem(name):
            return ctx.enter_context(nc.semaphore(name))

        bank = [ctx.enter_context(nc.psum_tensor(f"ex_bank{i}", [128, 512], F32)) for i in range(8)]
        raw_ga, raw_gb, raw_ua, raw_ub = (sb(n, [128, FE]) for n in ("raw_ga", "raw_gb", "raw_ua", "raw_ub"))
        raw_d = sb("raw_d", [128, NF, D])
        ga_h, ga_l, gb_h, ua_h, ua_l, ub_h = ([sb(f"{n}{i}", [128, FE], F32R) for i in range(2)] for n in (
            "ga_h", "ga_l", "gb_h", "ua_h", "ua_l", "ub_h"))
        gb_l, ub_l = ([sb(f"{n}{i}", [DB, FE], F32R) for i in range(2)] for n in ("gb_l", "ub_l"))
        wd = [sb(f"wd{i}", [128, NF, 2 * D], F32R) for i in range(2)]
        xg = [sb(f"xg{i}", [P, GT, ROW]) for i in range(2)]
        score = [sb(f"score{i}", [P, GT]) for i in range(2)]
        xa_h, xa_l, xb = ([sb(f"{n}{i}", [128, G], F32R) for i in range(2)] for n in ("xa_h", "xa_l", "xb"))
        silu = [sb(f"ex_silu{i}", [128, G]) for i in range(2)]
        hf = [sb(f"hf{i}", [128, G]) for i in range(2)]
        h_h, h_l = ([sb(f"{n}{i}", [128, NF, G], F32R) for i in range(2)] for n in ("h_h", "h_l"))
        yb = [sb(f"yb{i}", [P, D]) for i in range(2)]
        yo = [sb(f"yo{i}", [P, GT, D]) for i in range(2)]
        iota_f, iota_p, iota_q, tile_no = sb("iota_f", [P, P + 1 + EXPERTS + TILES]), sb("iota_p", [P, P], BF16), sb(
            "iota_q", [P, EXPERTS], BF16), sb("tile_no", [P, TILES], BF16)
        is_q = sb("is_q", [P, TILES, EXPERTS], BF16)
        list_rhs = sb("list_rhs", [P, TILES, 2 * EXPERTS], BF16)
        is_p = [sb(f"is_p{i}", [P, OHT, P], BF16) for i in range(2)]
        place = sb("place", [P, EXPERTS])
        index = [sb(f"index{i}", [P, EXPERTS], U32) for i in range(2)]

        iota_in, iota_set = sem("iota_in"), sem("iota_set")
        weights_in, high_ready, split_ready = sem("weights_in"), sem("high_ready"), sem("split_ready")
        isq_ready, rhs_ready, isp_ready, list_done, place_ready, index_ready = (sem(n) for n in (
            "isq_ready", "rhs_ready", "isp_ready", "list_done", "place_ready", "index_ready"))
        gathered = [sem(f"gathered{i}") for i in range(2)]
        added = [sem(f"added{i}") for i in range(2)]
        score_ready, tr_done = sem("score_ready"), sem("tr_done")
        xah_ready, xal_ready, xbh_ready, xbl_ready = (sem(n) for n in ("xah_ready", "xal_ready", "xbh_ready", "xbl_ready"))
        gu_done, silu_ready, hf_ready, hh_ready, hl_ready = (sem(n) for n in (
            "ex_gu_done", "ex_silu_ready", "hf_ready", "hh_ready", "hl_ready"))
        down_done, yb_ready, yo_ready = sem("ex_down_done"), sem("yb_ready"), sem("yo_ready")
        block = ctx.enter_context(nc.Block())

        def over_experts(eng, step):
            def known(n):
                for g in range(NG):
                    step(Group(n, n // 2, n % 2, True), g)

            known(0)
            known(1)
            with eng.Fori(0, EXPERTS // 2 - 2) as i:
                for par in range(2):
                    for g in range(NG):
                        step(Group(i * 2 + (2 + par), i + 1, par, False), g)
            known(EXPERTS - 2)
            known(EXPERTS - 1)

        def later(e, by):
            par = (e.par + by) % 2
            if e.known and e.n + by >= EXPERTS:
                return None
            return Group(e.n + by, e.half + (e.par + by - par) // 2, par, e.known)

        def following(e, g):
            return (e, g + 1) if g + 1 < NG else (later(e, 1), 0)

        def preceding(e, g):
            if g:
                return e, g - 1
            return (None if e.known and e.n == 0 else later(e, -1)), NG - 1

        FIRST = Group(0, 0, 0, True)
        LAST = Group(EXPERTS - 1, (EXPERTS - 1) // 2, (EXPERTS - 1) % 2, True)

        @block.sync
        def _(sp):
            sp.dma_start(iota_f[:, :], io["iotas"]).then_inc(iota_in, 16)

            def load(e):
                wait(sp, split_ready, 1, e)
                gate, up = io["wgT"][bass.ds(e.n * D, D), :], io["wuT"][bass.ds(e.n * D, D), :]
                for src, a, b in ((gate, raw_ga, raw_gb), (up, raw_ua, raw_ub)):
                    sp.dma_start(a[:, :], src[0:DA, :]).then_inc(weights_in, 16)
                    sp.dma_start(b[0:DB, :], src[DA:D, :]).then_inc(weights_in, 16)
                    sp.dma_start(b[DB:128, :], src[DA:D, :]).then_inc(weights_in, 16)
                sp.dma_start(raw_d[:, :, :], io["wdT"][bass.ds(e.n * FE, FE), :].rearrange("(c p) n -> p c n", p=128)).then_inc(weights_in, 16)

            load(FIRST)

            def step(e, g):
                if g == 0 and later(e, 1):
                    load(later(e, 1))

            over_experts(sp, step)

        @block.gpsimd
        def _(pool):
            def split_high(e):
                wait(pool, weights_in, 16 * NLOAD, e, 16 * NLOAD)
                wait(pool, down_done, NG * GT, e, less=1)
                apart(pool)
                p = e.par
                for dst, src in ((ga_h, raw_ga), (ua_h, raw_ua), (gb_h, raw_gb), (ub_h, raw_ub)):
                    nc.gpsimd.tensor_copy(dst[p][:, :], src[:, :])
                nc.gpsimd.tensor_copy(wd[p][:, :, 0:D], raw_d[:, :, :]).then_inc(high_ready, 1)

            def split_low(e, part):
                p = e.par
                if part == 0:
                    wait(pool, high_ready, 1, e, 1)
                    for dst, src, hi in ((ga_l, raw_ga, ga_h), (ua_l, raw_ua, ua_h)):
                        nc.gpsimd.tensor_tensor(dst[p][:, :], src[:, :], hi[p][:, :].bitcast(F32), ALU.subtract)
                else:
                    for dst, src, hi in ((gb_l, raw_gb, gb_h), (ub_l, raw_ub, ub_h)):
                        nc.gpsimd.tensor_tensor(dst[p][:, :], src[0:DB, :], hi[p][0:DB, :].bitcast(F32), ALU.subtract)
                    nc.gpsimd.tensor_tensor(wd[p][:, :, D:2 * D], raw_d[:, :, :], wd[p][:, :, 0:D].bitcast(F32),
                                            ALU.subtract).then_inc(split_ready, 1)

            def gather(e, g):
                wait(pool, index_ready, 1, e, 1)
                wait(pool, tr_done, 2 * NG, e, 2 * (g - 1))
                wait(pool, score_ready, NG, e, g - 1)
                apart(pool)
                for j in range(GT):
                    n = g * GT + j
                    nc.gpsimd.indirect_dma_start(
                        out=xg[g % 2][:, j, :], out_offset=None, in_=io["rows"],
                        in_offset=bass.IndirectOffsetOnAxis(ap=index[e.par][:, n:n + 1], axis=0)).then_inc(gathered[g % 2], 16)

            def scatter(e, g):
                if g == 0:
                    for i in range(2):
                        wait(pool, added[i], 16 * GT * NG // 2, e)
                for j in range(GT):
                    n = g * GT + j
                    wait(pool, yo_ready, NG * GT, e, n + 1)
                    apart(pool)
                    nc.gpsimd.indirect_dma_start(
                        out=io["out"], out_offset=bass.IndirectOffsetOnAxis(ap=index[e.par][:, n:n + 1], axis=0),
                        in_=yo[g % 2][:, j, :], in_offset=None, compute_op=ALU.add).then_inc(added[g % 2], 16)

            split_high(FIRST)
            split_low(FIRST, 0)
            split_low(FIRST, 1)
            gather(FIRST, 0)

            def step(e, g):
                ne, ng = following(e, g)
                if ne:
                    gather(ne, ng)
                after = later(e, 1)
                if after and g == 1:
                    split_high(after)
                if after and g > 1:
                    split_low(after, g - 2)
                pe_, pg = preceding(e, g)
                if pe_:
                    scatter(pe_, pg)

            over_experts(pool, step)
            scatter(LAST, NG - 1)
            for i in range(2):
                pool.wait_ge(added[i], EXPERTS * 16 * GT * NG // 2)

        @block.tensor
        def _(pe):
            def list_tokens(e, c):
                if c == 0:
                    wait(pe, rhs_ready, 1, e, 1)
                    wait(pe, index_ready, 1, e)
                wait(pe, isp_ready, NCH, e, c + 1)
                for t in range(OHT):
                    n = c * OHT + t
                    last = nc.tensor.matmul(bank[7][0:P, 0:2 * EXPERTS], is_p[c % 2][:, t, :], list_rhs[:, n, :],
                                            start=(n == 0), stop=(n == TILES - 1))
                last.then_inc(list_done, 1)

            def transpose(e, g, part):
                if part == 0:
                    wait(pe, gathered[g % 2], 16 * GT * NG // 2, e, 16 * GT * (g // 2 + 1))
                    wait(pe, xbl_ready, NG, e, g)
                else:
                    wait(pe, xal_ready, NG, e, g + 1)
                apart(pe)
                c0, m = ((0, DA), (DA, DB))[part]
                for j in range(GT):
                    last = nc.tensor.transpose(bank[6][0:m, j * P:(j + 1) * P], xg[g % 2][:, j, c0:c0 + m], ident[0:P, 0:P])
                last.then_inc(tr_done, 1)

            def up(e, g, f):
                if f == 0:
                    wait(pe, split_ready, 1, e, 1)
                    wait(pe, xal_ready, NG, e, g + 1)
                    wait(pe, xbl_ready, NG, e, g + 1)
                p, s, cols = e.par, g % 2, slice(f * 128, (f + 1) * 128)
                for w, (a_h, a_l, b_h, b_l) in enumerate(((ga_h, ga_l, gb_h, gb_l), (ua_h, ua_l, ub_h, ub_l))):
                    wait(pe, (silu_ready, hf_ready)[w], NG * NF, e, NF * g + f - 1)
                    to = bank[2 * (f % 2) + w][:, 0:G]
                    nc.tensor.matmul(to, a_h[p][:, cols], xa_h[s][:, :], start=True, stop=False)
                    nc.tensor.matmul(to, a_l[p][:, cols], xa_h[s][:, :], start=False, stop=False)
                    nc.tensor.matmul(to, a_h[p][:, cols], xa_l[s][:, :], start=False, stop=False)
                    nc.tensor.matmul(to, b_h[p][:, cols], xb[s][:, :], start=False, stop=False)
                    nc.tensor.matmul(to, b_l[p][:, cols], xb[s][0:DB, :], start=False, stop=True).then_inc(gu_done, 1)

            def down(e, g):
                wait(pe, hl_ready, NG * NF, e, NF * (g + 1))
                for j in range(GT):
                    wait(pe, yo_ready, NG * GT, e, GT * g + j - 1)
                    cols = slice(j * P, (j + 1) * P)
                    to = bank[4 + j % 2]
                    for f in range(NF):
                        nc.tensor.matmul(to[0:P, 0:2 * D], h_h[g % 2][:, f, cols], wd[e.par][:, f, :], start=(f == 0), stop=False)
                        last = nc.tensor.matmul(to[0:P, 0:D], h_l[g % 2][:, f, cols], wd[e.par][:, f, 0:D],
                                                start=False, stop=(f == NF - 1))
                    last.then_inc(down_done, 1)

            for c in range(NCH):
                list_tokens(FIRST, c)
            transpose(FIRST, 0, 0)
            transpose(FIRST, 0, 1)

            def step(e, g):
                ne, ng = following(e, g)
                after = later(e, 1)
                for f in range(NF):
                    up(e, g, f)
                    if f == 1:
                        pe_, pg = preceding(e, g)
                        if pe_:
                            down(pe_, pg)
                    if f == 2 and ne:
                        transpose(ne, ng, 0)
                    if f == 4 and ne:
                        transpose(ne, ng, 1)
                    if after and (g, f - 1) in AT:
                        list_tokens(after, AT[g, f - 1])

            over_experts(pe, step)
            down(LAST, NG - 1)

        @block.scalar
        def _(act):
            def x_high(e, g, part):
                wait(act, tr_done, 2 * NG, e, 2 * g + part + 1)
                wait(act, gu_done, 2 * NF * NG, e, 2 * NF * (g - 1))
                if part == 0:
                    nc.scalar.copy(xa_h[g % 2][:, :], bank[6][:, 0:G]).then_inc(xah_ready, 1)
                else:
                    nc.scalar.copy(xb[g % 2][0:DB, :], bank[6][0:DB, 0:G]).then_inc(xbh_ready, 1)

            def gate(e, g, f):
                wait(act, gu_done, 2 * NF * NG, e, 2 * (NF * g + f) + 1)
                wait(act, hf_ready, NF * NG, e, NF * g + f - 1)
                nc.scalar.activation(silu[f % 2][:, :], bank[2 * (f % 2)][:, 0:G], ACT.Silu).then_inc(silu_ready, 1)

            def h_high(e, g, f):
                wait(act, hf_ready, NF * NG, e, NF * g + f + 1)
                wait(act, down_done, NG * GT, e, GT * (g - 1))
                nc.scalar.copy(h_h[g % 2][:, f, :], hf[f % 2][:, :]).then_inc(hh_ready, 1)

            def y_low(e, g):
                for j in range(GT):
                    wait(act, down_done, NG * GT, e, GT * g + j + 1)
                    wait(act, score_ready, NG, e, g + 1)
                    wait(act, yo_ready, NG * GT, e, GT * g + j - 1)
                    nc.scalar.mul(yb[j % 2][:, :], bank[4 + j % 2][0:P, D:2 * D], score[g % 2][:, j:j + 1]).then_inc(yb_ready, 1)

            x_high(FIRST, 0, 0)
            x_high(FIRST, 0, 1)

            def step(e, g):
                ne, ng = following(e, g)
                gate(e, g, 0)
                gate(e, g, 1)
                h_high(e, g, 0)
                h_high(e, g, 1)
                pe_, pg = preceding(e, g)
                if pe_:
                    y_low(pe_, pg)
                for f in range(2, NF):
                    gate(e, g, f)
                    h_high(e, g, f)
                    if f in (2, 4) and ne:
                        x_high(ne, ng, f // 2 - 1)

            over_experts(act, step)
            y_low(LAST, NG - 1)

        @block.vector
        def _(dve):
            def list_rhs_of(e):
                wait(dve, list_done, NCH, e)
                nc.vector.tensor_tensor(
                    is_q[:, :, :], resident["slot_q"][:, bass.ds(e.n, 1), :].rearrange("p a t -> p (a t)").unsqueeze(2).to_broadcast([P, TILES, EXPERTS]),
                    iota_q[:, :].unsqueeze(1).to_broadcast([P, TILES, EXPERTS]), ALU.is_equal).then_inc(isq_ready, 1)
                wait(dve, isq_ready, 1, e, 1)
                nc.vector.tensor_scalar(list_rhs[:, :, 0:EXPERTS], is_q[:, :, :], iota_f[:, P:P + 1], None, ALU.mult)
                nc.vector.tensor_tensor(list_rhs[:, :, EXPERTS:2 * EXPERTS], is_q[:, :, :],
                                        tile_no[:, :].unsqueeze(2).to_broadcast([P, TILES, EXPERTS]), ALU.mult).then_inc(rhs_ready, 1)

            def list_lhs(e, c):
                wait(dve, list_done, NCH, e, c - 1)
                nc.vector.tensor_tensor(
                    is_p[c % 2][:, :, :],
                    resident["slot_p"][:, bass.ds(e.n, 1), c * OHT:(c + 1) * OHT].rearrange("p a t -> p (a t)").unsqueeze(2).to_broadcast([P, OHT, P]),
                    iota_p[:, :].unsqueeze(1).to_broadcast([P, OHT, P]), ALU.is_equal).then_inc(isp_ready, 1)

            def list_end(e):
                wait(dve, list_done, NCH, e, NCH)
                nc.vector.tensor_copy(place[:, :], bank[7][0:P, 0:EXPERTS]).then_inc(place_ready, 1)
                wait(dve, place_ready, 1, e, 1)
                for i in range(2):
                    wait(dve, added[i], 16 * GT * NG // 2, e, less=1)
                nc.vector.scalar_tensor_tensor(out=index[e.par][:, :], in0=bank[7][0:P, EXPERTS:2 * EXPERTS], scalar=float(P),
                                               in1=place[:, :], op0=ALU.mult, op1=ALU.add).then_inc(index_ready, 1)

            def scores(e, g):
                wait(dve, gathered[g % 2], 16 * GT * NG // 2, e, 16 * GT * (g // 2 + 1))
                apart(dve)
                nc.vector.tensor_copy(score[g % 2][:, :], xg[g % 2][:, :, bass.ds(e.n + D, 1)].rearrange("p j a -> p (j a)")).then_inc(score_ready, 1)

            def x_low(e, g, part):
                if part == 0:
                    wait(dve, xah_ready, NG, e, g + 1)
                    nc.vector.tensor_tensor(xa_l[g % 2][:, :], bank[6][:, 0:G], xa_h[g % 2][:, :].bitcast(F32), ALU.subtract).then_inc(xal_ready, 1)
                else:
                    wait(dve, xbh_ready, NG, e, g + 1)
                    nc.vector.tensor_tensor(xb[g % 2][DB:128, :], bank[6][0:DB, 0:G], xb[g % 2][0:DB, :].bitcast(F32), ALU.subtract).then_inc(xbl_ready, 1)

            def product(e, g, f):
                wait(dve, silu_ready, NF * NG, e, NF * g + f + 1)
                wait(dve, gu_done, 2 * NF * NG, e, 2 * (NF * g + f) + 2)
                wait(dve, hl_ready, NF * NG, e, NF * g + f - 1)
                nc.vector.tensor_tensor(hf[f % 2][:, :], silu[f % 2][:, :], bank[2 * (f % 2) + 1][:, 0:G], ALU.mult).then_inc(hf_ready, 1)

            def h_low(e, g, f):
                wait(dve, hh_ready, NF * NG, e, NF * g + f + 1)
                nc.vector.tensor_tensor(h_l[g % 2][:, f, :], hf[f % 2][:, :], h_h[g % 2][:, f, :].bitcast(F32), ALU.subtract).then_inc(hl_ready, 1)

            def y_sum(e, g):
                wait(dve, added[g % 2], 16 * GT * NG // 2, e, 16 * GT * (g // 2))
                for j in range(GT):
                    wait(dve, yb_ready, NG * GT, e, GT * g + j + 1)
                    nc.vector.scalar_tensor_tensor(out=yo[g % 2][:, j, :], in0=bank[4 + j % 2][0:P, 0:D], scalar=score[g % 2][:, j:j + 1],
                                                   in1=yb[j % 2][:, :], op0=ALU.mult, op1=ALU.add).then_inc(yo_ready, 1)

            dve.wait_ge(iota_in, 16)
            nc.vector.tensor_copy(iota_p[:, :], iota_f[:, 0:P])
            nc.vector.tensor_copy(iota_q[:, :], iota_f[:, P + 1:P + 1 + EXPERTS])
            nc.vector.tensor_copy(tile_no[:, :], iota_f[:, P + 1 + EXPERTS:]).then_inc(iota_set, 1)
            dve.wait_ge(iota_set, 1)
            list_rhs_of(FIRST)
            for c in range(NCH):
                list_lhs(FIRST, c)
            list_end(FIRST)
            scores(FIRST, 0)
            x_low(FIRST, 0, 0)
            x_low(FIRST, 0, 1)
            list_rhs_of(later(FIRST, 1))

            def step(e, g):
                ne, ng = following(e, g)
                after = later(e, 1)
                product(e, g, 0)
                product(e, g, 1)
                h_low(e, g, 0)
                h_low(e, g, 1)
                pe_, pg = preceding(e, g)
                if pe_:
                    y_sum(pe_, pg)
                for f in range(2, NF):
                    product(e, g, f)
                    if after and (g, f) in AT:
                        list_lhs(after, AT[g, f])
                    h_low(e, g, f)
                    if f == 2 and ne:
                        scores(ne, ng)
                    if f in (2, 4) and ne:
                        x_low(ne, ng, f // 2 - 1)
                if g == NG - 2 and after:
                    list_end(after)
                if g == NG - 1 and later(e, 2):
                    list_rhs_of(later(e, 2))

            over_experts(dve, step)
            y_sum(LAST, NG - 1)


def audio_tower(nc, io):
    with ExitStack() as ctx:
        resident = {
            "ident": ctx.enter_context(nc.sbuf_tensor("ident", [128, 128], F32)),
            "scores_tm": ctx.enter_context(nc.sbuf_tensor("scores_tm", [P, TILES, EXPERTS], F32)),
            "slot_p": ctx.enter_context(nc.sbuf_tensor("slot_p", [P, EXPERTS, TILES], BF16)),
            "slot_q": ctx.enter_context(nc.sbuf_tensor("slot_q", [P, EXPERTS, TILES], BF16)),
        }
        tower_phase(nc, io, resident)
        select_phase(nc, io, resident)
        experts_phase(nc, io, resident)


_IO = ["framesT", "dft", "mel", "dct", "w_proj", "b_proj", "wqkv", "wout", "b_out", "gateT", "wsgT", "wsuT", "wsdT",
       "wgT", "wuT", "wdT", "ident", "same_head", "head_of", "same_expert", "before", "iotas"]


def _constants():
    import numpy as np

    n = np.arange(FRAME)
    window = 0.54 - 0.46 * np.cos(2.0 * np.pi * n / (FRAME - 1))
    angle = 2.0 * np.pi * np.outer(n, np.arange(BINS // 2)) / FRAME
    dft = np.concatenate([np.cos(angle), -np.sin(angle)], axis=1) * window[:, None]
    d, r = np.arange(D), np.arange(128)
    iotas = np.concatenate([np.tile(np.arange(1, P + 1), (P, 1)), np.arange(P)[:, None],
                            np.tile(np.arange(EXPERTS), (P, 1)), np.tile(np.arange(TILES), (P, 1))], axis=1)
    f = np.float32
    same = r[:, None] % EXPERTS == r[None, :] % EXPERTS
    return {
        "dft": dft.astype(f),
        "ident": np.eye(128, dtype=f),
        "same_head": (d[:, None] // DH == d[None, :] // DH).astype(f),
        "head_of": (d[:, None] // DH == np.arange(HEADS)[None, :]).astype(f),
        "same_expert": same.astype(f),
        "before": (same & (r[:, None] < r[None, :])).astype(f),
        "iotas": iotas.astype(f),
    }


def _layout(a):
    import numpy as np

    step = (a["x"].shape[1] - FRAME) // (FRAMES - 1)
    at = np.arange(FRAMES)[:, None] * step + np.arange(FRAME)[None, :]
    return {
        "framesT": a["x"][:, at].reshape(TOKENS, FRAME).T,
        "mel": np.concatenate([a["L0_tok_mel_filters"].T] * 2, axis=0),
        "dct": a["L0_tok_dct"],
        "w_proj": a["L0_tok_w_proj"],
        "b_proj": a["L0_tok_b_proj"][None, :],
        "wqkv": a["L0_attn_W_qkv"],
        "wout": a["L0_attn_W_out"],
        "b_out": a["L0_attn_b_out"][None, :],
        "gateT": a["L0_ffn_gate_weight"].T,
        "wsgT": a["L0_ffn_Ws_g"].T,
        "wsuT": a["L0_ffn_Ws_u"].T,
        "wsdT": a["L0_ffn_Ws_d"].T,
        "wgT": a["L0_ffn_Wg"].transpose(0, 2, 1).reshape(EXPERTS * D, FE),
        "wuT": a["L0_ffn_Wu"].transpose(0, 2, 1).reshape(EXPERTS * D, FE),
        "wdT": a["L0_ffn_Wd"].transpose(0, 2, 1).reshape(EXPERTS * FE, D),
    }


def kernel(**inputs):
    import concourse.bacc as bacc
    import numpy as np
    from concourse.bass_utils import run_bass_kernel_spmd

    laid = _layout({name: np.asarray(a) for name, a in inputs.items()}) | _constants()
    nc = bacc.Bacc("TRN2", target_bir_lowering=False, num_devices=1)
    arrays, io = {}, {}
    for name in _IO:
        a = np.ascontiguousarray(laid[name])
        arrays[f"in_{name}"] = a
        io[name] = nc.dram_tensor(f"in_{name}", a.shape, mybir.dt.from_np(a.dtype), kind="ExternalInput").ap()
    io["rows"] = nc.dram_tensor("rows", (TOKENS, ROW), F32, kind="Internal").ap()
    io["out"] = nc.dram_tensor("out", (TOKENS, D), F32, kind="ExternalOutput").ap()
    audio_tower(nc, io)
    result = run_bass_kernel_spmd(nc, [arrays], core_ids=[0])
    return result.results[0]["out"].reshape(BATCH, FRAMES, D)
```

```python
from collections import namedtuple
from contextlib import ExitStack

import concourse.bass as bass
from concourse import mybir

F32 = mybir.dt.float32
F32R = mybir.dt.float32r
BF16 = mybir.dt.bfloat16
I32 = mybir.dt.int32
U32 = mybir.dt.uint32
ALU = mybir.AluOpType
ACT = mybir.ActivationFunctionType

BATCH, FRAMES, FRAME = 64, 250, 100
BINS = 2 * (FRAME // 2 + 1)
MEL = 40
D = 192
DA, DB = 128, 64
HEADS, DH = 12, 16
EXPERTS = 16
FE, FS = 768, 384
TOKENS = BATCH * FRAMES
CAP = 2000
P = 125
TILES = TOKENS // P
GT = 4
G = GT * P
GROUPS = TOKENS // G
ROW = D + EXPERTS
CHUNKS = 128 // EXPERTS
CT = TILES // CHUNKS
CLEN = CT * P
EPS_LOG, EPS_LN, EPS_ATT = 1e-6, 1e-5, 1e-6
ROUND = float(3 << 22)

Group = namedtuple("Group", "n half par known")


def wait(eng, sem, per, g, off=0, less=0):
    if g.known and per * (g.n - less) + off <= 0:
        return
    eng.wait_ge(sem, (g.n - less) * per + off)


def apart(eng):
    eng.nop(nofuse=True)


def wait_alone(eng, *which, **how):
    wait(eng, *which, **how)
    apart(eng)


def skewed(eng, step):
    STAGES, FIRST = 5, 6

    def groups(n, half, par, known):
        out = []
        for s in range(STAGES):
            gpar = (par - s) % 2
            gh = half + (par - s - gpar) // 2
            out.append(Group(n - s, gh, gpar, known) if not known or 0 <= n - s < GROUPS else None)
        return out

    for it in range(FIRST):
        step(groups(it, it // 2, it % 2, True))
    with eng.Fori(0, (GROUPS - FIRST) // 2) as i:
        for par in range(2):
            step(groups(i * 2 + (FIRST + par), i + FIRST // 2, par, False))
    for it in range(GROUPS, GROUPS + STAGES - 1):
        step(groups(it, it // 2, it % 2, True))


def tower_phase(nc, io, resident):
    scores_tm, ident = resident["scores_tm"], resident["ident"]
    with ExitStack() as ctx:
        def sb(name, shape, dt=F32):
            return ctx.enter_context(nc.sbuf_tensor(name, shape, dt))

        def sem(name):
            return ctx.enter_context(nc.semaphore(name))

        bank = [ctx.enter_context(nc.psum_tensor(f"bank{i}", [128, 512], F32)) for i in range(8)]

        dft = sb("dft", [FRAME, BINS])
        mel = sb("mel", [BINS, MEL])
        dctT = sb("dctT", [13, MEL])
        wproj = sb("wproj", [13, D])
        cproj = sb("cproj", [MEL + 1, D])
        wqkv_a, wqkv_b = sb("wqkv_a", [DA, 3 * D]), sb("wqkv_b", [128, 3 * D])
        wqkv_ah, wqkv_al, wqkv_bh = (sb(n, [128, 3 * D], F32R) for n in ("wqkv_ah", "wqkv_al", "wqkv_bh"))
        wqkv_bl = sb("wqkv_bl", [DB, 3 * D], F32R)
        wout_a, wout_b = sb("wout_a", [DA, D]), sb("wout_b", [128, D])
        wout_ah, wout_al, wout_bh = (sb(n, [128, D], F32R) for n in ("wout_ah", "wout_al", "wout_bh"))
        wout_bl = sb("wout_bl", [DB, D], F32R)
        b_out = sb("b_out", [P, D])
        gate_a, gate_b = sb("gate_a", [DA, EXPERTS]), sb("gate_b", [DB, EXPERTS])
        same_a, same_b = sb("same_a", [DA, D]), sb("same_b", [DB, D])
        head_a, head_b = sb("head_a", [DA, HEADS]), sb("head_b", [DB, HEADS])
        eps_log, eps_ln = sb("eps_log", [MEL, 1]), sb("eps_ln", [P, 1])

        frames = [sb(f"frames{i}", [FRAME, G]) for i in range(2)]
        power = sb("power", [BINS, G])
        logmel = sb("logmel", [MEL + 1, G])
        h = [sb(f"h{i}", [P, GT, D]) for i in range(2)]
        hb = [sb(f"hb{i}", [P, GT, D]) for i in range(2)]
        stats, stats2 = sb("stats", [P, GT, 6]), sb("stats2", [P, GT, 6])
        mv, mv2 = sb("mv", [P, GT, 2]), sb("mv2", [P, GT, 2])
        lnv, rstd = sb("lnv", [P, GT]), sb("rstd", [P, GT])
        lnv2, rstd2 = sb("lnv2", [P, GT]), sb("rstd2", [P, GT])
        xn = sb("xn", [P, GT, D])
        xa_h, xa_l, xb = (sb(n, [128, G], F32R) for n in ("xa_h", "xa_l", "xb"))
        expq_a, expq_b = sb("expq_a", [DA, G]), sb("expq_b", [DB, G])
        expk = sb("expk", [P, GT, D])
        q_a = [sb(f"q_a{i}", [DA, G]) for i in range(2)]
        q_b = [sb(f"q_b{i}", [DB, G]) for i in range(2)]
        k = [sb(f"k{i}", [P, GT, D]) for i in range(2)]
        v = [sb(f"v{i}", [P, GT, D + 1]) for i in range(2)]
        kv_a, kv_b = sb("kv_a", [DA, 2, D + HEADS]), sb("kv_b", [DB, 2, D + HEADS])
        ks_a, ks_b = sb("ks_a", [DA, 2]), sb("ks_b", [DB, 2])
        den, z = sb("den", [P, GT, HEADS]), sb("z", [P, GT, HEADS])
        o = sb("o", [P, GT, D])
        oa_h, oa_l, ob = (sb(n, [128, G], F32R) for n in ("oa_h", "oa_l", "ob"))
        h1 = [sb(f"h1_{i}", [P, GT, D]) for i in range(2)]
        row = [sb(f"row{i}", [P, GT, ROW]) for i in range(2)]
        x2T_a = [sb(f"x2T_a{i}", [DA, G]) for i in range(2)]
        x2T_b = [sb(f"x2T_b{i}", [DB, G]) for i in range(2)]
        exps, sig = sb("exps", [P, GT, EXPERTS]), sb("sig", [P, GT, EXPERTS])

        consts_in, consts_set, cproj_mm, cproj_set = sem("consts_in"), sem("consts_set"), sem("cproj_mm"), sem("cproj_set")
        high_set, low_set = sem("high_set"), sem("low_set")
        frames_in = [sem(f"frames_in{i}") for i in range(2)]
        dft_done, power_ready, mel_done, logmel_ready, proj_done = (sem(n) for n in (
            "dft_done", "power_ready", "mel_done", "logmel_ready", "proj_done"))
        h_ready, hb_ready, stats_ready, mv_ready, lnv_ready, rstd_ready, xn_ready = (sem(n) for n in (
            "h_ready", "hb_ready", "stats_ready", "mv_ready", "lnv_ready", "rstd_ready", "xn_ready"))
        xT_done, xh_ready, xl_ready = sem("xT_done"), sem("xh_ready"), sem("xl_ready")
        q_done, kv_done, expq_ready, expk_ready = sem("q_done"), sem("kv_done"), sem("expq_ready"), sem("expk_ready")
        minq_ready, mink_ready, q_ready, k_ready, v_ready = (sem(n) for n in (
            "minq_ready", "mink_ready", "q_ready", "k_ready", "v_ready"))
        ktv_done, ks_ready, kvm_ready = sem("ktv_done"), sem("ks_ready"), sem("kvm_ready")
        att_done, den_ready, z_ready, o_ready = sem("att_done"), sem("den_ready"), sem("z_ready"), sem("o_ready")
        oT_done, oh_ready, ol_ready, wo_done = sem("oT_done"), sem("oh_ready"), sem("ol_ready"), sem("wo_done")
        h1_ready, stats2_ready, mv2_ready, lnv2_ready, rstd2_ready, x2_ready = (sem(n) for n in (
            "h1_ready", "stats2_ready", "mv2_ready", "lnv2_ready", "rstd2_ready", "x2_ready"))
        x2T_done, x2Ta_ready, x2Tb_ready = sem("x2T_done"), sem("x2Ta_ready"), sem("x2Tb_ready")
        router_done, exps_ready, sig1_ready, sig_ready, scores_ready = (sem(n) for n in (
            "router_done", "exps_ready", "sig1_ready", "sig_ready", "scores_ready"))
        h1_out, xT_out, rows_out = ([sem(f"{n}{i}") for i in range(2)] for n in ("h1_out", "xT_out", "rows_out"))

        whole = [dft, mel, dctT, wproj, b_out, gate_a, gate_b, same_a, same_b, head_a, head_b, ident]
        loads = list(zip(whole, [
            io["dft"], io["mel"], io["dct"], io["w_proj"], io["b_out"].to_broadcast([P, D]),
            io["gateT"][0:DA, :], io["gateT"][DA:D, :], io["same_head"][0:DA, :], io["same_head"][DA:D, :],
            io["head_of"][0:DA, :], io["head_of"][DA:D, :], io["ident"]]))
        loads = [(t[:, :], src) for t, src in loads] + [
            (cproj[MEL:MEL + 1, :], io["b_proj"]),
            (wqkv_a[:, :], io["wqkv"][0:DA, :]), (wqkv_b[0:DB, :], io["wqkv"][DA:D, :]), (wqkv_b[DB:128, :], io["wqkv"][DA:D, :]),
            (wout_a[:, :], io["wout"][0:DA, :]), (wout_b[0:DB, :], io["wout"][DA:D, :]), (wout_b[DB:128, :], io["wout"][DA:D, :]),
        ]
        splits = [(wqkv_a, wqkv_ah, wqkv_al, 128), (wqkv_b, wqkv_bh, wqkv_bl, DB),
                  (wout_a, wout_ah, wout_al, 128), (wout_b, wout_bh, wout_bl, DB)]
        block = ctx.enter_context(nc.Block())

        @block.sync
        def _(sp):
            for dst, src in loads:
                sp.dma_start(dst, src).then_inc(consts_in, 16)

            def by_tile(dram, g):
                return dram[bass.ds(g.n * G, G), :].rearrange("(j p) c -> p j c", p=P)

            def step(gs):
                g0, _, _, g3, g4 = gs
                if g0:
                    wait_alone(sp, dft_done, 1, g0, less=1)
                    sp.dma_start(frames[g0.par][:, :], io["framesT"][:, bass.ds(g0.n * G, G)]).then_inc(frames_in[g0.par], 16)
                if g4:
                    wait_alone(sp, x2Ta_ready, 1, g4, 1)
                    wait_alone(sp, x2Tb_ready, 1, g4, 1)
                    sp.dma_start(io["x2T"][0:DA, bass.ds(g4.n * G, G)], x2T_a[g4.par][:, :]).then_inc(xT_out[g4.par], 16)
                    sp.dma_start(io["x2T"][DA:D, bass.ds(g4.n * G, G)], x2T_b[g4.par][:, :]).then_inc(xT_out[g4.par], 16)
                if g3:
                    wait_alone(sp, h1_ready, 1, g3, 1)
                    sp.dma_start(by_tile(io["out"], g3), h1[g3.par][:, :, :]).then_inc(h1_out[g3.par], 16)
                if g4:
                    wait_alone(sp, scores_ready, 1, g4, 1)
                    sp.dma_start(by_tile(io["rows"], g4), row[g4.par][:, :, :]).then_inc(rows_out[g4.par], 16)

            skewed(sp, step)
            for i in range(2):
                sp.wait_ge(rows_out[i], 16 * (GROUPS // 2))
                sp.wait_ge(h1_out[i], 16 * (GROUPS // 2))
                sp.wait_ge(xT_out[i], 32 * (GROUPS // 2))

        @block.gpsimd
        def _(pool):
            pool.wait_ge(consts_in, 16 * len(loads))

            def step(gs):
                g1 = gs[1]
                if g1:
                    wait(pool, h_ready, 1, g1, 1)
                    wait(pool, h1_ready, 1, g1, less=1)
                    nc.gpsimd.tensor_tensor(hb[g1.par][:, :, :], h[g1.par][:, :, :],
                                            b_out[:, :].unsqueeze(1).to_broadcast([P, GT, D]), ALU.add).then_inc(hb_ready, 1)

            skewed(pool, step)

        @block.tensor
        def _(pe):
            pe.wait_ge(consts_in, 16 * len(loads))
            nc.tensor.matmul(bank[0][0:MEL, 0:D], dctT[:, :], wproj[:, :], start=True, stop=True).then_inc(cproj_mm, 1)
            pe.wait_ge(cproj_set, 1)
            pe.wait_ge(low_set, 1)

            def transpose(src, to_a, to_b, done):
                for j in range(GT):
                    nc.tensor.transpose(to_a[0:DA, j * P:(j + 1) * P], src[:, j, 0:DA], ident[0:P, 0:P])
                for j in range(GT):
                    last = nc.tensor.transpose(to_b[0:DB, j * P:(j + 1) * P], src[:, j, DA:D], ident[0:P, 0:P])
                last.then_inc(done, 1)

            def split_product(to, pairs):
                for n, (w, x) in enumerate(pairs):
                    last = nc.tensor.matmul(to, w, x, start=(n == 0), stop=(n == len(pairs) - 1))
                return last

            def spectrum(g):
                pe.wait_ge(frames_in[g.par], (g.half + 1) * 16)
                wait(pe, h_ready, 1, g)
                nc.tensor.matmul(bank[0][0:BINS, 0:G], dft[:, :], frames[g.par][:, :], start=True, stop=True).then_inc(dft_done, 1)

            def filterbank(g):
                wait(pe, power_ready, 1, g, 1)
                nc.tensor.matmul(bank[1][0:MEL, 0:G], mel[:, :], power[:, :], start=True, stop=True).then_inc(mel_done, 1)

            def project(g):
                wait(pe, logmel_ready, 1, g, 1)
                for j in range(GT):
                    last = nc.tensor.matmul(bank[j // 2][0:P, (j % 2) * D:(j % 2 + 1) * D],
                                            logmel[:, j * P:(j + 1) * P], cproj[:, :], start=True, stop=True)
                last.then_inc(proj_done, 1)

            def queries(g):
                wait(pe, xh_ready, 2, g, 2)
                wait(pe, xl_ready, 2, g, 2)
                for to, c0, m in ((bank[2], 0, DA), (bank[3], DA, DB)):
                    c = slice(c0, c0 + m)
                    for n, (w, x) in enumerate(((wqkv_ah[:, c], xa_h[:, :]), (wqkv_al[:, c], xa_h[:, :]), (wqkv_ah[:, c], xa_l[:, :]),
                                                (wqkv_bh[:, c], xb[:, :]), (wqkv_bl[:, c], xb[0:DB, :]))):
                        last = nc.tensor.matmul(to[0:m, 0:G], w, x, start=(n == 0), stop=(n == 4))
                    last.then_inc(q_done, 1)

            def keys(g):
                for j, to in enumerate((4, 2, 3, 4)):
                    if j == 0:
                        wait(pe, x2Tb_ready, 1, g, 1, less=2)
                    if j in (1, 2):
                        wait(pe, q_ready, 2, g, j)
                    if j == 3:
                        wait(pe, k_ready, 4, g, 1)
                    t = slice(j * P, (j + 1) * P)
                    split_product(bank[to][0:P, 0:2 * D], (
                        (xa_h[:, t], wqkv_ah[:, D:3 * D]), (xa_h[:, t], wqkv_al[:, D:3 * D]), (xa_l[:, t], wqkv_ah[:, D:3 * D]),
                        (xb[:, t], wqkv_bh[:, D:3 * D]), (xb[0:DB, t], wqkv_bl[:, D:3 * D]))).then_inc(kv_done, 1)

            def keys_values(g):
                wait(pe, k_ready, 4, g, 4)
                wait(pe, v_ready, 4, g, 4)
                wait(pe, h1_ready, 1, g)
                for b in range(2):
                    for c, to, m in ((0, bank[5], DA), (DA, bank[6], DB)):
                        for j in (2 * b, 2 * b + 1):
                            last = nc.tensor.matmul(to[0:m, b * (D + 1):(b + 1) * (D + 1)], k[g.par][:, j, c:c + m],
                                                    v[g.par][:, j, :], start=(j % 2 == 0), stop=(j % 2 == 1))
                last.then_inc(ktv_done, 1)

            def attend(g):
                wait(pe, kvm_ready, 1, g, 1)
                wait(pe, q_ready, 2, g, 2)
                for j in range(GT):
                    to = bank[5 + j // 2][0:P, (j % 2) * (D + HEADS):(j % 2 + 1) * (D + HEADS)]
                    t = slice(j * P, (j + 1) * P)
                    nc.tensor.matmul(to, q_a[g.par][:, t], kv_a[:, j // 2, :], start=True, stop=False)
                    last = nc.tensor.matmul(to, q_b[g.par][:, t], kv_b[:, j // 2, :], start=False, stop=True)
                last.then_inc(att_done, 1)

            def out_proj(g):
                wait(pe, oh_ready, 2, g, 2)
                wait(pe, ol_ready, 2, g, 2)
                for j in range(GT):
                    t = slice(j * P, (j + 1) * P)
                    last = split_product(bank[5 + j // 2][0:P, (j % 2) * D:(j % 2 + 1) * D], (
                        (oa_h[:, t], wout_ah[:, :]), (oa_h[:, t], wout_al[:, :]), (oa_l[:, t], wout_ah[:, :]),
                        (ob[:, t], wout_bh[:, :]), (ob[0:DB, t], wout_bl[:, :])))
                last.then_inc(wo_done, 1)

            def router(g):
                wait(pe, x2Ta_ready, 1, g, 1)
                wait(pe, x2Tb_ready, 1, g, 1)
                for j in range(GT):
                    to = bank[7][0:P, j * EXPERTS:(j + 1) * EXPERTS]
                    t = slice(j * P, (j + 1) * P)
                    nc.tensor.matmul(to, x2T_a[g.par][:, t], gate_a[:, :], start=True, stop=False)
                    last = nc.tensor.matmul(to, x2T_b[g.par][:, t], gate_b[:, :], start=False, stop=True)
                last.then_inc(router_done, 1)

            def step(gs):
                _, g1, g2, g3, g4 = gs
                if g1:
                    spectrum(g1)
                if g2:
                    wait(pe, xn_ready, 1, g2, 1)
                    wait(pe, k_ready, 4, g2)
                    transpose(xn, bank[2], bank[3], xT_done)
                if g3:
                    keys_values(g3)
                if g1:
                    filterbank(g1)
                if g2:
                    queries(g2)
                if g3:
                    attend(g3)
                if g1:
                    project(g1)
                if g4:
                    wait(pe, x2_ready, 1, g4, 1)
                    wait(pe, exps_ready, 1, g4)
                    transpose(row[g4.par], bank[7], bank[4], x2T_done)
                if g3:
                    wait(pe, o_ready, 1, g3, 1)
                    transpose(o, bank[5], bank[6], oT_done)
                if g2:
                    keys(g2)
                if g3:
                    out_proj(g3)
                if g4:
                    router(g4)

            skewed(pe, step)

        @block.scalar
        def _(act):
            act.wait_ge(consts_in, 16 * len(loads))
            for src, high, _, _ in splits:
                last = nc.scalar.copy(high[:, :], src[:, :])
            last.then_inc(high_set, 1)
            act.wait_ge(consts_set, 5)

            def inv_std(g, mvx, lnx, rx, mv_sem, ln_sem, r_sem):
                wait(act, mv_sem, 1, g, 1)
                nc.scalar.activation(lnx[:, :], mvx[:, :, 1], ACT.Ln, bias=eps_ln[:, :]).then_inc(ln_sem, 1)
                wait(act, ln_sem, 1, g, 1)
                nc.scalar.activation(rx[:, :], lnx[:, :], ACT.Exp, scale=-0.5).then_inc(r_sem, 1)

            def step(gs):
                _, g1, g2, g3, g4 = gs
                if g1:
                    wait(act, dft_done, 1, g1, 1)
                    wait(act, mel_done, 1, g1)
                    nc.scalar.activation(power[:, :], bank[0][0:BINS, 0:G], ACT.Square).then_inc(power_ready, 1)
                if g2:
                    wait(act, xT_done, 1, g2, 1)
                    wait(act, kv_done, 4, g2)
                    nc.scalar.copy(xa_h[:, :], bank[2][:, 0:G]).then_inc(xh_ready, 1)
                    nc.scalar.copy(xb[0:DB, :], bank[3][0:DB, 0:G]).then_inc(xh_ready, 1)
                if g1:
                    wait(act, mel_done, 1, g1, 1)
                    wait(act, proj_done, 1, g1)
                    nc.scalar.activation(logmel[0:MEL, :], bank[1][0:MEL, 0:G], ACT.Ln, bias=eps_log[:, :]).then_inc(logmel_ready, 1)
                if g2:
                    for n, (e, b, m) in enumerate(((expq_a, bank[2], DA), (expq_b, bank[3], DB))):
                        wait(act, q_done, 2, g2, n + 1)
                        wait(act, q_ready, 2, g2)
                        nc.scalar.activation(e[:, :], b[0:m, 0:G], ACT.Exp).then_inc(expq_ready, 1)
                if g1:
                    wait(act, proj_done, 1, g1, 1)
                    wait(act, hb_ready, 1, g1, less=1)
                    wait(act, xn_ready, 1, g1, less=1)
                    for b in range(2):
                        last = nc.scalar.copy(h[g1.par][:, 2 * b:2 * b + 2, :],
                                              bank[b][0:P, 0:2 * D].rearrange("p (j c) -> p j c", c=D))
                    last.then_inc(h_ready, 1)
                if g4:
                    wait(act, x2T_done, 1, g4, 1)
                    wait(act, router_done, 1, g4, less=1)
                    if not g4.known or g4.n >= 2:
                        act.wait_ge(xT_out[g4.par], g4.half * 32)
                    nc.scalar.copy(x2T_a[g4.par][:, :], bank[7][:, 0:G]).then_inc(x2Ta_ready, 1)
                if g1:
                    inv_std(g1, mv, lnv, rstd, mv_ready, lnv_ready, rstd_ready)
                if g3:
                    wait(act, oT_done, 1, g3, 1)
                    wait(act, wo_done, 1, g3)
                    nc.scalar.copy(oa_h[:, :], bank[5][:, 0:G]).then_inc(oh_ready, 1)
                    nc.scalar.copy(ob[0:DB, :], bank[6][0:DB, 0:G]).then_inc(oh_ready, 1)
                if g2:
                    for j, b in enumerate((4, 2, 3, 4)):
                        wait(act, kv_done, 4, g2, j + 1)
                        wait(act, k_ready, 4, g2)
                        nc.scalar.activation(expk[:, j, :], bank[b][0:P, 0:D], ACT.Exp).then_inc(expk_ready, 1)
                        wait(act, ktv_done, 1, g2, less=1)
                        nc.scalar.copy(v[g2.par][:, j, 0:D], bank[b][0:P, D:2 * D]).then_inc(v_ready, 1)
                if g3:
                    inv_std(g3, mv2, lnv2, rstd2, mv2_ready, lnv2_ready, rstd2_ready)
                if g4:
                    wait(act, router_done, 1, g4, 1)
                    wait(act, sig1_ready, 1, g4)
                    nc.scalar.activation(exps[:, :, :], bank[7][0:P, 0:GT * EXPERTS].rearrange("p (j e) -> p j e", e=EXPERTS),
                                         ACT.Exp, scale=-1.0).then_inc(exps_ready, 1)

            nc.scalar.preload_act_table_set("natural_log_exp_and_others")
            skewed(act, step)

        @block.vector
        def _(dve):
            nc.vector.memset(eps_log[:, :], EPS_LOG).then_inc(consts_set, 1)
            nc.vector.memset(eps_ln[:, :], EPS_LN).then_inc(consts_set, 1)
            nc.vector.memset(logmel[:, :], 1.0).then_inc(consts_set, 1)
            for i in range(2):
                nc.vector.memset(v[i][:, :, D:D + 1], 1.0).then_inc(consts_set, 1)
            dve.wait_ge(cproj_mm, 1)
            nc.vector.tensor_copy(cproj[0:MEL, :], bank[0][0:MEL, 0:D]).then_inc(cproj_set, 1)
            dve.wait_ge(high_set, 1)
            for src, high, low, m in splits:
                last = nc.vector.tensor_tensor(low[:, :], src[0:m, :], high[0:m, :].bitcast(F32), ALU.subtract)
            last.then_inc(low_set, 1)

            def moments(g, src, st, mvx, st_sem, mv_sem):
                for j in range(GT):
                    last = nc.vector.bn_stats(st[:, j, :], src(j))
                last.then_inc(st_sem, 1)
                wait(dve, st_sem, 1, g, 1)
                apart(dve)
                for j in range(GT):
                    last = nc.vector.bn_aggr(mvx[:, j, :], st[:, j, :])
                last.then_inc(mv_sem, 1)

            def relu_plus(g, to, src, e, exp_sem, per, off, min_sem, done):
                wait(dve, exp_sem, per, g, off)
                nc.vector.tensor_scalar(e, e, 1.0, None, ALU.min).then_inc(min_sem, 1)
                wait(dve, min_sem, per, g, off)
                nc.vector.scalar_tensor_tensor(out=to, in0=src, scalar=0.0, in1=e, op0=ALU.max, op1=ALU.add).then_inc(done, 1)

            def step(gs):
                _, g1, g2, g3, g4 = gs
                if g2:
                    for n, (to, b, m, hi) in enumerate(((xa_l[:, :], bank[2], DA, xa_h), (xb[DB:128, :], bank[3], DB, xb))):
                        wait(dve, xh_ready, 2, g2, n + 1)
                        nc.vector.tensor_tensor(to, b[0:m, 0:G], hi[0:m, :].bitcast(F32), ALU.subtract).then_inc(xl_ready, 1)
                if g3:
                    wait(dve, ktv_done, 1, g3, 1)
                    for kvx, ksx, b, m, same in ((kv_a, ks_a, bank[5], DA, same_a), (kv_b, ks_b, bank[6], DB, same_b)):
                        both = b[0:m, 0:2 * (D + 1)].rearrange("p (b c) -> p b c", b=2)
                        nc.vector.tensor_tensor(kvx[:, :, 0:D], both[:, :, 0:D],
                                                same[:, :].unsqueeze(1).to_broadcast([m, 2, D]), ALU.mult)
                        last = nc.vector.tensor_scalar(ksx[:, :], both[:, :, D], 1.0, None, ALU.add)
                    last.then_inc(ks_ready, 1)
                    wait(dve, ks_ready, 1, g3, 1)
                    for kvx, ksx, head in ((kv_a, ks_a, head_a), (kv_b, ks_b, head_b)):
                        for b in range(2):
                            last = nc.vector.tensor_scalar(kvx[:, b, D:D + HEADS], head[:, :], ksx[:, b:b + 1], None, ALU.mult)
                    last.then_inc(kvm_ready, 1)
                if g2:
                    for n, (to, b, e, m) in enumerate(((q_a, bank[2], expq_a, DA), (q_b, bank[3], expq_b, DB))):
                        relu_plus(g2, to[g2.par][:, :], b[0:m, 0:G], e[:, :], expq_ready, 2, n + 1, minq_ready, q_ready)
                if g3:
                    wait(dve, att_done, 1, g3, 1)
                    for b in range(2):
                        both = bank[5 + b][0:P, 0:2 * (D + HEADS)].rearrange("p (j c) -> p j c", j=2)
                        last = nc.vector.tensor_scalar(den[:, 2 * b:2 * b + 2, :], both[:, :, D:D + HEADS], EPS_ATT, None, ALU.add)
                    last.then_inc(den_ready, 1)
                    wait(dve, den_ready, 1, g3, 1)
                    nc.vector.reciprocal(z[:, :, :], den[:, :, :]).then_inc(z_ready, 1)
                    wait(dve, z_ready, 1, g3, 1)
                    for j in range(GT):
                        c0 = (j % 2) * (D + HEADS)
                        last = nc.vector.tensor_tensor(
                            o[:, j, :].rearrange("p (h d) -> p h d", d=DH),
                            bank[5 + j // 2][0:P, c0:c0 + D].rearrange("p (h d) -> p h d", d=DH),
                            z[:, j, :].unsqueeze(2).to_broadcast([P, HEADS, DH]), ALU.mult)
                    last.then_inc(o_ready, 1)
                if g1:
                    wait(dve, h_ready, 1, g1, 1)
                    moments(g1, lambda j: h[g1.par][:, j, :], stats, mv, stats_ready, mv_ready)
                if g4:
                    wait(dve, x2T_done, 1, g4, 1)
                    wait(dve, router_done, 1, g4, less=1)
                    if not g4.known or g4.n >= 2:
                        dve.wait_ge(xT_out[g4.par], g4.half * 32)
                    apart(dve)
                    nc.vector.tensor_copy(x2T_b[g4.par][:, :], bank[4][0:DB, 0:G]).then_inc(x2Tb_ready, 1)
                if g3:
                    for n, (to, b, m, hi) in enumerate(((oa_l[:, :], bank[5], DA, oa_h), (ob[DB:128, :], bank[6], DB, ob))):
                        wait(dve, oh_ready, 2, g3, n + 1)
                        nc.vector.tensor_tensor(to, b[0:m, 0:G], hi[0:m, :].bitcast(F32), ALU.subtract).then_inc(ol_ready, 1)
                if g1:
                    wait(dve, rstd_ready, 1, g1, 1)
                    for j in range(GT):
                        last = nc.vector.tensor_scalar(xn[:, j, :], h[g1.par][:, j, :], mv[:, j, 0:1], rstd[:, j:j + 1],
                                                       ALU.subtract, ALU.mult)
                    last.then_inc(xn_ready, 1)
                if g2:
                    for j, b in enumerate((4, 2, 3, 4)):
                        wait(dve, v_ready, 4, g2, j + 1)
                        relu_plus(g2, k[g2.par][:, j, :], bank[b][0:P, 0:D], expk[:, j, :], expk_ready, 4, j + 1, mink_ready, k_ready)
                if g3:
                    wait(dve, wo_done, 1, g3, 1)
                    wait(dve, hb_ready, 1, g3, 1)
                    if not g3.known or g3.n >= 2:
                        dve.wait_ge(h1_out[g3.par], g3.half * 16)
                    for b in range(2):
                        last = nc.vector.tensor_tensor(h1[g3.par][:, 2 * b:2 * b + 2, :], hb[g3.par][:, 2 * b:2 * b + 2, :],
                                                       bank[5 + b][0:P, 0:2 * D].rearrange("p (j c) -> p j c", c=D), ALU.add)
                    last.then_inc(h1_ready, 1)
                    wait(dve, h1_ready, 1, g3, 1)
                    moments(g3, lambda j: h1[g3.par][:, j, :], stats2, mv2, stats2_ready, mv2_ready)
                if g4:
                    wait(dve, exps_ready, 1, g4, 1)
                    nc.vector.tensor_scalar(sig[:, :, :], exps[:, :, :], 1.0, None, ALU.add).then_inc(sig1_ready, 1)
                    wait(dve, sig1_ready, 1, g4, 1)
                    nc.vector.reciprocal(row[g4.par][:, :, D:ROW], sig[:, :, :]).then_inc(sig_ready, 1)
                    wait(dve, sig_ready, 1, g4, 1)
                    apart(dve)
                    nc.vector.tensor_copy(scores_tm[:, bass.ds(g4.n * GT, GT), :], row[g4.par][:, :, D:ROW]).then_inc(scores_ready, 1)
                if g3:
                    wait(dve, rstd2_ready, 1, g3, 1)
                    if not g3.known or g3.n >= 2:
                        dve.wait_ge(rows_out[g3.par], g3.half * 16)
                    for j in range(GT):
                        last = nc.vector.tensor_scalar(row[g3.par][:, j, 0:D], h1[g3.par][:, j, :], mv2[:, j, 0:1],
                                                       rstd2[:, j:j + 1], ALU.subtract, ALU.mult)
                    last.then_inc(x2_ready, 1)

            skewed(dve, step)


def shared_phase(nc, io, resident):
    scores_tm, ident = resident["scores_tm"], resident["ident"]
    NF = FS // 128
    BITS = 30
    SEARCH, TIES, REST = 2, 2 + BITS // 2, 26
    with ExitStack() as ctx:
        def sb(name, shape, dt=F32):
            return ctx.enter_context(nc.sbuf_tensor(name, shape, dt))

        def sem(name):
            return ctx.enter_context(nc.semaphore(name))

        bank = [ctx.enter_context(nc.psum_tensor(f"sh_bank{i}", [128, 512], F32)) for i in range(8)]
        raw_ga, raw_gb, raw_ua, raw_ub = (sb(f"sh_{n}", [128, FS]) for n in ("raw_ga", "raw_gb", "raw_ua", "raw_ub"))
        raw_d = sb("sh_raw_d", [128, NF, D])
        ga_h, ga_l, gb_h, ua_h, ua_l, ub_h = (sb(f"sh_{n}", [128, FS], F32R) for n in ("ga_h", "ga_l", "gb_h", "ua_h", "ua_l", "ub_h"))
        gb_l, ub_l = (sb(f"sh_{n}", [DB, FS], F32R) for n in ("gb_l", "ub_l"))
        wd = sb("sh_wd", [128, NF, 2 * D], F32R)
        x_a = [sb(f"sh_x_a{i}", [DA, G]) for i in range(2)]
        x_b = [sb(f"sh_x_b{i}", [DB, G]) for i in range(2)]
        xa_h, xa_l, xb = ([sb(f"sh_{n}{i}", [128, G], F32R) for i in range(2)] for n in ("xa_h", "xa_l", "xb"))
        silu = [sb(f"sh_silu{i}", [128, G]) for i in range(2)]
        hf = [sb(f"sh_hf{i}", [128, G]) for i in range(2)]
        h_h, h_l = ([sb(f"sh_{n}{i}", [128, NF, G], F32R) for i in range(2)] for n in ("h_h", "h_l"))
        h1 = [sb(f"sh_h1_{i}", [P, GT, D]) for i in range(2)]
        half_y = [sb(f"half_y{i}", [P, D]) for i in range(2)]
        y = [sb(f"sh_y{i}", [P, GT, D]) for i in range(2)]

        same, before = sb("same", [128, 128]), sb("before", [128, 128])
        by_piece = sb("by_piece", [P, CT * 128])
        s = sb("s", [128, CLEN])
        mark = sb("mark", [128, CLEN], BF16)
        above, equal, ties, chosen, slot, slot_q, slot_p = (sb(n, [128, CLEN]) for n in (
            "above", "equal", "ties", "chosen", "slot", "quot", "rest"))
        zero, bit_f, count = sb("zero", [128, 1]), sb("bit_f", [128, 1]), sb("count", [128, 1])
        bit, thr, cand, keep = (sb(n, [128, 1], I32) for n in ("bit", "thr", "cand", "keep"))
        room, offset = sb("room", [128, 1]), sb("offset", [128, 1])

        weights_in, high_set, low_set = sem("sh_weights_in"), sem("sh_high_set"), sem("sh_low_set")
        x_in, h1_in, y_out = ([sem(f"sh_{n}{i}") for i in range(2)] for n in ("x_in", "h1_in", "y_out"))
        xh_ready, xal_ready, xbl_ready = sem("sh_xh_ready"), sem("sh_xal_ready"), sem("sh_xbl_ready")
        gu_done, silu_ready, hf_ready, hh_ready, hl_ready = (sem(f"sh_{n}") for n in (
            "gu_done", "silu_ready", "hf_ready", "hh_ready", "hl_ready"))
        down_done, half_ready, y_ready = sem("sh_down_done"), sem("sh_half_ready"), sem("sh_y_ready")

        mats_in, by_piece_ready, s_done, s_ready, init_set = (sem(n) for n in ("mats_in", "by_piece_ready", "s_done", "s_ready", "init_set"))
        cand_ready, count_ready, total_done, keep_ready, thr_ready, bit_ready = (sem(n) for n in (
            "cand_ready", "count_ready", "total_done", "keep_ready", "thr_ready", "bit_ready"))
        ties_ready, offsets_done, chosen_ready, slots_ready = (sem(n) for n in (
            "ties_ready", "offsets_done", "chosen_ready", "slots_ready"))
        link, maps_done, maps_read = sem("link"), sem("maps_done"), sem("maps_read")
        block = ctx.enter_context(nc.Block())

        def over_groups(eng, step):
            def known(n):
                step(Group(n, n // 2, n % 2, True), SEARCH <= n < TIES)

            def loop(first, end, search):
                with eng.Fori(0, (end - first) // 2) as i:
                    for par in range(2):
                        step(Group(i * 2 + (first + par), i + first // 2, par, False), search)

            for n in range(SEARCH + 2):
                known(n)
            loop(SEARCH + 2, TIES - 1, True)
            for n in range(TIES - 1, REST):
                known(n)
            loop(REST, GROUPS - 2, False)
            known(GROUPS - 2)
            known(GROUPS - 1)

        def later(g, by):
            par = (g.par + by) % 2
            if g.known and not 0 <= g.n + by < GROUPS:
                return None
            return Group(g.n + by, g.half + (g.par + by - par) // 2, par, g.known)

        FIRST = Group(0, 0, 0, True)
        LAST = Group(GROUPS - 1, (GROUPS - 1) // 2, (GROUPS - 1) % 2, True)

        def bit_no(g, second):
            return g.n * 2 + (second - 2 * SEARCH)

        def at(g, n):
            return g.known and g.n == n

        @block.sync
        def _(sp):
            for a, b, src in ((raw_ga, raw_gb, io["wsgT"]), (raw_ua, raw_ub, io["wsuT"])):
                sp.dma_start(a[:, :], src[0:DA, :]).then_inc(weights_in, 16)
                sp.dma_start(b[0:DB, :], src[DA:D, :]).then_inc(weights_in, 16)
                sp.dma_start(b[DB:128, :], src[DA:D, :]).then_inc(weights_in, 16)
            sp.dma_start(raw_d[:, :, :], io["wsdT"].rearrange("(c p) n -> p c n", p=128)).then_inc(weights_in, 16)

            def by_tile(g):
                return io["out"][bass.ds(g.n * G, G), :].rearrange("(j p) c -> p j c", p=P)

            def load_x(g):
                wait_alone(sp, xh_ready, 2, g, less=1)
                wait_alone(sp, xal_ready, 1, g, less=1)
                wait_alone(sp, xbl_ready, 1, g, less=1)
                sp.dma_start(x_a[g.par][:, :], io["x2T"][0:DA, bass.ds(g.n * G, G)]).then_inc(x_in[g.par], 16)
                sp.dma_start(x_b[g.par][:, :], io["x2T"][DA:D, bass.ds(g.n * G, G)]).then_inc(x_in[g.par], 16)

            def load_h1(g):
                wait_alone(sp, y_ready, GT, g, less=1)
                sp.dma_start(h1[g.par][:, :, :], by_tile(g)).then_inc(h1_in[g.par], 16)

            def store(g):
                wait_alone(sp, y_ready, GT, g, GT)
                sp.dma_start(by_tile(g), y[g.par][:, :, :]).then_inc(y_out[g.par], 16)

            load_x(FIRST)
            load_h1(FIRST)
            sp.dma_start(same[:, :], io["same_expert"]).then_inc(mats_in, 16)
            sp.dma_start(before[:, :], io["before"]).then_inc(mats_in, 16)

            def step(g, search):
                if later(g, 1):
                    load_x(later(g, 1))
                if later(g, -1):
                    store(later(g, -1))
                if later(g, 1):
                    load_h1(later(g, 1))

            over_groups(sp, step)
            store(LAST)
            for i in range(2):
                sp.wait_ge(y_out[i], 16 * (GROUPS // 2))

        @block.gpsimd
        def _(pool):
            def x_low(g):
                wait(pool, xh_ready, 2, g, 1)
                wait(pool, gu_done, 2 * NF, g, less=1)
                nc.gpsimd.tensor_tensor(xa_l[g.par][:, :], x_a[g.par][:, :], xa_h[g.par][:, :].bitcast(F32), ALU.subtract).then_inc(xal_ready, 1)

            def h_low(g, f):
                wait(pool, hh_ready, NF, g, f + 1)
                nc.gpsimd.tensor_tensor(h_l[g.par][:, f, :], hf[(g.par + f) % 2][:, :], h_h[g.par][:, f, :].bitcast(F32),
                                        ALU.subtract).then_inc(hl_ready, 1)

            x_low(FIRST)

            def step(g, search):
                h_low(g, 0)
                h_low(g, 1)
                if later(g, 1):
                    x_low(later(g, 1))
                h_low(g, 2)

            over_groups(pool, step)

        @block.tensor
        def _(pe):
            def up(g, f):
                if f == 0:
                    wait(pe, xal_ready, 1, g, 1)
                    wait(pe, xbl_ready, 1, g, 1)
                s, cols = g.par, slice(f * 128, (f + 1) * 128)
                for w, (a_h, a_l, b_h, b_l) in enumerate(((ga_h, ga_l, gb_h, gb_l), (ua_h, ua_l, ub_h, ub_l))):
                    wait(pe, (silu_ready, hf_ready)[w], NF, g, f - 1)
                    to = bank[2 * ((g.par + f) % 2) + w][:, 0:G]
                    nc.tensor.matmul(to, a_h[:, cols], xa_h[s][:, :], start=True, stop=False)
                    nc.tensor.matmul(to, a_l[:, cols], xa_h[s][:, :], start=False, stop=False)
                    nc.tensor.matmul(to, a_h[:, cols], xa_l[s][:, :], start=False, stop=False)
                    nc.tensor.matmul(to, b_h[:, cols], xb[s][:, :], start=False, stop=False)
                    nc.tensor.matmul(to, b_l[:, cols], xb[s][0:DB, :], start=False, stop=True).then_inc(gu_done, 1)

            def down(g):
                wait(pe, hl_ready, NF, g, NF)
                for j in range(GT):
                    wait(pe, y_ready, GT, g, j - 1)
                    cols, to = slice(j * P, (j + 1) * P), bank[4 + j % 2]
                    for f in range(NF):
                        nc.tensor.matmul(to[0:P, 0:2 * D], h_h[g.par][:, f, cols], wd[:, f, :], start=(f == 0), stop=False)
                        last = nc.tensor.matmul(to[0:P, 0:D], h_l[g.par][:, f, cols], wd[:, f, 0:D], start=False, stop=(f == NF - 1))
                    last.then_inc(down_done, 1)

            def total(it):
                pe.wait_ge(count_ready, it + 1)
                nc.tensor.matmul(bank[7][:, 0:1], same[:, :], count[:, :], start=True, stop=True).then_inc(total_done, 1)

            def scores_rows(first):
                for b in range(first, first + 8):
                    nc.tensor.transpose(bank[6 + b % 8 // 4][:, (b % 4) * P:(b % 4 + 1) * P],
                                        by_piece[:, b * 128:(b + 1) * 128], ident[0:P, 0:P]).then_inc(s_done, 1)

            def map_back(n, src, first):
                if n:
                    pe.wait_ge(maps_read, 2 * n)
                for b in range(first, first + 8):
                    last = nc.tensor.transpose(bank[6 + b % 8 // 4][0:P, (b % 4) * 128:(b % 4 + 1) * 128],
                                               src[:, b * P:(b + 1) * P], ident[:, :])
                    if b % 4 == 3:
                        last.then_inc(maps_done, 1)

            pe.wait_ge(low_set, 1)
            pe.wait_ge(mats_in, 32)

            def step(g, search):
                up(g, 0)
                if (search and not at(g, SEARCH)) or at(g, TIES):
                    total(bit_no(g, -1))
                if at(g, TIES + 3):
                    pe.wait_ge(chosen_ready, 1)
                    nc.tensor.matmul(bank[7][:, 3:4], before[:, :], slot[:, CLEN - 1:CLEN], start=True, stop=True).then_inc(offsets_done, 1)
                up(g, 1)
                if later(g, -1):
                    down(later(g, -1))
                if search:
                    total(bit_no(g, 0))
                if at(g, 0):
                    pe.wait_ge(by_piece_ready, 1)
                    scores_rows(0)
                if at(g, 1):
                    pe.wait_ge(s_ready, 1)
                    scores_rows(8)
                if at(g, TIES + 1):
                    pe.wait_ge(ties_ready, 1)
                    nc.tensor.matmul(bank[7][:, 1:2], same[:, :], count[:, :], start=True, stop=True)
                    nc.tensor.matmul(bank[7][:, 2:3], before[:, :], ties[:, CLEN - 1:CLEN], start=True, stop=True).then_inc(offsets_done, 1)
                for n, (src, first) in enumerate(((slot_q, 0), (slot_q, 8), (slot_p, 0), (slot_p, 8))):
                    if at(g, TIES + 4 + n):
                        if n == 0:
                            pe.wait_ge(slots_ready, 1)
                        map_back(n, src, first)
                up(g, 2)

            over_groups(pe, step)
            down(LAST)

        @block.scalar
        def _(act):
            act.wait_ge(weights_in, 7 * 16)
            for high, src in ((ga_h, raw_ga), (gb_h, raw_gb), (ua_h, raw_ua), (ub_h, raw_ub)):
                nc.scalar.copy(high[:, :], src[:, :])
            nc.scalar.copy(wd[:, :, 0:D], raw_d[:, :, :]).then_inc(high_set, 1)

            def x_high(g):
                act.wait_ge(x_in[g.par], (g.half + 1) * 32)
                wait(act, gu_done, 2 * NF, g, less=1)
                nc.scalar.copy(xa_h[g.par][:, :], x_a[g.par][:, :]).then_inc(xh_ready, 1)
                nc.scalar.copy(xb[g.par][0:DB, :], x_b[g.par][:, :]).then_inc(xh_ready, 1)

            def gate(g, f):
                m = (g.par + f) % 2
                wait(act, gu_done, 2 * NF, g, 2 * f + 1)
                wait(act, hf_ready, NF, g, f - 1)
                nc.scalar.activation(silu[m][:, :], bank[2 * m][:, 0:G], ACT.Silu).then_inc(silu_ready, 1)

            def h_high(g, f):
                wait(act, hf_ready, NF, g, f + 1)
                wait(act, down_done, GT, g, less=1)
                nc.scalar.copy(h_h[g.par][:, f, :], hf[(g.par + f) % 2][:, :]).then_inc(hh_ready, 1)

            x_high(FIRST)

            def step(g, search):
                gate(g, 0)
                gate(g, 1)
                h_high(g, 0)
                h_high(g, 1)
                if later(g, 1):
                    x_high(later(g, 1))
                gate(g, 2)
                h_high(g, 2)

            over_groups(act, step)

        @block.vector
        def _(dve):
            links = [0]

            def then(instruction):
                links[0] += 1
                instruction.then_inc(link, 1)
                dve.wait_ge(link, links[0])

            def x_low(g):
                wait(dve, xh_ready, 2, g, 2)
                wait(dve, gu_done, 2 * NF, g, less=1)
                nc.vector.tensor_tensor(xb[g.par][DB:128, :], x_b[g.par][:, :], xb[g.par][0:DB, :].bitcast(F32), ALU.subtract).then_inc(xbl_ready, 1)

            def product(g, f):
                m = (g.par + f) % 2
                wait(dve, silu_ready, NF, g, f + 1)
                wait(dve, gu_done, 2 * NF, g, 2 * f + 2)
                wait(dve, hl_ready, NF, g, f - 1)
                nc.vector.tensor_tensor(hf[m][:, :], silu[m][:, :], bank[2 * m + 1][:, 0:G], ALU.mult).then_inc(hf_ready, 1)

            def y_sum(g):
                dve.wait_ge(h1_in[g.par], (g.half + 1) * 16)
                if not g.known or g.n >= 2:
                    dve.wait_ge(y_out[g.par], g.half * 16)
                for j in range(GT):
                    wait(dve, down_done, GT, g, j + 1)
                    wait(dve, y_ready, GT, g, j - 1)
                    nc.vector.tensor_tensor(half_y[j % 2][:, :], bank[4 + j % 2][0:P, 0:D], h1[g.par][:, j, :], ALU.add).then_inc(half_ready, 1)
                    wait(dve, half_ready, GT, g, j + 1)
                    nc.vector.tensor_tensor(y[g.par][:, j, :], half_y[j % 2][:, :], bank[4 + j % 2][0:P, D:2 * D], ALU.add).then_inc(y_ready, 1)

            def try_bit(it):
                dve.wait_ge(bit_ready, it + 1)
                nc.vector.tensor_tensor(cand[:, :], thr[:, :], bit[:, :], ALU.bitwise_or).then_inc(cand_ready, 1)
                dve.wait_ge(cand_ready, it + 1)
                nc.vector.tensor_scalar(mark[:, :], s[:, :], cand[:, :].bitcast(F32), None, ALU.is_ge, ALU.add,
                                        accum_out=count[:, :]).then_inc(count_ready, 1)

            def settle_bit(it):
                dve.wait_ge(total_done, it + 1)
                nc.vector.tensor_scalar(keep[:, :], bank[7][:, 0:1], float(CAP), bit_f[:, :], ALU.is_ge, ALU.mult).then_inc(keep_ready, 1)
                dve.wait_ge(keep_ready, it + 1)
                nc.vector.tensor_scalar(bit_f[:, :], bit_f[:, :], 0.5, None, ALU.mult)
                nc.vector.tensor_tensor(thr[:, :], thr[:, :], keep[:, :], ALU.bitwise_or).then_inc(thr_ready, 1)
                dve.wait_ge(thr_ready, it + 1)
                nc.vector.tensor_copy(bit[:, :], bit_f[:, :]).then_inc(bit_ready, 1)

            def rows_read(first):
                for b in range(first, first + 8, 4):
                    dve.wait_ge(s_done, b + 4)
                    last = nc.vector.tensor_copy(s[:, b * P:(b + 4) * P], bank[6 + b % 8 // 4][:, 0:4 * P])
                last.then_inc(s_ready, 1)

            def map_read(n, to, first):
                view = to[:, :, :].rearrange("p e (c b) -> p b c e", b=CT)
                for i in range(2):
                    dve.wait_ge(maps_done, 2 * n + i + 1)
                    b = first + 4 * i
                    nc.vector.tensor_copy(view[:, b:b + 4], bank[6 + i][0:P, :].rearrange(
                        "p (b c e) -> p b c e", b=4, c=CHUNKS)).then_inc(maps_read, 1)

            nc.vector.tensor_copy(by_piece[:, :].rearrange("p (b c e) -> p c b e", b=CT, c=CHUNKS),
                                  scores_tm[:, :, :].rearrange("p (c b) e -> p c b e", b=CT)).then_inc(by_piece_ready, 1)
            nc.vector.memset(zero[:, :], 0.0)
            nc.vector.memset(bit_f[:, :], float(2 ** (BITS - 1)))
            nc.vector.memset(thr[:, :], 0).then_inc(init_set, 1)
            dve.wait_ge(init_set, 1)
            nc.vector.tensor_copy(bit[:, :], bit_f[:, :]).then_inc(bit_ready, 1)
            dve.wait_ge(high_set, 1)
            for low, src, high, m in ((ga_l, raw_ga, ga_h, 128), (gb_l, raw_gb, gb_h, DB), (ua_l, raw_ua, ua_h, 128), (ub_l, raw_ub, ub_h, DB)):
                nc.vector.tensor_tensor(low[:, :], src[0:m, :], high[0:m, :].bitcast(F32), ALU.subtract)
            nc.vector.tensor_tensor(wd[:, :, D:2 * D], raw_d[:, :, :], wd[:, :, 0:D].bitcast(F32), ALU.subtract).then_inc(low_set, 1)
            x_low(FIRST)

            def step(g, search):
                if (search and not at(g, SEARCH)) or at(g, TIES):
                    settle_bit(bit_no(g, -1))
                if search:
                    try_bit(bit_no(g, 0))
                best = thr[:, :].bitcast(F32)
                if at(g, TIES):
                    dve.wait_ge(thr_ready, BITS)
                    then(nc.vector.tensor_scalar(above[:, :], s[:, :], best, None, ALU.is_gt, ALU.add, accum_out=count[:, :]))
                if at(g, TIES + 1):
                    nc.vector.tensor_tensor_scan(ties[:, :], equal[:, :], zero[:, :].to_broadcast([128, CLEN]), 0.0,
                                                 ALU.add, ALU.add).then_inc(ties_ready, 1)
                if at(g, TIES + 2):
                    then(nc.vector.tensor_tensor(chosen[:, :], chosen[:, :], above[:, :], ALU.add))
                if at(g, TIES + 3):
                    dve.wait_ge(offsets_done, 2)
                    then(nc.vector.tensor_copy(offset[:, :], bank[7][:, 3:4]))
                    then(nc.vector.scalar_tensor_tensor(out=slot[:, :], in0=slot[:, :], scalar=offset[:, :], in1=chosen[:, :],
                                                        op0=ALU.add, op1=ALU.mult))
                if at(g, TIES + 4):
                    nc.vector.scalar_tensor_tensor(out=slot_p[:, :], in0=slot_q[:, :], scalar=float(-P), in1=slot[:, :],
                                                   op0=ALU.mult, op1=ALU.add).then_inc(slots_ready, 1)
                product(g, 0)
                product(g, 1)
                if later(g, -1):
                    y_sum(later(g, -1))
                if search:
                    settle_bit(bit_no(g, 0))
                    try_bit(bit_no(g, 1))
                if at(g, 0):
                    rows_read(0)
                if at(g, 1):
                    rows_read(8)
                    dve.wait_ge(s_ready, 2)
                if at(g, TIES):
                    then(nc.vector.tensor_scalar(equal[:, :], s[:, :], best, None, ALU.is_equal))
                if at(g, TIES + 1):
                    dve.wait_ge(offsets_done, 1)
                    then(nc.vector.tensor_scalar(room[:, :], bank[7][:, 1:2], -1.0, float(CAP), ALU.mult, ALU.add))
                    then(nc.vector.tensor_tensor(room[:, :], room[:, :], bank[7][:, 2:3], ALU.subtract))
                    then(nc.vector.scalar_tensor_tensor(out=chosen[:, :], in0=ties[:, :], scalar=room[:, :], in1=equal[:, :],
                                                        op0=ALU.is_le, op1=ALU.mult))
                if at(g, TIES + 2):
                    nc.vector.tensor_tensor_scan(slot[:, :], chosen[:, :], zero[:, :].to_broadcast([128, CLEN]), 0.0,
                                                 ALU.add, ALU.add).then_inc(chosen_ready, 1)
                if at(g, TIES + 3):
                    then(nc.vector.tensor_scalar(slot_q[:, :], slot[:, :], 1.0 / P, -(P // 2 + 1) / P, ALU.mult, ALU.add))
                    then(nc.vector.tensor_scalar(slot_q[:, :], slot_q[:, :], ROUND, ROUND, ALU.add, ALU.subtract))
                for n, (to, first) in enumerate(((resident["slot_q"], 0), (resident["slot_q"], 8),
                                                 (resident["slot_p"], 0), (resident["slot_p"], 8))):
                    if at(g, TIES + 4 + n):
                        map_read(n, to, first)
                product(g, 2)
                if later(g, 1):
                    x_low(later(g, 1))

            over_groups(dve, step)
            y_sum(LAST)


def experts_phase(nc, io, resident):
    ident = resident["ident"]
    NF = FE // 128
    NG = CAP // G
    OHT = 16
    NCH = TILES // OHT
    AT = {(g, f): c for c, (g, f) in enumerate([(g, f) for g in range(NG - 1) for f in (2, 3, 4)][:NCH])}
    NLOAD, NHIGH = 7, 5
    with ExitStack() as ctx:
        def sb(name, shape, dt=F32):
            return ctx.enter_context(nc.sbuf_tensor(name, shape, dt))

        def sem(name):
            return ctx.enter_context(nc.semaphore(name))

        bank = [ctx.enter_context(nc.psum_tensor(f"ex_bank{i}", [128, 512], F32)) for i in range(8)]
        raw_ga, raw_gb, raw_ua, raw_ub = (sb(n, [128, FE]) for n in ("raw_ga", "raw_gb", "raw_ua", "raw_ub"))
        raw_d = sb("raw_d", [128, NF, D])
        ga_h, ga_l, gb_h, ua_h, ua_l, ub_h = ([sb(f"{n}{i}", [128, FE], F32R) for i in range(2)] for n in (
            "ga_h", "ga_l", "gb_h", "ua_h", "ua_l", "ub_h"))
        gb_l, ub_l = ([sb(f"{n}{i}", [DB, FE], F32R) for i in range(2)] for n in ("gb_l", "ub_l"))
        wd = [sb(f"wd{i}", [128, NF, 2 * D], F32R) for i in range(2)]
        xg = [sb(f"xg{i}", [P, GT, ROW]) for i in range(2)]
        score = [sb(f"score{i}", [P, GT]) for i in range(2)]
        xa_h, xa_l, xb = ([sb(f"{n}{i}", [128, G], F32R) for i in range(2)] for n in ("xa_h", "xa_l", "xb"))
        silu = [sb(f"ex_silu{i}", [128, G]) for i in range(2)]
        hf = [sb(f"hf{i}", [128, G]) for i in range(2)]
        h_h, h_l = ([sb(f"{n}{i}", [128, NF, G], F32R) for i in range(2)] for n in ("h_h", "h_l"))
        yb = [sb(f"yb{i}", [P, D]) for i in range(2)]
        yo = [sb(f"yo{i}", [P, GT, D]) for i in range(2)]
        iota_f = sb("iota_f", [P, P + 1 + EXPERTS + TILES])
        iota_p, iota_q, tile_no = sb("iota_p", [P, P, OHT], BF16), sb("iota_q", [P, EXPERTS, TILES], BF16), sb("tile_no", [P, TILES], BF16)
        is_q = sb("is_q", [P, EXPERTS, TILES], BF16)
        list_rhs = sb("list_rhs", [P, 2 * EXPERTS, TILES], BF16)
        is_p = [sb(f"is_p{i}", [P, P, OHT], BF16) for i in range(2)]
        place = sb("place", [P, EXPERTS])
        index = [sb(f"index{i}", [P, EXPERTS], U32) for i in range(2)]

        iota_in, iota_set = sem("iota_in"), sem("iota_set")
        weights_in, high_ready, split_ready = sem("weights_in"), sem("high_ready"), sem("split_ready")
        isq_ready, rhs_ready, isp_ready, list_done, place_ready, index_ready = (sem(n) for n in (
            "isq_ready", "rhs_ready", "isp_ready", "list_done", "place_ready", "index_ready"))
        gathered = [sem(f"gathered{i}") for i in range(2)]
        added = [sem(f"added{i}") for i in range(2)]
        score_ready, tr_done = sem("score_ready"), sem("tr_done")
        xah_ready, xal_ready, xbh_ready, xbl_ready = (sem(n) for n in ("xah_ready", "xal_ready", "xbh_ready", "xbl_ready"))
        gu_done, silu_ready, hf_ready, hh_ready, hl_ready = (sem(n) for n in (
            "ex_gu_done", "ex_silu_ready", "hf_ready", "hh_ready", "hl_ready"))
        down_done, yb_ready, yo_ready = sem("ex_down_done"), sem("yb_ready"), sem("yo_ready")
        block = ctx.enter_context(nc.Block())

        def over_experts(eng, step):
            def known(n):
                for g in range(NG):
                    step(Group(n, n // 2, n % 2, True), g)

            known(0)
            known(1)
            with eng.Fori(0, EXPERTS // 2 - 2) as i:
                for par in range(2):
                    for g in range(NG):
                        step(Group(i * 2 + (2 + par), i + 1, par, False), g)
            known(EXPERTS - 2)
            known(EXPERTS - 1)

        def later(e, by):
            par = (e.par + by) % 2
            if e.known and e.n + by >= EXPERTS:
                return None
            return Group(e.n + by, e.half + (e.par + by - par) // 2, par, e.known)

        def following(e, g):
            return (e, g + 1) if g + 1 < NG else (later(e, 1), 0)

        def preceding(e, g):
            if g:
                return e, g - 1
            return (None if e.known and e.n == 0 else later(e, -1)), NG - 1

        FIRST = Group(0, 0, 0, True)
        LAST = Group(EXPERTS - 1, (EXPERTS - 1) // 2, (EXPERTS - 1) % 2, True)

        @block.sync
        def _(sp):
            sp.dma_start(iota_f[:, :], io["iotas"]).then_inc(iota_in, 16)

            def load(e):
                wait_alone(sp, split_ready, 1, e)
                gate, up = io["wgT"][bass.ds(e.n * D, D), :], io["wuT"][bass.ds(e.n * D, D), :]
                for src, a, b in ((gate, raw_ga, raw_gb), (up, raw_ua, raw_ub)):
                    sp.dma_start(a[:, :], src[0:DA, :]).then_inc(weights_in, 16)
                    sp.dma_start(b[0:DB, :], src[DA:D, :]).then_inc(weights_in, 16)
                    sp.dma_start(b[DB:128, :], src[DA:D, :]).then_inc(weights_in, 16)
                sp.dma_start(raw_d[:, :, :], io["wdT"][bass.ds(e.n * FE, FE), :].rearrange("(c p) n -> p c n", p=128)).then_inc(weights_in, 16)

            load(FIRST)

            def step(e, g):
                if g == 0 and later(e, 1):
                    load(later(e, 1))

            over_experts(sp, step)

        @block.gpsimd
        def _(pool):
            def split_low(e, part):
                p = e.par
                wait(pool, high_ready, NHIGH, e, (2, NHIGH)[part])
                if part == 0:
                    for dst, src, hi in ((ga_l, raw_ga, ga_h), (ua_l, raw_ua, ua_h)):
                        nc.gpsimd.tensor_tensor(dst[p][:, :], src[:, :], hi[p][:, :].bitcast(F32), ALU.subtract)
                else:
                    for dst, src, hi in ((gb_l, raw_gb, gb_h), (ub_l, raw_ub, ub_h)):
                        nc.gpsimd.tensor_tensor(dst[p][:, :], src[0:DB, :], hi[p][0:DB, :].bitcast(F32), ALU.subtract)
                    nc.gpsimd.tensor_tensor(wd[p][:, :, D:2 * D], raw_d[:, :, :], wd[p][:, :, 0:D].bitcast(F32),
                                            ALU.subtract).then_inc(split_ready, 1)

            def gather(e, g):
                wait(pool, index_ready, 1, e, 1)
                wait(pool, tr_done, 2 * NG, e, 2 * (g - 1))
                wait(pool, score_ready, NG, e, g - 1)
                apart(pool)
                for j in range(GT):
                    n = g * GT + j
                    nc.gpsimd.indirect_dma_start(
                        out=xg[g % 2][:, j, :], out_offset=None, in_=io["rows"],
                        in_offset=bass.IndirectOffsetOnAxis(ap=index[e.par][:, n:n + 1], axis=0)).then_inc(gathered[g % 2], 16)

            def scatter(e, g):
                if g == 0:
                    for i in range(2):
                        wait(pool, added[i], 16 * GT * NG // 2, e)
                for j in range(GT):
                    n = g * GT + j
                    wait(pool, yo_ready, NG * GT, e, n + 1)
                    apart(pool)
                    nc.gpsimd.indirect_dma_start(
                        out=io["out"], out_offset=bass.IndirectOffsetOnAxis(ap=index[e.par][:, n:n + 1], axis=0),
                        in_=yo[g % 2][:, j, :], in_offset=None, compute_op=ALU.add).then_inc(added[g % 2], 16)

            split_low(FIRST, 0)
            split_low(FIRST, 1)
            gather(FIRST, 0)

            def step(e, g):
                ne, ng = following(e, g)
                if ne:
                    gather(ne, ng)
                after = later(e, 1)
                if after and g in (1, 2):
                    split_low(after, g - 1)
                pe_, pg = preceding(e, g)
                if pe_:
                    scatter(pe_, pg)

            over_experts(pool, step)
            scatter(LAST, NG - 1)
            for i in range(2):
                pool.wait_ge(added[i], EXPERTS * 16 * GT * NG // 2)

        @block.tensor
        def _(pe):
            def list_tokens(e, c):
                if c == 0:
                    wait(pe, rhs_ready, 1, e, 1)
                    wait(pe, index_ready, 1, e)
                wait(pe, isp_ready, NCH, e, c + 1)
                for t in range(OHT):
                    n = c * OHT + t
                    last = nc.tensor.matmul(bank[7][0:P, 0:2 * EXPERTS], is_p[c % 2][:, :, t], list_rhs[:, :, n],
                                            start=(n == 0), stop=(n == TILES - 1))
                last.then_inc(list_done, 1)

            def transpose(e, g, part):
                if part == 0:
                    wait(pe, gathered[g % 2], 16 * GT * NG // 2, e, 16 * GT * (g // 2 + 1))
                    wait(pe, xbl_ready, NG, e, g)
                else:
                    wait(pe, xal_ready, NG, e, g + 1)
                apart(pe)
                c0, m = ((0, DA), (DA, DB))[part]
                for j in range(GT):
                    last = nc.tensor.transpose(bank[6][0:m, j * P:(j + 1) * P], xg[g % 2][:, j, c0:c0 + m], ident[0:P, 0:P])
                last.then_inc(tr_done, 1)

            def up(e, g, f):
                if f == 0:
                    wait(pe, split_ready, 1, e, 1)
                    wait(pe, xal_ready, NG, e, g + 1)
                    wait(pe, xbl_ready, NG, e, g + 1)
                p, s, cols = e.par, g % 2, slice(f * 128, (f + 1) * 128)
                for w, (a_h, a_l, b_h, b_l) in enumerate(((ga_h, ga_l, gb_h, gb_l), (ua_h, ua_l, ub_h, ub_l))):
                    wait(pe, (silu_ready, hf_ready)[w], NG * NF, e, NF * g + f - 1)
                    to = bank[2 * (f % 2) + w][:, 0:G]
                    nc.tensor.matmul(to, a_h[p][:, cols], xa_h[s][:, :], start=True, stop=False)
                    nc.tensor.matmul(to, a_l[p][:, cols], xa_h[s][:, :], start=False, stop=False)
                    nc.tensor.matmul(to, a_h[p][:, cols], xa_l[s][:, :], start=False, stop=False)
                    nc.tensor.matmul(to, b_h[p][:, cols], xb[s][:, :], start=False, stop=False)
                    nc.tensor.matmul(to, b_l[p][:, cols], xb[s][0:DB, :], start=False, stop=True).then_inc(gu_done, 1)

            def down(e, g):
                wait(pe, hl_ready, NG * NF, e, NF * (g + 1))
                for j in range(GT):
                    wait(pe, yo_ready, NG * GT, e, GT * g + j - 1)
                    cols = slice(j * P, (j + 1) * P)
                    to = bank[4 + j % 2]
                    for f in range(NF):
                        nc.tensor.matmul(to[0:P, 0:2 * D], h_h[g % 2][:, f, cols], wd[e.par][:, f, :], start=(f == 0), stop=False)
                        last = nc.tensor.matmul(to[0:P, 0:D], h_l[g % 2][:, f, cols], wd[e.par][:, f, 0:D],
                                                start=False, stop=(f == NF - 1))
                    last.then_inc(down_done, 1)

            for c in range(NCH):
                list_tokens(FIRST, c)
            transpose(FIRST, 0, 0)
            transpose(FIRST, 0, 1)

            def step(e, g):
                ne, ng = following(e, g)
                after = later(e, 1)
                for f in range(NF):
                    up(e, g, f)
                    if f == 1:
                        pe_, pg = preceding(e, g)
                        if pe_:
                            down(pe_, pg)
                    if f == 2 and ne:
                        transpose(ne, ng, 0)
                    if f == 4 and ne:
                        transpose(ne, ng, 1)
                    if after and (g, f - 1) in AT:
                        list_tokens(after, AT[g, f - 1])

            over_experts(pe, step)
            down(LAST, NG - 1)

        @block.scalar
        def _(act):
            def x_high(e, g, part):
                wait(act, tr_done, 2 * NG, e, 2 * g + part + 1)
                wait(act, gu_done, 2 * NF * NG, e, 2 * NF * (g - 1))
                if part == 0:
                    nc.scalar.copy(xa_h[g % 2][:, :], bank[6][:, 0:G]).then_inc(xah_ready, 1)
                else:
                    nc.scalar.copy(xb[g % 2][0:DB, :], bank[6][0:DB, 0:G]).then_inc(xbh_ready, 1)

            def gate(e, g, f):
                wait(act, gu_done, 2 * NF * NG, e, 2 * (NF * g + f) + 1)
                wait(act, hf_ready, NF * NG, e, NF * g + f - 1)
                nc.scalar.activation(silu[f % 2][:, :], bank[2 * (f % 2)][:, 0:G], ACT.Silu).then_inc(silu_ready, 1)

            def h_high(e, g, f):
                wait(act, hf_ready, NF * NG, e, NF * g + f + 1)
                wait(act, down_done, NG * GT, e, GT * (g - 1))
                nc.scalar.copy(h_h[g % 2][:, f, :], hf[f % 2][:, :]).then_inc(hh_ready, 1)

            def y_low(e, g):
                for j in range(GT):
                    wait(act, down_done, NG * GT, e, GT * g + j + 1)
                    wait(act, score_ready, NG, e, g + 1)
                    wait(act, yo_ready, NG * GT, e, GT * g + j - 1)
                    nc.scalar.mul(yb[j % 2][:, :], bank[4 + j % 2][0:P, D:2 * D], score[g % 2][:, j:j + 1]).then_inc(yb_ready, 1)

            def split_high(e, n):
                if n == 0:
                    wait(act, weights_in, 16 * NLOAD, e, 16 * NLOAD)
                    wait(act, down_done, NG * GT, e, less=1)
                if n < 4:
                    high, raw = ((ga_h, raw_ga), (ua_h, raw_ua), (gb_h, raw_gb), (ub_h, raw_ub))[n]
                    last = nc.scalar.copy(high[e.par][:, :], raw[:, :])
                else:
                    last = nc.scalar.copy(wd[e.par][:, :, 0:D], raw_d[:, :, :])
                last.then_inc(high_ready, 1)

            for n in range(NHIGH):
                split_high(FIRST, n)
            x_high(FIRST, 0, 0)
            x_high(FIRST, 0, 1)

            def step(e, g):
                ne, ng = following(e, g)
                gate(e, g, 0)
                gate(e, g, 1)
                h_high(e, g, 0)
                h_high(e, g, 1)
                pe_, pg = preceding(e, g)
                if pe_:
                    y_low(pe_, pg)
                for f in range(2, NF):
                    gate(e, g, f)
                    h_high(e, g, f)
                    if f in (2, 4) and ne:
                        x_high(ne, ng, f // 2 - 1)
                    if later(e, 1) and f > 2 and 3 * g + f - 3 < NHIGH:
                        split_high(later(e, 1), 3 * g + f - 3)

            over_experts(act, step)
            y_low(LAST, NG - 1)

        @block.vector
        def _(dve):
            def list_rhs_of(e):
                wait(dve, list_done, NCH, e)
                nc.vector.tensor_tensor(is_q[:, :, :], resident["slot_q"][:, bass.ds(e.n, 1), :].to_broadcast([P, EXPERTS, TILES]),
                                        iota_q[:, :, :], ALU.is_equal).then_inc(isq_ready, 1)
                wait(dve, isq_ready, 1, e, 1)
                nc.vector.tensor_scalar(list_rhs[:, 0:EXPERTS, :], is_q[:, :, :], iota_f[:, P:P + 1], None, ALU.mult)
                nc.vector.tensor_tensor(list_rhs[:, EXPERTS:2 * EXPERTS, :], is_q[:, :, :],
                                        tile_no[:, :].unsqueeze(1).to_broadcast([P, EXPERTS, TILES]), ALU.mult).then_inc(rhs_ready, 1)

            def list_lhs(e, c):
                wait(dve, list_done, NCH, e, c - 1)
                nc.vector.tensor_tensor(
                    is_p[c % 2][:, :, :],
                    resident["slot_p"][:, bass.ds(e.n, 1), c * OHT:(c + 1) * OHT].to_broadcast([P, P, OHT]),
                    iota_p[:, :, :], ALU.is_equal).then_inc(isp_ready, 1)

            def list_end(e):
                wait(dve, list_done, NCH, e, NCH)
                nc.vector.tensor_copy(place[:, :], bank[7][0:P, 0:EXPERTS]).then_inc(place_ready, 1)
                wait(dve, place_ready, 1, e, 1)
                for i in range(2):
                    wait(dve, added[i], 16 * GT * NG // 2, e, less=1)
                nc.vector.scalar_tensor_tensor(out=index[e.par][:, :], in0=bank[7][0:P, EXPERTS:2 * EXPERTS], scalar=float(P),
                                               in1=place[:, :], op0=ALU.mult, op1=ALU.add).then_inc(index_ready, 1)

            def scores(e, g):
                wait(dve, gathered[g % 2], 16 * GT * NG // 2, e, 16 * GT * (g // 2 + 1))
                apart(dve)
                nc.vector.tensor_copy(score[g % 2][:, :], xg[g % 2][:, :, bass.ds(e.n + D, 1)].rearrange("p j a -> p (j a)")).then_inc(score_ready, 1)

            def x_low(e, g, part):
                if part == 0:
                    wait(dve, xah_ready, NG, e, g + 1)
                    nc.vector.tensor_tensor(xa_l[g % 2][:, :], bank[6][:, 0:G], xa_h[g % 2][:, :].bitcast(F32), ALU.subtract).then_inc(xal_ready, 1)
                else:
                    wait(dve, xbh_ready, NG, e, g + 1)
                    nc.vector.tensor_tensor(xb[g % 2][DB:128, :], bank[6][0:DB, 0:G], xb[g % 2][0:DB, :].bitcast(F32), ALU.subtract).then_inc(xbl_ready, 1)

            def product(e, g, f):
                wait(dve, silu_ready, NF * NG, e, NF * g + f + 1)
                wait(dve, gu_done, 2 * NF * NG, e, 2 * (NF * g + f) + 2)
                wait(dve, hl_ready, NF * NG, e, NF * g + f - 1)
                nc.vector.tensor_tensor(hf[f % 2][:, :], silu[f % 2][:, :], bank[2 * (f % 2) + 1][:, 0:G], ALU.mult).then_inc(hf_ready, 1)

            def h_low(e, g, f):
                wait(dve, hh_ready, NF * NG, e, NF * g + f + 1)
                nc.vector.tensor_tensor(h_l[g % 2][:, f, :], hf[f % 2][:, :], h_h[g % 2][:, f, :].bitcast(F32), ALU.subtract).then_inc(hl_ready, 1)

            def y_sum(e, g):
                wait(dve, added[g % 2], 16 * GT * NG // 2, e, 16 * GT * (g // 2))
                for j in range(GT):
                    wait(dve, yb_ready, NG * GT, e, GT * g + j + 1)
                    nc.vector.scalar_tensor_tensor(out=yo[g % 2][:, j, :], in0=bank[4 + j % 2][0:P, 0:D], scalar=score[g % 2][:, j:j + 1],
                                                   in1=yb[j % 2][:, :], op0=ALU.mult, op1=ALU.add).then_inc(yo_ready, 1)

            dve.wait_ge(iota_in, 16)
            nc.vector.tensor_copy(iota_p[:, :, :], iota_f[:, 0:P].unsqueeze(2).to_broadcast([P, P, OHT]))
            nc.vector.tensor_copy(iota_q[:, :, :], iota_f[:, P + 1:P + 1 + EXPERTS].unsqueeze(2).to_broadcast([P, EXPERTS, TILES]))
            nc.vector.tensor_copy(tile_no[:, :], iota_f[:, P + 1 + EXPERTS:]).then_inc(iota_set, 1)
            dve.wait_ge(iota_set, 1)
            list_rhs_of(FIRST)
            for c in range(NCH):
                list_lhs(FIRST, c)
            list_end(FIRST)
            scores(FIRST, 0)
            x_low(FIRST, 0, 0)
            x_low(FIRST, 0, 1)
            list_rhs_of(later(FIRST, 1))

            def step(e, g):
                ne, ng = following(e, g)
                after = later(e, 1)
                product(e, g, 0)
                product(e, g, 1)
                h_low(e, g, 0)
                h_low(e, g, 1)
                pe_, pg = preceding(e, g)
                if pe_:
                    y_sum(pe_, pg)
                for f in range(2, NF):
                    product(e, g, f)
                    if after and (g, f) in AT:
                        list_lhs(after, AT[g, f])
                    h_low(e, g, f)
                    if f == 2 and ne:
                        scores(ne, ng)
                    if f in (2, 4) and ne:
                        x_low(ne, ng, f // 2 - 1)
                if g == NG - 2 and after:
                    list_end(after)
                if g == NG - 1 and later(e, 2):
                    list_rhs_of(later(e, 2))

            over_experts(dve, step)
            y_sum(LAST, NG - 1)


def audio_tower(nc, io):
    with ExitStack() as ctx:
        resident = {
            "ident": ctx.enter_context(nc.sbuf_tensor("ident", [128, 128], F32)),
            "slot_p": ctx.enter_context(nc.sbuf_tensor("slot_p", [P, EXPERTS, TILES], BF16)),
            "slot_q": ctx.enter_context(nc.sbuf_tensor("slot_q", [P, EXPERTS, TILES], BF16)),
        }
        with nc.sbuf_tensor("scores_tm", [P, TILES, EXPERTS], F32) as scores_tm:
            tower_phase(nc, io, resident | {"scores_tm": scores_tm})
            shared_phase(nc, io, resident | {"scores_tm": scores_tm})
        experts_phase(nc, io, resident)


_IO = ["framesT", "dft", "mel", "dct", "w_proj", "b_proj", "wqkv", "wout", "b_out", "gateT", "wsgT", "wsuT", "wsdT",
       "wgT", "wuT", "wdT", "ident", "same_head", "head_of", "same_expert", "before", "iotas"]


def _constants():
    import numpy as np

    n = np.arange(FRAME)
    window = 0.54 - 0.46 * np.cos(2.0 * np.pi * n / (FRAME - 1))
    angle = 2.0 * np.pi * np.outer(n, np.arange(BINS // 2)) / FRAME
    dft = np.concatenate([np.cos(angle), -np.sin(angle)], axis=1) * window[:, None]
    d, r = np.arange(D), np.arange(128)
    iotas = np.concatenate([np.tile(np.arange(1, P + 1), (P, 1)), np.arange(P)[:, None],
                            np.tile(np.arange(EXPERTS), (P, 1)), np.tile(np.arange(TILES), (P, 1))], axis=1)
    f = np.float32
    same = r[:, None] % EXPERTS == r[None, :] % EXPERTS
    return {
        "dft": dft.astype(f),
        "ident": np.eye(128, dtype=f),
        "same_head": (d[:, None] // DH == d[None, :] // DH).astype(f),
        "head_of": (d[:, None] // DH == np.arange(HEADS)[None, :]).astype(f),
        "same_expert": same.astype(f),
        "before": (same & (r[:, None] < r[None, :])).astype(f),
        "iotas": iotas.astype(f),
    }


def _layout(a):
    import numpy as np

    step = (a["x"].shape[1] - FRAME) // (FRAMES - 1)
    at = np.arange(FRAMES)[:, None] * step + np.arange(FRAME)[None, :]
    return {
        "framesT": a["x"][:, at].reshape(TOKENS, FRAME).T,
        "mel": np.concatenate([a["L0_tok_mel_filters"].T] * 2, axis=0),
        "dct": a["L0_tok_dct"],
        "w_proj": a["L0_tok_w_proj"],
        "b_proj": a["L0_tok_b_proj"][None, :],
        "wqkv": a["L0_attn_W_qkv"],
        "wout": a["L0_attn_W_out"],
        "b_out": a["L0_attn_b_out"][None, :],
        "gateT": a["L0_ffn_gate_weight"].T,
        "wsgT": a["L0_ffn_Ws_g"].T,
        "wsuT": a["L0_ffn_Ws_u"].T,
        "wsdT": a["L0_ffn_Ws_d"].T,
        "wgT": a["L0_ffn_Wg"].transpose(0, 2, 1).reshape(EXPERTS * D, FE),
        "wuT": a["L0_ffn_Wu"].transpose(0, 2, 1).reshape(EXPERTS * D, FE),
        "wdT": a["L0_ffn_Wd"].transpose(0, 2, 1).reshape(EXPERTS * FE, D),
    }


def kernel(**inputs):
    import concourse.bacc as bacc
    import numpy as np
    from concourse.bass_utils import run_bass_kernel_spmd

    laid = _layout({name: np.asarray(a) for name, a in inputs.items()}) | _constants()
    nc = bacc.Bacc("TRN2", target_bir_lowering=False, num_devices=1)
    arrays, io = {}, {}
    for name in _IO:
        a = np.ascontiguousarray(laid[name])
        arrays[f"in_{name}"] = a
        io[name] = nc.dram_tensor(f"in_{name}", a.shape, mybir.dt.from_np(a.dtype), kind="ExternalInput").ap()
    io["x2T"] = nc.dram_tensor("x2T", (D, TOKENS), F32, kind="Internal").ap()
    io["rows"] = nc.dram_tensor("rows", (TOKENS, ROW), F32, kind="Internal").ap()
    io["out"] = nc.dram_tensor("out", (TOKENS, D), F32, kind="ExternalOutput").ap()
    audio_tower(nc, io)
    result = run_bass_kernel_spmd(nc, [arrays], core_ids=[0])
    return result.results[0]["out"].reshape(BATCH, FRAMES, D)
```

```python
from collections import namedtuple
from contextlib import ExitStack

import concourse.bass as bass
from concourse import mybir

F32 = mybir.dt.float32
F32R = mybir.dt.float32r
BF16 = mybir.dt.bfloat16
I32 = mybir.dt.int32
U32 = mybir.dt.uint32
ALU = mybir.AluOpType
ACT = mybir.ActivationFunctionType

BATCH, FRAMES, FRAME = 64, 250, 100
BINS = 2 * (FRAME // 2 + 1)
MEL = 40
D = 192
DA, DB = 128, 64
HEADS, DH = 12, 16
HA, HB = DA // DH, DB // DH
EXPERTS = 16
FE, FS = 768, 384
TOKENS = BATCH * FRAMES
CAP = 2000
P = 125
TILES = TOKENS // P
GT = 4
G = GT * P
GROUPS = TOKENS // G
ROW = D + EXPERTS
CHUNKS = 128 // EXPERTS
CT = TILES // CHUNKS
CLEN = CT * P
EPS_LOG, EPS_LN, EPS_ATT = 1e-6, 1e-5, 1e-6
OHT = 16
ROUND = float(3 << 22)

Group = namedtuple("Group", "n half par known")


def wait(eng, sem, per, g, off=0, less=0):
    if g.known and per * (g.n - less) + off <= 0:
        return
    eng.wait_ge(sem, (g.n - less) * per + off)


def apart(eng):
    eng.nop(nofuse=True)


def wait_alone(eng, *which, **how):
    wait(eng, *which, **how)
    apart(eng)


def skewed(eng, step):
    STAGES, FIRST = 6, 6

    def groups(n, half, par, known):
        out = []
        for s in range(STAGES):
            gpar = (par - s) % 2
            gh = half + (par - s - gpar) // 2
            out.append(Group(n - s, gh, gpar, known) if not known or 0 <= n - s < GROUPS else None)
        return out

    for it in range(FIRST):
        step(groups(it, it // 2, it % 2, True))
    with eng.Fori(0, (GROUPS - FIRST) // 2) as i:
        for par in range(2):
            step(groups(i * 2 + (FIRST + par), i + FIRST // 2, par, False))
    for it in range(GROUPS, GROUPS + STAGES - 1):
        step(groups(it, it // 2, it % 2, True))


def tower_phase(nc, io, resident):
    scores_tm, ident = resident["scores_tm"], resident["ident"]
    raw_ga, raw_gb, raw_ua, raw_ub, raw_d = resident["shared_raw"]
    ga_h, ga_l, gb_h, gb_l, ua_h, ua_l, ub_h, ub_l, wd = resident["shared_parts"]
    iota_f, iota_p, iota_q, tile_no = (resident[n] for n in ("iota_f", "iota_p", "iota_q", "tile_no"))
    with ExitStack() as ctx:
        def sb(name, shape, dt=F32):
            return ctx.enter_context(nc.sbuf_tensor(name, shape, dt))

        def sem(name):
            return ctx.enter_context(nc.semaphore(name))

        bank = [ctx.enter_context(nc.psum_tensor(f"bank{i}", [128, 512], F32)) for i in range(8)]

        dft = sb("dft", [FRAME, BINS])
        mel = sb("mel", [BINS, MEL])
        dctT = sb("dctT", [13, MEL])
        wproj = sb("wproj", [13, D])
        cproj = sb("cproj", [MEL + 1, D])
        wqkv_a, wqkv_b = sb("wqkv_a", [DA, 3 * D]), sb("wqkv_b", [128, 3 * D])
        wqkv_ah, wqkv_al, wqkv_bh, wqkv_bl = (sb(n, [128, 3 * D], F32R) for n in ("wqkv_ah", "wqkv_al", "wqkv_bh", "wqkv_bl"))
        wout_a, wout_b = sb("wout_a", [DA, D]), sb("wout_b", [128, D])
        wout_ah, wout_al, wout_bh, wout_bl = (sb(n, [128, D], F32R) for n in ("wout_ah", "wout_al", "wout_bh", "wout_bl"))
        b_out = sb("b_out", [P, D])
        gate_a, gate_b = sb("gate_a", [DA, EXPERTS]), sb("gate_b", [DB, EXPERTS])
        same_a, same_b = sb("same_a", [DA, DA]), sb("same_b", [DB, DB])
        head_a, head_b = sb("head_a", [DA, HA]), sb("head_b", [DB, HB])
        eps_log, eps_ln = sb("eps_log", [MEL, 1]), sb("eps_ln", [P, 1])

        frames = [sb(f"frames{i}", [FRAME, G]) for i in range(2)]
        power = sb("power", [BINS, G])
        logmel = sb("logmel", [MEL + 1, G])
        h = [sb(f"h{i}", [P, GT, D]) for i in range(2)]
        hb = [sb(f"hb{i}", [P, GT, D]) for i in range(2)]
        stats, stats2 = sb("stats", [P, GT, 6]), sb("stats2", [P, GT, 6])
        mv, mv2 = sb("mv", [P, GT, 2]), sb("mv2", [P, GT, 2])
        lnv, rstd = sb("lnv", [P, GT]), sb("rstd", [P, GT])
        lnv2, rstd2 = sb("lnv2", [P, GT]), sb("rstd2", [P, GT])
        xn = sb("xn", [P, GT, D])
        xa_h, xa_l, xb = (sb(n, [128, G], F32R) for n in ("xa_h", "xa_l", "xb"))
        expq_a, expq_b = sb("expq_a", [DA, G]), sb("expq_b", [DB, G])
        expk = sb("expk", [P, GT, D])
        q_a = [sb(f"q_a{i}", [DA, G]) for i in range(2)]
        q_b = [sb(f"q_b{i}", [DB, G]) for i in range(2)]
        k = [sb(f"k{i}", [P, GT, D]) for i in range(2)]
        v = [sb(f"v{i}", [P, GT, D + 2]) for i in range(2)]
        kv_a, kv_b = sb("kv_a", [DA, 2, HA + DA]), sb("kv_b", [DB, 2, DB + HB])
        ks_a, ks_b = sb("ks_a", [DA, 2]), sb("ks_b", [DB, 2])
        den, z = sb("den", [P, GT, HEADS]), sb("z", [P, GT, HEADS])
        o = sb("o", [P, GT, D])
        oa_h, oa_l, ob = (sb(n, [128, G], F32R) for n in ("oa_h", "oa_l", "ob"))
        h1 = [sb(f"h1_{i}", [P, GT, D]) for i in range(2)]
        row = [sb(f"row{i}", [P, GT, ROW]) for i in range(2)]
        x2T_a = [sb(f"x2T_a{i}", [DA, G]) for i in range(2)]
        x2T_b = [sb(f"x2T_b{i}", [DB, G]) for i in range(2)]
        logitsT = sb("logitsT", [EXPERTS, G])
        exps, sig = sb("exps", [P, GT, EXPERTS]), sb("sig", [P, GT, EXPERTS])

        consts_in, consts_set, cproj_mm, cproj_set = sem("consts_in"), sem("consts_set"), sem("cproj_mm"), sem("cproj_set")
        high_set, low_set = sem("high_set"), sem("low_set")
        frames_in = [sem(f"frames_in{i}") for i in range(2)]
        dft_done, power_ready, mel_done, logmel_ready, proj_done = (sem(n) for n in (
            "dft_done", "power_ready", "mel_done", "logmel_ready", "proj_done"))
        h_ready, hb_ready, stats_ready, mv_ready, lnv_ready, rstd_ready, xn_ready = (sem(n) for n in (
            "h_ready", "hb_ready", "stats_ready", "mv_ready", "lnv_ready", "rstd_ready", "xn_ready"))
        xT_done, xh_ready, xl_ready = sem("xT_done"), sem("xh_ready"), sem("xl_ready")
        q_done, kv_done, expq_ready, expk_ready = sem("q_done"), sem("kv_done"), sem("expq_ready"), sem("expk_ready")
        minq_ready, mink_ready, q_ready, k_ready, v_ready = (sem(n) for n in (
            "minq_ready", "mink_ready", "q_ready", "k_ready", "v_ready"))
        ktv_done, ks_ready, kvm_ready = sem("ktv_done"), sem("ks_ready"), sem("kvm_ready")
        att_done, den_ready, z_ready, o_ready = sem("att_done"), sem("den_ready"), sem("z_ready"), sem("o_ready")
        oT_done, oh_ready, ol_ready, wo_done = sem("oT_done"), sem("oh_ready"), sem("ol_ready"), sem("wo_done")
        h1_ready, stats2_ready, mv2_ready, lnv2_ready, rstd2_ready, x2_ready = (sem(n) for n in (
            "h1_ready", "stats2_ready", "mv2_ready", "lnv2_ready", "rstd2_ready", "x2_ready"))
        x2T_done, x2Ta_ready, x2Tb_ready = sem("x2T_done"), sem("x2Ta_ready"), sem("x2Tb_ready")
        router_done, logitsT_ready, logits_done, exps_ready, sig1_ready, sig_ready, scores_ready = (sem(n) for n in (
            "router_done", "logitsT_ready", "logits_done", "exps_ready", "sig1_ready", "sig_ready", "scores_ready"))
        next_in, next_high = sem("next_in"), sem("next_high")
        h1_out, xT_out, rows_out = ([sem(f"{n}{i}") for i in range(2)] for n in ("h1_out", "xT_out", "rows_out"))

        whole = [dft, mel, dctT, wproj, b_out, gate_a, gate_b, same_a, same_b, head_a, head_b, ident]
        loads = list(zip(whole, [
            io["dft"], io["mel"], io["dct"], io["w_proj"], io["b_out"].to_broadcast([P, D]),
            io["gateT"][0:DA, :], io["gateT"][DA:D, :], io["same_head"][0:DA, 0:DA], io["same_head"][DA:D, DA:D],
            io["head_of"][0:DA, 0:HA], io["head_of"][DA:D, HA:HEADS], io["ident"]]))
        loads = [(t[:, :], src) for t, src in loads] + [
            (cproj[MEL:MEL + 1, :], io["b_proj"]),
            (wqkv_a[:, :], io["wqkv"][0:DA, :]), (wqkv_b[0:DB, :], io["wqkv"][DA:D, :]), (wqkv_b[DB:128, :], io["wqkv"][DA:D, :]),
            (wout_a[:, :], io["wout"][0:DA, :]), (wout_b[0:DB, :], io["wout"][DA:D, :]), (wout_b[DB:128, :], io["wout"][DA:D, :]),
        ]
        splits = [(wqkv_a, wqkv_ah, wqkv_al), (wqkv_b, wqkv_bh, wqkv_bl), (wout_a, wout_ah, wout_al), (wout_b, wout_bh, wout_bl)]
        KEY_BANK = (2, 3, 4, 3)
        block = ctx.enter_context(nc.Block())

        @block.sync
        def _(sp):
            for dst, src in loads:
                sp.dma_start(dst, src).then_inc(consts_in, 16)

            def by_tile(dram, g):
                return dram[bass.ds(g.n * G, G), :].rearrange("(j p) c -> p j c", p=P)

            def step(gs):
                g0, _, _, g3, g4, g5 = gs
                if g0:
                    wait_alone(sp, dft_done, 1, g0, less=1)
                    sp.dma_start(frames[g0.par][:, :], io["framesT"][:, bass.ds(g0.n * G, G)]).then_inc(frames_in[g0.par], 16)
                if g0 and g0.known and g0.n == 4:
                    for a, b, src in ((raw_ga, raw_gb, io["wsgT"]), (raw_ua, raw_ub, io["wsuT"])):
                        sp.dma_start(a[:, :], src[0:DA, :]).then_inc(next_in, 16)
                        sp.dma_start(b[0:DB, :], src[DA:D, :]).then_inc(next_in, 16)
                        sp.dma_start(b[DB:128, :], src[DA:D, :]).then_inc(next_in, 16)
                    sp.dma_start(raw_d[:, :, :], io["wsdT"].rearrange("(c p) n -> p c n", p=128)).then_inc(next_in, 16)
                    sp.dma_start(iota_f[:, :], io["iotas"]).then_inc(next_in, 16)
                if g4:
                    wait_alone(sp, x2Ta_ready, 1, g4, 1)
                    wait_alone(sp, x2Tb_ready, 1, g4, 1)
                    sp.dma_start(io["x2T"][0:DA, bass.ds(g4.n * G, G)], x2T_a[g4.par][:, :]).then_inc(xT_out[g4.par], 16)
                    sp.dma_start(io["x2T"][DA:D, bass.ds(g4.n * G, G)], x2T_b[g4.par][:, :]).then_inc(xT_out[g4.par], 16)
                if g3:
                    wait_alone(sp, h1_ready, 1, g3, 1)
                    sp.dma_start(by_tile(io["out"], g3), h1[g3.par][:, :, :]).then_inc(h1_out[g3.par], 16)
                if g5:
                    wait_alone(sp, scores_ready, 1, g5, 1)
                    sp.dma_start(by_tile(io["rows"], g5), row[g5.par][:, :, :]).then_inc(rows_out[g5.par], 16)

            skewed(sp, step)
            for i in range(2):
                sp.wait_ge(rows_out[i], 16 * (GROUPS // 2))
                sp.wait_ge(h1_out[i], 16 * (GROUPS // 2))
                sp.wait_ge(xT_out[i], 32 * (GROUPS // 2))

        @block.gpsimd
        def _(pool):
            pool.wait_ge(consts_in, 16 * len(loads))

            def step(gs):
                _, g1, _, _, g4, _ = gs
                if g4:
                    wait(pool, rstd2_ready, 1, g4, 1)
                    if not g4.known or g4.n >= 2:
                        pool.wait_ge(rows_out[g4.par], g4.half * 16)
                    apart(pool)
                    for j in range(GT):
                        last = nc.gpsimd.tensor_scalar(row[g4.par][:, j, 0:D], h1[g4.par][:, j, :], mv2[:, j, 0:1],
                                                       rstd2[:, j:j + 1], ALU.subtract, ALU.mult)
                    last.then_inc(x2_ready, 1)
                if g1:
                    wait(pool, h_ready, 1, g1, 1)
                    wait(pool, h1_ready, 1, g1, less=1)
                    nc.gpsimd.tensor_tensor(hb[g1.par][:, :, :], h[g1.par][:, :, :],
                                            b_out[:, :].unsqueeze(1).to_broadcast([P, GT, D]), ALU.add).then_inc(hb_ready, 1)

            skewed(pool, step)

        @block.tensor
        def _(pe):
            pe.wait_ge(consts_in, 16 * len(loads))
            nc.tensor.matmul(bank[0][0:MEL, 0:D], dctT[:, :], wproj[:, :], start=True, stop=True).then_inc(cproj_mm, 1)
            pe.wait_ge(cproj_set, 1)
            pe.wait_ge(low_set, 1)

            def transpose_piece(src, to, c, m):
                for j in range(GT):
                    last = nc.tensor.transpose(to[0:m, j * P:(j + 1) * P], src[:, j, c:c + m], ident[0:P, 0:P])
                return last

            def transpose(src, to_a, to_b, done):
                transpose_piece(src, to_a, 0, DA)
                transpose_piece(src, to_b, DA, DB).then_inc(done, 1)

            def split_product(to, pairs):
                for n, (w, x) in enumerate(pairs):
                    last = nc.tensor.matmul(to, w, x, start=(n == 0), stop=(n == len(pairs) - 1))
                return last

            def spectrum(g):
                pe.wait_ge(frames_in[g.par], (g.half + 1) * 16)
                wait(pe, h_ready, 1, g)
                nc.tensor.matmul(bank[0][0:BINS, 0:G], dft[:, :], frames[g.par][:, :], start=True, stop=True).then_inc(dft_done, 1)

            def filterbank(g):
                wait(pe, power_ready, 1, g, 1)
                nc.tensor.matmul(bank[1][0:MEL, 0:G], mel[:, :], power[:, :], start=True, stop=True).then_inc(mel_done, 1)

            def project(g):
                wait(pe, logmel_ready, 1, g, 1)
                for j in range(GT):
                    last = nc.tensor.matmul(bank[j // 2][0:P, (j % 2) * D:(j % 2 + 1) * D],
                                            logmel[:, j * P:(j + 1) * P], cproj[:, :], start=True, stop=True)
                last.then_inc(proj_done, 1)

            def queries(g):
                wait(pe, xh_ready, 2, g, 2)
                wait(pe, xl_ready, 2, g, 2)
                for to, c0, m in ((bank[2], 0, DA), (bank[3], DA, DB)):
                    c = slice(c0, c0 + m)
                    for n, (w, x) in enumerate(((wqkv_ah[:, c], xa_h[:, :]), (wqkv_al[:, c], xa_h[:, :]), (wqkv_ah[:, c], xa_l[:, :]),
                                                (wqkv_bh[:, c], xb[:, :]), (wqkv_bl[:, c], xb[:, :]))):
                        last = nc.tensor.matmul(to[0:m, 0:G], w, x, start=(n == 0), stop=(n == 4))
                    last.then_inc(q_done, 1)

            def keys(g, j):
                if j < 2:
                    wait(pe, q_ready, 2, g, j + 1)
                if j == 2:
                    wait(pe, x2Tb_ready, 1, g, 1, less=2)
                if j == 3:
                    wait(pe, k_ready, 4, g, 2)
                t = slice(j * P, (j + 1) * P)
                split_product(bank[KEY_BANK[j]][0:P, 0:2 * D], (
                    (xa_h[:, t], wqkv_ah[:, D:3 * D]), (xa_h[:, t], wqkv_al[:, D:3 * D]), (xa_l[:, t], wqkv_ah[:, D:3 * D]),
                    (xb[:, t], wqkv_bh[:, D:3 * D]), (xb[:, t], wqkv_bl[:, D:3 * D]))).then_inc(kv_done, 1)

            def keys_values(g):
                wait(pe, k_ready, 4, g, 4)
                wait(pe, v_ready, 4, g, 4)
                wait(pe, h1_ready, 1, g)
                for b in range(2):
                    for c, to, m in ((0, bank[5], DA), (DA, bank[6], DB)):
                        c1 = c + (c > 0)
                        for j in (2 * b, 2 * b + 1):
                            last = nc.tensor.matmul(to[0:m, b * (m + 1):(b + 1) * (m + 1)], k[g.par][:, j, c:c + m],
                                                    v[g.par][:, j, c1:c1 + m + 1], start=(j % 2 == 0), stop=(j % 2 == 1))
                last.then_inc(ktv_done, 1)

            def attend(g):
                wait(pe, kvm_ready, 1, g, 1)
                wait(pe, q_ready, 2, g, 2)
                for j in range(GT):
                    c0 = (j % 2) * (D + HEADS)
                    c1 = c0 + HA + DA
                    t = slice(j * P, (j + 1) * P)
                    nc.tensor.matmul(bank[5 + j // 2][0:P, c0:c1], q_a[g.par][:, t], kv_a[:, j // 2, :], start=True, stop=True)
                    last = nc.tensor.matmul(bank[5 + j // 2][0:P, c1:c1 + DB + HB], q_b[g.par][:, t], kv_b[:, j // 2, :],
                                            start=True, stop=True)
                last.then_inc(att_done, 1)

            def out_proj(g):
                wait(pe, oh_ready, 2, g, 2)
                wait(pe, ol_ready, 2, g, 2)
                for j in range(GT):
                    t = slice(j * P, (j + 1) * P)
                    last = split_product(bank[5 + j // 2][0:P, (j % 2) * D:(j % 2 + 1) * D], (
                        (oa_h[:, t], wout_ah[:, :]), (oa_h[:, t], wout_al[:, :]), (oa_l[:, t], wout_ah[:, :]),
                        (ob[:, t], wout_bh[:, :]), (ob[:, t], wout_bl[:, :])))
                last.then_inc(wo_done, 1)

            def router(g):
                wait(pe, x2Ta_ready, 1, g, 1)
                nc.tensor.matmul(bank[7][0:EXPERTS, 0:G], gate_a[:, :], x2T_a[g.par][:, :], start=True, stop=False)
                wait(pe, x2Tb_ready, 1, g, 1)
                apart(pe)
                nc.tensor.matmul(bank[7][0:EXPERTS, 0:G], gate_b[:, :], x2T_b[g.par][:, :], start=False, stop=True).then_inc(router_done, 1)

            def logits(g):
                wait(pe, logitsT_ready, 1, g, 1)
                apart(pe)
                for j in range(GT):
                    last = nc.tensor.transpose(bank[7][0:P, j * EXPERTS:(j + 1) * EXPERTS], logitsT[:, j * P:(j + 1) * P],
                                               ident[0:EXPERTS, 0:EXPERTS])
                last.then_inc(logits_done, 1)

            def step(gs):
                _, g1, g2, g3, g4, _ = gs
                if g2:
                    wait(pe, xn_ready, 1, g2, 1)
                    wait(pe, k_ready, 4, g2, -1)
                    transpose_piece(xn, bank[2], 0, DA).then_inc(xT_done, 1)
                if g1:
                    spectrum(g1)
                if g2:
                    wait(pe, k_ready, 4, g2)
                    apart(pe)
                    transpose_piece(xn, bank[3], DA, DB).then_inc(xT_done, 1)
                if g3:
                    keys_values(g3)
                if g1:
                    filterbank(g1)
                if g2:
                    queries(g2)
                if g3:
                    attend(g3)
                if g1:
                    project(g1)
                if g4:
                    wait(pe, x2_ready, 1, g4, 1)
                    wait(pe, exps_ready, 1, g4)
                    transpose(row[g4.par], bank[7], bank[4], x2T_done)
                if g3:
                    wait(pe, o_ready, 1, g3, 1)
                    transpose(o, bank[5], bank[6], oT_done)
                if g2:
                    keys(g2, 0)
                    keys(g2, 1)
                if g4:
                    router(g4)
                if g2:
                    keys(g2, 2)
                if g3:
                    out_proj(g3)
                if g2:
                    keys(g2, 3)
                if g4:
                    logits(g4)

            skewed(pe, step)

        @block.scalar
        def _(act):
            act.wait_ge(consts_in, 16 * len(loads))
            for src, high, _ in splits:
                last = nc.scalar.copy(high[:, :], src[:, :])
            last.then_inc(high_set, 1)
            act.wait_ge(consts_set, 5)

            def inv_std(g, mvx, lnx, rx, mv_sem, ln_sem, r_sem, used):
                wait(act, mv_sem, 1, g, 1)
                nc.scalar.activation(lnx[:, :], mvx[:, :, 1], ACT.Ln, bias=eps_ln[:, :]).then_inc(ln_sem, 1)
                wait(act, ln_sem, 1, g, 1)
                wait(act, used, 1, g)
                nc.scalar.activation(rx[:, :], lnx[:, :], ACT.Exp, scale=-0.5).then_inc(r_sem, 1)

            def key_and_value(g, j):
                wait(act, kv_done, 4, g, j + 1)
                wait(act, k_ready, 4, g)
                nc.scalar.activation(expk[:, j, :], bank[KEY_BANK[j]][0:P, 0:D], ACT.Exp).then_inc(expk_ready, 1)
                wait(act, ktv_done, 1, g, less=1)
                nc.scalar.copy(v[g.par][:, j, 1:D + 1], bank[KEY_BANK[j]][0:P, D:2 * D]).then_inc(v_ready, 1)

            def step(gs):
                _, g1, g2, g3, g4, _ = gs
                if g2:
                    wait(act, xT_done, 2, g2, 1)
                    wait(act, kv_done, 4, g2)
                    nc.scalar.copy(xa_h[:, :], bank[2][:, 0:G]).then_inc(xh_ready, 1)
                if g1:
                    wait(act, dft_done, 1, g1, 1)
                    wait(act, mel_done, 1, g1)
                    nc.scalar.activation(power[:, :], bank[0][0:BINS, 0:G], ACT.Square).then_inc(power_ready, 1)
                if g2:
                    wait(act, xT_done, 2, g2, 2)
                    nc.scalar.copy(xb[0:DB, :], bank[3][0:DB, 0:G]).then_inc(xh_ready, 1)
                if g4:
                    inv_std(g4, mv2, lnv2, rstd2, mv2_ready, lnv2_ready, rstd2_ready, x2_ready)
                if g1:
                    wait(act, mel_done, 1, g1, 1)
                    wait(act, proj_done, 1, g1)
                    nc.scalar.activation(logmel[0:MEL, :], bank[1][0:MEL, 0:G], ACT.Ln, bias=eps_log[:, :]).then_inc(logmel_ready, 1)
                if g2:
                    for n, (e, b, m) in enumerate(((expq_a, bank[2], DA), (expq_b, bank[3], DB))):
                        wait(act, q_done, 2, g2, n + 1)
                        wait(act, q_ready, 2, g2)
                        nc.scalar.activation(e[:, :], b[0:m, 0:G], ACT.Exp).then_inc(expq_ready, 1)
                if g1:
                    wait(act, proj_done, 1, g1, 1)
                    wait(act, hb_ready, 1, g1, less=1)
                    wait(act, xn_ready, 1, g1, less=1)
                    for b in range(2):
                        last = nc.scalar.copy(h[g1.par][:, 2 * b:2 * b + 2, :],
                                              bank[b][0:P, 0:2 * D].rearrange("p (j c) -> p j c", c=D))
                    last.then_inc(h_ready, 1)
                if g4:
                    wait(act, x2T_done, 1, g4, 1)
                    wait(act, router_done, 1, g4, less=1)
                    if not g4.known or g4.n >= 2:
                        act.wait_ge(xT_out[g4.par], g4.half * 32)
                    nc.scalar.copy(x2T_a[g4.par][:, :], bank[7][:, 0:G]).then_inc(x2Ta_ready, 1)
                    nc.scalar.copy(x2T_b[g4.par][:, :], bank[4][0:DB, 0:G]).then_inc(x2Tb_ready, 1)
                if g3:
                    wait(act, oT_done, 1, g3, 1)
                    wait(act, wo_done, 1, g3)
                    nc.scalar.copy(oa_h[:, :], bank[5][:, 0:G]).then_inc(oh_ready, 1)
                    nc.scalar.copy(ob[0:DB, :], bank[6][0:DB, 0:G]).then_inc(oh_ready, 1)
                if g2:
                    key_and_value(g2, 0)
                    key_and_value(g2, 1)
                if g1:
                    inv_std(g1, mv, lnv, rstd, mv_ready, lnv_ready, rstd_ready, xn_ready)
                if g4:
                    wait(act, router_done, 1, g4, 1)
                    wait(act, logits_done, 1, g4)
                    nc.scalar.copy(logitsT[:, :], bank[7][0:EXPERTS, 0:G]).then_inc(logitsT_ready, 1)
                if g2:
                    key_and_value(g2, 2)
                    key_and_value(g2, 3)
                if g4:
                    wait(act, logits_done, 1, g4, 1)
                    wait(act, sig1_ready, 1, g4)
                    nc.scalar.activation(exps[:, :, :], bank[7][0:P, 0:GT * EXPERTS].rearrange("p (j e) -> p j e", e=EXPERTS),
                                         ACT.Exp, scale=-1.0).then_inc(exps_ready, 1)
                if g3 and g3.known and g3.n == GROUPS - 1:
                    act.wait_ge(next_in, 8 * 16)
                    for high, src in ((ga_h, raw_ga), (gb_h, raw_gb), (ua_h, raw_ua), (ub_h, raw_ub)):
                        nc.scalar.copy(high[:, :], src[:, :])
                    nc.scalar.copy(wd[:, :, 0:D], raw_d[:, :, :]).then_inc(next_high, 1)

            nc.scalar.preload_act_table_set("natural_log_exp_and_others")
            skewed(act, step)

        @block.vector
        def _(dve):
            nc.vector.memset(eps_log[:, :], EPS_LOG).then_inc(consts_set, 1)
            nc.vector.memset(eps_ln[:, :], EPS_LN).then_inc(consts_set, 1)
            nc.vector.memset(logmel[:, :], 1.0).then_inc(consts_set, 1)
            for i in range(2):
                nc.vector.memset(v[i][:, :, :], 1.0).then_inc(consts_set, 1)
            dve.wait_ge(cproj_mm, 1)
            nc.vector.tensor_copy(cproj[0:MEL, :], bank[0][0:MEL, 0:D]).then_inc(cproj_set, 1)
            dve.wait_ge(high_set, 1)
            for src, high, low in splits:
                last = nc.vector.tensor_tensor(low[:, :], src[:, :], high[:, :].bitcast(F32), ALU.subtract)
            last.then_inc(low_set, 1)

            def moments(g, src, st, mvx, st_sem, mv_sem):
                for j in range(GT):
                    last = nc.vector.bn_stats(st[:, j, :], src(j))
                last.then_inc(st_sem, 1)
                wait(dve, st_sem, 1, g, 1)
                apart(dve)
                for j in range(GT):
                    last = nc.vector.bn_aggr(mvx[:, j, :], st[:, j, :])
                last.then_inc(mv_sem, 1)

            def relu_plus(g, to, src, e, exp_sem, per, off, min_sem, done):
                wait(dve, exp_sem, per, g, off)
                nc.vector.tensor_scalar(e, e, 1.0, None, ALU.min).then_inc(min_sem, 1)
                wait(dve, min_sem, per, g, off)
                nc.vector.scalar_tensor_tensor(out=to, in0=src, scalar=0.0, in1=e, op0=ALU.max, op1=ALU.add).then_inc(done, 1)

            def key(g, j):
                wait(dve, v_ready, 4, g, j + 1)
                relu_plus(g, k[g.par][:, j, :], bank[KEY_BANK[j]][0:P, 0:D], expk[:, j, :], expk_ready, 4, j + 1, mink_ready, k_ready)

            def step(gs):
                _, g1, g2, g3, g4, g5 = gs
                if g2:
                    for n, (to, b, m, hi) in enumerate(((xa_l[:, :], bank[2], DA, xa_h), (xb[DB:128, :], bank[3], DB, xb))):
                        wait(dve, xh_ready, 2, g2, n + 1)
                        nc.vector.tensor_tensor(to, b[0:m, 0:G], hi[0:m, :].bitcast(F32), ALU.subtract).then_inc(xl_ready, 1)
                if g3:
                    wait(dve, ktv_done, 1, g3, 1)
                    for kvx, ksx, b, m, same, kv0, ks0, at in ((kv_a, ks_a, bank[5], DA, same_a, 1, 0, HA), (kv_b, ks_b, bank[6], DB, same_b, 0, DB, 0)):
                        both = b[0:m, 0:2 * (m + 1)].rearrange("p (b c) -> p b c", b=2)
                        nc.vector.tensor_tensor(kvx[:, :, at:at + m], both[:, :, kv0:kv0 + m],
                                                same[:, :].unsqueeze(1).to_broadcast([m, 2, m]), ALU.mult)
                        last = nc.vector.tensor_scalar(ksx[:, :], both[:, :, ks0], 1.0, None, ALU.add)
                    last.then_inc(ks_ready, 1)
                    wait(dve, ks_ready, 1, g3, 1)
                    for kvx, ksx, head, at, n in ((kv_a, ks_a, head_a, 0, HA), (kv_b, ks_b, head_b, DB, HB)):
                        for b in range(2):
                            last = nc.vector.tensor_scalar(kvx[:, b, at:at + n], head[:, :], ksx[:, b:b + 1], None, ALU.mult)
                    last.then_inc(kvm_ready, 1)
                if g2:
                    for n, (to, b, e, m) in enumerate(((q_a, bank[2], expq_a, DA), (q_b, bank[3], expq_b, DB))):
                        relu_plus(g2, to[g2.par][:, :], b[0:m, 0:G], e[:, :], expq_ready, 2, n + 1, minq_ready, q_ready)
                if g3:
                    wait(dve, att_done, 1, g3, 1)
                    for b in range(2):
                        both = bank[5 + b][0:P, 0:2 * (D + HEADS)].rearrange("p (j c) -> p j c", j=2)
                        nc.vector.tensor_scalar(den[:, 2 * b:2 * b + 2, 0:HA], both[:, :, 0:HA], EPS_ATT, None, ALU.add)
                        last = nc.vector.tensor_scalar(den[:, 2 * b:2 * b + 2, HA:HEADS], both[:, :, HA + D:HEADS + D], EPS_ATT, None, ALU.add)
                    last.then_inc(den_ready, 1)
                    wait(dve, den_ready, 1, g3, 1)
                    nc.vector.reciprocal(z[:, :, :], den[:, :, :]).then_inc(z_ready, 1)
                    wait(dve, z_ready, 1, g3, 1)
                    for j in range(GT):
                        c0 = (j % 2) * (D + HEADS) + HA
                        last = nc.vector.tensor_tensor(
                            o[:, j, :].rearrange("p (h d) -> p h d", d=DH),
                            bank[5 + j // 2][0:P, c0:c0 + D].rearrange("p (h d) -> p h d", d=DH),
                            z[:, j, :].unsqueeze(2).to_broadcast([P, HEADS, DH]), ALU.mult)
                    last.then_inc(o_ready, 1)
                if g5:
                    wait(dve, exps_ready, 1, g5, 1)
                    nc.vector.tensor_scalar(sig[:, :, :], exps[:, :, :], 1.0, None, ALU.add).then_inc(sig1_ready, 1)
                    wait(dve, sig1_ready, 1, g5, 1)
                    nc.vector.reciprocal(row[g5.par][:, :, D:ROW], sig[:, :, :]).then_inc(sig_ready, 1)
                    wait(dve, sig_ready, 1, g5, 1)
                    apart(dve)
                    nc.vector.tensor_copy(scores_tm[:, bass.ds(g5.n * GT, GT), :], row[g5.par][:, :, D:ROW]).then_inc(scores_ready, 1)
                if g1:
                    wait(dve, h_ready, 1, g1, 1)
                    moments(g1, lambda j: h[g1.par][:, j, :], stats, mv, stats_ready, mv_ready)
                if g3:
                    for n, (to, b, m, hi) in enumerate(((oa_l[:, :], bank[5], DA, oa_h), (ob[DB:128, :], bank[6], DB, ob))):
                        wait(dve, oh_ready, 2, g3, n + 1)
                        nc.vector.tensor_tensor(to, b[0:m, 0:G], hi[0:m, :].bitcast(F32), ALU.subtract).then_inc(ol_ready, 1)
                if g2:
                    key(g2, 0)
                    key(g2, 1)
                if g1:
                    wait(dve, rstd_ready, 1, g1, 1)
                    for j in range(GT):
                        last = nc.vector.tensor_scalar(xn[:, j, :], h[g1.par][:, j, :], mv[:, j, 0:1], rstd[:, j:j + 1],
                                                       ALU.subtract, ALU.mult)
                    last.then_inc(xn_ready, 1)
                if g2:
                    key(g2, 2)
                if g3:
                    wait(dve, wo_done, 1, g3, 1)
                    wait(dve, hb_ready, 1, g3, 1)
                    wait(dve, x2_ready, 1, g3, less=1)
                    if not g3.known or g3.n >= 2:
                        dve.wait_ge(h1_out[g3.par], g3.half * 16)
                    for b in range(2):
                        last = nc.vector.tensor_tensor(h1[g3.par][:, 2 * b:2 * b + 2, :], hb[g3.par][:, 2 * b:2 * b + 2, :],
                                                       bank[5 + b][0:P, 0:2 * D].rearrange("p (j c) -> p j c", c=D), ALU.add)
                    last.then_inc(h1_ready, 1)
                if g2:
                    key(g2, 3)
                if g3:
                    wait(dve, h1_ready, 1, g3, 1)
                    wait(dve, x2_ready, 1, g3)
                    moments(g3, lambda j: h1[g3.par][:, j, :], stats2, mv2, stats2_ready, mv2_ready)
                if g3 and g3.known and g3.n == GROUPS - 1:
                    dve.wait_ge(next_high, 1)
                    for low, src, high in ((ga_l, raw_ga, ga_h), (gb_l, raw_gb, gb_h), (ua_l, raw_ua, ua_h), (ub_l, raw_ub, ub_h)):
                        nc.vector.tensor_tensor(low[:, :], src[:, :], high[:, :].bitcast(F32), ALU.subtract)
                    nc.vector.tensor_tensor(wd[:, :, D:2 * D], raw_d[:, :, :], wd[:, :, 0:D].bitcast(F32), ALU.subtract)
                    nc.vector.tensor_copy(iota_p[:, :, :], iota_f[:, 0:P].unsqueeze(2).to_broadcast([P, P, OHT]))
                    nc.vector.tensor_copy(iota_q[:, :, :], iota_f[:, P + 1:P + 1 + EXPERTS].unsqueeze(2).to_broadcast([P, EXPERTS, TILES]))
                    nc.vector.tensor_copy(tile_no[:, :], iota_f[:, P + 1 + EXPERTS:])

            skewed(dve, step)


def shared_phase(nc, io, resident):
    scores_tm, ident = resident["scores_tm"], resident["ident"]
    NF = FS // 128
    BITS = 30
    PAIR = 3
    SEARCH, TIES = 2, 2 + 2 * BITS // PAIR
    DOWN_BANK = (4, 5, 6, 4)
    with ExitStack() as ctx:
        def sb(name, shape, dt=F32):
            return ctx.enter_context(nc.sbuf_tensor(name, shape, dt))

        def sem(name):
            return ctx.enter_context(nc.semaphore(name))

        bank = [ctx.enter_context(nc.psum_tensor(f"sh_bank{i}", [128, 512], F32)) for i in range(8)]
        ga_h, ga_l, gb_h, gb_l, ua_h, ua_l, ub_h, ub_l, wd = resident["shared_parts"]
        x_a = [sb(f"sh_x_a{i}", [DA, G]) for i in range(2)]
        x_b = [sb(f"sh_x_b{i}", [DB, G]) for i in range(2)]
        xa_h, xa_l, xb = ([sb(f"sh_{n}{i}", [128, G], F32R) for i in range(2)] for n in ("xa_h", "xa_l", "xb"))
        silu = [sb(f"sh_silu{i}", [128, G]) for i in range(2)]
        hf = [sb(f"sh_hf{i}", [128, G]) for i in range(2)]
        h_h, h_l = ([sb(f"sh_{n}{i}", [128, NF, G], F32R) for i in range(2)] for n in ("h_h", "h_l"))
        h1 = [sb(f"sh_h1_{i}", [P, GT, D]) for i in range(2)]
        half_y = [sb(f"half_y{i}", [P, D]) for i in range(2)]
        y = [sb(f"sh_y{i}", [P, GT, D]) for i in range(2)]

        same, before = sb("same", [128, 128]), sb("before", [128, 128])
        by_piece = sb("by_piece", [P, CT * 128])
        s = sb("s", [128, CLEN])
        mark = sb("mark", [128, CLEN], BF16)
        above, equal, ties, chosen, slot, slot_q, slot_p = (sb(n, [128, CLEN]) for n in (
            "above", "equal", "ties", "chosen", "slot", "quot", "rest"))
        zero, bit_f, count = sb("zero", [128, 1]), sb("bit_f", [128, 1]), sb("count", [128, 1])
        bit, thr, cand, keep = (sb(n, [128, 1], I32) for n in ("bit", "thr", "cand", "keep"))
        room, offset = sb("room", [128, 1]), sb("offset", [128, 1])

        x_in, h1_in, y_out = ([sem(f"sh_{n}{i}") for i in range(2)] for n in ("x_in", "h1_in", "y_out"))
        xh_ready, xal_ready, xbl_ready = sem("sh_xh_ready"), sem("sh_xal_ready"), sem("sh_xbl_ready")
        gu_done, silu_ready, hf_ready, hh_ready, hl_ready = (sem(f"sh_{n}") for n in (
            "gu_done", "silu_ready", "hf_ready", "hh_ready", "hl_ready"))
        down_done, half_ready, y_ready = sem("sh_down_done"), sem("sh_half_ready"), sem("sh_y_ready")

        mats_in, by_piece_ready, s_done, s_ready, init_set = (sem(n) for n in ("mats_in", "by_piece_ready", "s_done", "s_ready", "init_set"))
        cand_ready, count_ready, total_done, keep_ready, thr_ready, bit_ready = (sem(n) for n in (
            "cand_ready", "count_ready", "total_done", "keep_ready", "thr_ready", "bit_ready"))
        ties_ready, offsets_done, chosen_ready, slots_ready = (sem(n) for n in (
            "ties_ready", "offsets_done", "chosen_ready", "slots_ready"))
        link, maps_done, maps_read = sem("link"), sem("maps_done"), sem("maps_read")
        block = ctx.enter_context(nc.Block())

        def over_groups(eng, step):
            def known(n):
                step(Group(n, n // 2, n % 2, True), SEARCH <= n < TIES)

            for n in range(SEARCH + 2):
                known(n)
            with eng.Fori(0, (TIES - SEARCH) // 2 - 1) as i:
                for par in range(2):
                    step(Group(i * 2 + (SEARCH + 2 + par), i + (SEARCH // 2 + 1), par, False), True)
            for n in range(TIES, GROUPS):
                known(n)

        def later(g, by):
            par = (g.par + by) % 2
            if g.known and not 0 <= g.n + by < GROUPS:
                return None
            return Group(g.n + by, g.half + (g.par + by - par) // 2, par, g.known)

        FIRST = Group(0, 0, 0, True)
        LAST = Group(GROUPS - 1, (GROUPS - 1) // 2, (GROUPS - 1) % 2, True)

        def bit_no(g, n):
            return g.half * PAIR + (n - PAIR * (SEARCH // 2))

        def at(g, n):
            return g.known and g.n == n

        @block.sync
        def _(sp):
            def by_tile(g):
                return io["out"][bass.ds(g.n * G, G), :].rearrange("(j p) c -> p j c", p=P)

            def load_x(g):
                wait_alone(sp, xh_ready, 2, g, less=1)
                wait_alone(sp, xal_ready, 1, g, less=1)
                wait_alone(sp, xbl_ready, 1, g, less=1)
                sp.dma_start(x_a[g.par][:, :], io["x2T"][0:DA, bass.ds(g.n * G, G)]).then_inc(x_in[g.par], 16)
                sp.dma_start(x_b[g.par][:, :], io["x2T"][DA:D, bass.ds(g.n * G, G)]).then_inc(x_in[g.par], 16)

            def load_h1(g):
                wait_alone(sp, y_ready, GT, g, less=1)
                sp.dma_start(h1[g.par][:, :, :], by_tile(g)).then_inc(h1_in[g.par], 16)

            def store(g):
                wait_alone(sp, y_ready, GT, g, GT)
                sp.dma_start(by_tile(g), y[g.par][:, :, :]).then_inc(y_out[g.par], 16)

            load_x(FIRST)
            load_h1(FIRST)
            sp.dma_start(same[:, :], io["same_expert"]).then_inc(mats_in, 16)
            sp.dma_start(before[:, :], io["before"]).then_inc(mats_in, 16)

            def step(g, search):
                if later(g, 1):
                    load_x(later(g, 1))
                if later(g, -1):
                    store(later(g, -1))
                if later(g, 1):
                    load_h1(later(g, 1))

            over_groups(sp, step)
            store(LAST)
            for i in range(2):
                sp.wait_ge(y_out[i], 16 * (GROUPS // 2))

        @block.gpsimd
        def _(pool):
            def x_low(g):
                wait(pool, xh_ready, 2, g, 1)
                wait(pool, gu_done, 2 * NF, g, less=1)
                nc.gpsimd.tensor_tensor(xa_l[g.par][:, :], x_a[g.par][:, :], xa_h[g.par][:, :].bitcast(F32), ALU.subtract).then_inc(xal_ready, 1)

            def h_low(g, f):
                wait(pool, hh_ready, NF, g, f + 1)
                nc.gpsimd.tensor_tensor(h_l[g.par][:, f, :], hf[(g.par + f) % 2][:, :], h_h[g.par][:, f, :].bitcast(F32),
                                        ALU.subtract).then_inc(hl_ready, 1)

            x_low(FIRST)

            def step(g, search):
                h_low(g, 0)
                if later(g, 1):
                    x_low(later(g, 1))
                h_low(g, 1)
                h_low(g, 2)

            over_groups(pool, step)

        @block.tensor
        def _(pe):
            def up(g, f, between=None):
                if f == 0:
                    wait(pe, xal_ready, 1, g, 1)
                    wait(pe, xbl_ready, 1, g, 1)
                s, cols = g.par, slice(f * 128, (f + 1) * 128)
                for w, (a_h, a_l, b_h, b_l) in enumerate(((ga_h, ga_l, gb_h, gb_l), (ua_h, ua_l, ub_h, ub_l))):
                    wait(pe, (silu_ready, hf_ready)[w], NF, g, f - 1)
                    to = bank[2 * ((g.par + f) % 2) + w][:, 0:G]
                    nc.tensor.matmul(to, a_h[:, cols], xa_h[s][:, :], start=True, stop=False)
                    nc.tensor.matmul(to, a_l[:, cols], xa_h[s][:, :], start=False, stop=False)
                    nc.tensor.matmul(to, a_h[:, cols], xa_l[s][:, :], start=False, stop=False)
                    nc.tensor.matmul(to, b_h[:, cols], xb[s][:, :], start=False, stop=False)
                    nc.tensor.matmul(to, b_l[:, cols], xb[s][:, :], start=False, stop=True).then_inc(gu_done, 1)
                    if w == 0 and between is not None:
                        total(between)

            def down(g):
                wait(pe, hl_ready, NF, g, NF)
                for j in range(GT):
                    if j == 0:
                        wait(pe, y_ready, GT, g)
                    if j == 3:
                        wait(pe, y_ready, GT, g, 1)
                    if j == 2:
                        for n in range(2):
                            if at(g, n):
                                pe.wait_ge(s_ready, n + 1)
                        for n in range(4):
                            if at(g, TIES + 4 + n):
                                pe.wait_ge(maps_read, 2 * (n + 1))
                    cols, to = slice(j * P, (j + 1) * P), bank[DOWN_BANK[j]]
                    for f in range(NF):
                        nc.tensor.matmul(to[0:P, 0:2 * D], h_h[g.par][:, f, cols], wd[:, f, :], start=(f == 0), stop=False)
                        last = nc.tensor.matmul(to[0:P, 0:D], h_l[g.par][:, f, cols], wd[:, f, 0:D], start=False, stop=(f == NF - 1))
                    last.then_inc(down_done, 1)

            def total(it):
                pe.wait_ge(count_ready, it + 1)
                nc.tensor.matmul(bank[7][:, 0:1], same[:, :], count[:, :], start=True, stop=True).then_inc(total_done, 1)

            def scores_rows(first):
                if first:
                    pe.wait_ge(y_ready, GT)
                for b in range(first, first + 8):
                    nc.tensor.transpose(bank[6 + b % 8 // 4][:, (b % 4) * P:(b % 4 + 1) * P],
                                        by_piece[:, b * 128:(b + 1) * 128], ident[0:P, 0:P]).then_inc(s_done, 1)

            def map_back(n, src, first):
                pe.wait_ge(y_ready, (TIES + 4 + n) * GT)
                if n:
                    pe.wait_ge(maps_read, 2 * n)
                for b in range(first, first + 8):
                    last = nc.tensor.transpose(bank[6 + b % 8 // 4][0:P, (b % 4) * 128:(b % 4 + 1) * 128],
                                               src[:, b * P:(b + 1) * P], ident[:, :])
                    if b % 4 == 3:
                        last.then_inc(maps_done, 1)

            pe.wait_ge(mats_in, 32)

            def step(g, search):
                up(g, 0, bit_no(g, 1) if search and g.par else None)
                if at(g, TIES + 3):
                    pe.wait_ge(chosen_ready, 1)
                    nc.tensor.matmul(bank[7][:, 3:4], before[:, :], slot[:, CLEN - 1:CLEN], start=True, stop=True).then_inc(offsets_done, 1)
                up(g, 1)
                if later(g, -1):
                    down(later(g, -1))
                if search:
                    total(bit_no(g, 2 * g.par))
                if at(g, 0):
                    pe.wait_ge(by_piece_ready, 1)
                    scores_rows(0)
                if at(g, 1):
                    pe.wait_ge(s_ready, 1)
                    scores_rows(8)
                if at(g, TIES + 1):
                    pe.wait_ge(ties_ready, 1)
                    nc.tensor.matmul(bank[7][:, 1:2], same[:, :], count[:, :], start=True, stop=True)
                    nc.tensor.matmul(bank[7][:, 2:3], before[:, :], ties[:, CLEN - 1:CLEN], start=True, stop=True).then_inc(offsets_done, 1)
                for n, (src, first) in enumerate(((slot_q, 0), (slot_q, 8), (slot_p, 0), (slot_p, 8))):
                    if at(g, TIES + 4 + n):
                        if n == 0:
                            pe.wait_ge(slots_ready, 1)
                        map_back(n, src, first)
                up(g, 2)

            over_groups(pe, step)
            down(LAST)

        @block.scalar
        def _(act):
            def x_high(g):
                act.wait_ge(x_in[g.par], (g.half + 1) * 32)
                wait(act, gu_done, 2 * NF, g, less=1)
                nc.scalar.copy(xa_h[g.par][:, :], x_a[g.par][:, :]).then_inc(xh_ready, 1)
                nc.scalar.copy(xb[g.par][0:DB, :], x_b[g.par][:, :]).then_inc(xh_ready, 1)

            def gate(g, f):
                m = (g.par + f) % 2
                wait(act, gu_done, 2 * NF, g, 2 * f + 1)
                wait(act, hf_ready, NF, g, f - 1)
                nc.scalar.activation(silu[m][:, :], bank[2 * m][:, 0:G], ACT.Silu).then_inc(silu_ready, 1)

            def h_high(g, f):
                wait(act, hf_ready, NF, g, f + 1)
                wait(act, down_done, GT, g, less=1)
                nc.scalar.copy(h_h[g.par][:, f, :], hf[(g.par + f) % 2][:, :]).then_inc(hh_ready, 1)

            x_high(FIRST)

            def step(g, search):
                gate(g, 0)
                h_high(g, 0)
                gate(g, 1)
                if later(g, 1):
                    x_high(later(g, 1))
                h_high(g, 1)
                gate(g, 2)
                h_high(g, 2)

            over_groups(act, step)

        @block.vector
        def _(dve):
            links = [0]

            def then(instruction):
                links[0] += 1
                instruction.then_inc(link, 1)
                dve.wait_ge(link, links[0])

            def x_low(g):
                wait(dve, xh_ready, 2, g, 2)
                wait(dve, gu_done, 2 * NF, g, less=1)
                nc.vector.tensor_tensor(xb[g.par][DB:128, :], x_b[g.par][:, :], xb[g.par][0:DB, :].bitcast(F32), ALU.subtract).then_inc(xbl_ready, 1)

            def product(g, f):
                m = (g.par + f) % 2
                wait(dve, silu_ready, NF, g, f + 1)
                wait(dve, gu_done, 2 * NF, g, 2 * f + 2)
                wait(dve, hl_ready, NF, g, f - 1)
                nc.vector.tensor_tensor(hf[m][:, :], silu[m][:, :], bank[2 * m + 1][:, 0:G], ALU.mult).then_inc(hf_ready, 1)

            def y_sum(g):
                dve.wait_ge(h1_in[g.par], (g.half + 1) * 16)
                if not g.known or g.n >= 2:
                    dve.wait_ge(y_out[g.par], g.half * 16)
                for j in range(GT):
                    wait(dve, down_done, GT, g, j + 1)
                    wait(dve, y_ready, GT, g, j - 1)
                    nc.vector.tensor_tensor(half_y[j % 2][:, :], bank[DOWN_BANK[j]][0:P, 0:D], h1[g.par][:, j, :], ALU.add).then_inc(half_ready, 1)
                    wait(dve, half_ready, GT, g, j + 1)
                    nc.vector.tensor_tensor(y[g.par][:, j, :], half_y[j % 2][:, :], bank[DOWN_BANK[j]][0:P, D:2 * D], ALU.add).then_inc(y_ready, 1)

            def try_bit(it):
                dve.wait_ge(bit_ready, it + 1)
                nc.vector.tensor_tensor(cand[:, :], thr[:, :], bit[:, :], ALU.bitwise_or).then_inc(cand_ready, 1)
                dve.wait_ge(cand_ready, it + 1)
                nc.vector.tensor_scalar(mark[:, :], s[:, :], cand[:, :].bitcast(F32), None, ALU.is_ge, ALU.add,
                                        accum_out=count[:, :]).then_inc(count_ready, 1)

            def settle_bit(it):
                dve.wait_ge(total_done, it + 1)
                nc.vector.tensor_scalar(keep[:, :], bank[7][:, 0:1], float(CAP), bit_f[:, :], ALU.is_ge, ALU.mult).then_inc(keep_ready, 1)
                dve.wait_ge(keep_ready, it + 1)
                nc.vector.tensor_scalar(bit_f[:, :], bit_f[:, :], 0.5, None, ALU.mult)
                nc.vector.tensor_tensor(thr[:, :], thr[:, :], keep[:, :], ALU.bitwise_or).then_inc(thr_ready, 1)
                dve.wait_ge(thr_ready, it + 1)
                nc.vector.tensor_copy(bit[:, :], bit_f[:, :]).then_inc(bit_ready, 1)

            def rows_read(first):
                for b in range(first, first + 8, 4):
                    dve.wait_ge(s_done, b + 4)
                    last = nc.vector.tensor_copy(s[:, b * P:(b + 4) * P], bank[6 + b % 8 // 4][:, 0:4 * P])
                last.then_inc(s_ready, 1)

            def map_read(n, to, first):
                view = to[:, :, :].rearrange("p e (c b) -> p b c e", b=CT)
                for i in range(2):
                    dve.wait_ge(maps_done, 2 * n + i + 1)
                    b = first + 4 * i
                    nc.vector.tensor_copy(view[:, b:b + 4], bank[6 + i][0:P, :].rearrange(
                        "p (b c e) -> p b c e", b=4, c=CHUNKS)).then_inc(maps_read, 1)

            nc.vector.tensor_copy(by_piece[:, :].rearrange("p (b c e) -> p c b e", b=CT, c=CHUNKS),
                                  scores_tm[:, :, :].rearrange("p (c b) e -> p c b e", b=CT)).then_inc(by_piece_ready, 1)
            nc.vector.memset(zero[:, :], 0.0)
            nc.vector.memset(bit_f[:, :], float(2 ** (BITS - 1)))
            nc.vector.memset(thr[:, :], 0).then_inc(init_set, 1)
            dve.wait_ge(init_set, 1)
            nc.vector.tensor_copy(bit[:, :], bit_f[:, :]).then_inc(bit_ready, 1)
            x_low(FIRST)

            def step(g, search):
                product(g, 0)
                if search:
                    if g.par:
                        settle_bit(bit_no(g, 1))
                    try_bit(bit_no(g, 2 * g.par))
                best = thr[:, :].bitcast(F32)
                if at(g, TIES):
                    dve.wait_ge(thr_ready, BITS)
                    then(nc.vector.tensor_scalar(above[:, :], s[:, :], best, None, ALU.is_gt, ALU.add, accum_out=count[:, :]))
                if at(g, TIES + 1):
                    nc.vector.tensor_tensor_scan(ties[:, :], equal[:, :], zero[:, :].to_broadcast([128, CLEN]), 0.0,
                                                 ALU.add, ALU.add).then_inc(ties_ready, 1)
                if at(g, TIES + 2):
                    then(nc.vector.tensor_tensor(chosen[:, :], chosen[:, :], above[:, :], ALU.add))
                if at(g, TIES + 3):
                    dve.wait_ge(offsets_done, 2)
                    then(nc.vector.tensor_copy(offset[:, :], bank[7][:, 3:4]))
                    then(nc.vector.scalar_tensor_tensor(out=slot[:, :], in0=slot[:, :], scalar=offset[:, :], in1=chosen[:, :],
                                                        op0=ALU.add, op1=ALU.mult))
                if at(g, TIES + 4):
                    nc.vector.scalar_tensor_tensor(out=slot_p[:, :], in0=slot_q[:, :], scalar=float(-P), in1=slot[:, :],
                                                   op0=ALU.mult, op1=ALU.add).then_inc(slots_ready, 1)
                product(g, 1)
                if later(g, -1):
                    y_sum(later(g, -1))
                if later(g, 1):
                    x_low(later(g, 1))
                if search:
                    settle_bit(bit_no(g, 2 * g.par))
                    if not g.par:
                        try_bit(bit_no(g, 1))
                if at(g, 0):
                    rows_read(0)
                if at(g, 1):
                    rows_read(8)
                    dve.wait_ge(s_ready, 2)
                if at(g, TIES):
                    then(nc.vector.tensor_scalar(equal[:, :], s[:, :], best, None, ALU.is_equal))
                if at(g, TIES + 1):
                    dve.wait_ge(offsets_done, 1)
                    then(nc.vector.tensor_scalar(room[:, :], bank[7][:, 1:2], -1.0, float(CAP), ALU.mult, ALU.add))
                    then(nc.vector.tensor_tensor(room[:, :], room[:, :], bank[7][:, 2:3], ALU.subtract))
                    then(nc.vector.scalar_tensor_tensor(out=chosen[:, :], in0=ties[:, :], scalar=room[:, :], in1=equal[:, :],
                                                        op0=ALU.is_le, op1=ALU.mult))
                if at(g, TIES + 2):
                    nc.vector.tensor_tensor_scan(slot[:, :], chosen[:, :], zero[:, :].to_broadcast([128, CLEN]), 0.0,
                                                 ALU.add, ALU.add).then_inc(chosen_ready, 1)
                if at(g, TIES + 3):
                    then(nc.vector.tensor_scalar(slot_q[:, :], slot[:, :], 1.0 / P, -(P // 2 + 1) / P, ALU.mult, ALU.add))
                    then(nc.vector.tensor_scalar(slot_q[:, :], slot_q[:, :], ROUND, ROUND, ALU.add, ALU.subtract))
                for n, (to, first) in enumerate(((resident["slot_q"], 0), (resident["slot_q"], 8),
                                                 (resident["slot_p"], 0), (resident["slot_p"], 8))):
                    if at(g, TIES + 4 + n):
                        map_read(n, to, first)
                product(g, 2)

            over_groups(dve, step)
            y_sum(LAST)


def experts_phase(nc, io, resident):
    ident = resident["ident"]
    NF = FE // 128
    NG = CAP // G
    NCH = TILES // OHT
    AT = {(g, f): c for c, (g, f) in enumerate([(g, f) for g in range(NG - 1) for f in (2, 3, 4)][:NCH])}
    NLOAD, NHIGH = 7, 5
    with ExitStack() as ctx:
        def sb(name, shape, dt=F32):
            return ctx.enter_context(nc.sbuf_tensor(name, shape, dt))

        def sem(name):
            return ctx.enter_context(nc.semaphore(name))

        bank = [ctx.enter_context(nc.psum_tensor(f"ex_bank{i}", [128, 512], F32)) for i in range(8)]
        raw_ga, raw_gb, raw_ua, raw_ub = (sb(n, [128, FE]) for n in ("raw_ga", "raw_gb", "raw_ua", "raw_ub"))
        raw_d = sb("raw_d", [128, NF, D])
        ga_h, ga_l, gb_h, gb_l, ua_h, ua_l, ub_h, ub_l = ([sb(f"{n}{i}", [128, FE], F32R) for i in range(2)] for n in (
            "ga_h", "ga_l", "gb_h", "gb_l", "ua_h", "ua_l", "ub_h", "ub_l"))
        wd = [sb(f"wd{i}", [128, NF, 2 * D], F32R) for i in range(2)]
        xg = [sb(f"xg{i}", [P, GT, ROW]) for i in range(2)]
        score = [sb(f"score{i}", [P, GT]) for i in range(2)]
        xa_h, xa_l, xb = ([sb(f"{n}{i}", [128, G], F32R) for i in range(2)] for n in ("xa_h", "xa_l", "xb"))
        silu = [sb(f"ex_silu{i}", [128, G]) for i in range(2)]
        hf = [sb(f"hf{i}", [128, G]) for i in range(2)]
        h_h, h_l = ([sb(f"{n}{i}", [128, NF, G], F32R) for i in range(2)] for n in ("h_h", "h_l"))
        yb = [sb(f"yb{i}", [P, D]) for i in range(2)]
        yo = [sb(f"yo{i}", [P, GT, D]) for i in range(2)]
        iota_f, iota_p, iota_q, tile_no = (resident[n] for n in ("iota_f", "iota_p", "iota_q", "tile_no"))
        is_q = sb("is_q", [P, EXPERTS, TILES], BF16)
        list_rhs = sb("list_rhs", [P, 2 * EXPERTS, TILES], BF16)
        is_p = [sb(f"is_p{i}", [P, P, OHT], BF16) for i in range(2)]
        place = sb("place", [P, EXPERTS])
        index = [sb(f"index{i}", [P, EXPERTS], U32) for i in range(2)]

        weights_in, high_ready, split_ready = sem("weights_in"), sem("high_ready"), sem("split_ready")
        isq_ready, rhs_ready, isp_ready, list_done, place_ready, index_ready = (sem(n) for n in (
            "isq_ready", "rhs_ready", "isp_ready", "list_done", "place_ready", "index_ready"))
        gathered = [sem(f"gathered{i}") for i in range(2)]
        added = [sem(f"added{i}") for i in range(2)]
        score_ready, tr_done = sem("score_ready"), sem("tr_done")
        xah_ready, xal_ready, xbh_ready, xbl_ready = (sem(n) for n in ("xah_ready", "xal_ready", "xbh_ready", "xbl_ready"))
        gu_done, silu_ready, hf_ready, hh_ready, hl_ready = (sem(n) for n in (
            "ex_gu_done", "ex_silu_ready", "hf_ready", "hh_ready", "hl_ready"))
        down_done, yb_ready, yo_ready = sem("ex_down_done"), sem("yb_ready"), sem("yo_ready")
        block = ctx.enter_context(nc.Block())

        def over_experts(eng, step):
            def known(n):
                for g in range(NG):
                    step(Group(n, n // 2, n % 2, True), g)

            known(0)
            known(1)
            with eng.Fori(0, EXPERTS // 2 - 2) as i:
                for par in range(2):
                    for g in range(NG):
                        step(Group(i * 2 + (2 + par), i + 1, par, False), g)
            known(EXPERTS - 2)
            known(EXPERTS - 1)

        def later(e, by):
            par = (e.par + by) % 2
            if e.known and e.n + by >= EXPERTS:
                return None
            return Group(e.n + by, e.half + (e.par + by - par) // 2, par, e.known)

        def following(e, g):
            return (e, g + 1) if g + 1 < NG else (later(e, 1), 0)

        def preceding(e, g):
            if g:
                return e, g - 1
            return (None if e.known and e.n == 0 else later(e, -1)), NG - 1

        FIRST = Group(0, 0, 0, True)
        LAST = Group(EXPERTS - 1, (EXPERTS - 1) // 2, (EXPERTS - 1) % 2, True)

        @block.sync
        def _(sp):
            def load(e):
                wait_alone(sp, split_ready, 1, e)
                gate, up = io["wgT"][bass.ds(e.n * D, D), :], io["wuT"][bass.ds(e.n * D, D), :]
                for src, a, b in ((gate, raw_ga, raw_gb), (up, raw_ua, raw_ub)):
                    sp.dma_start(a[:, :], src[0:DA, :]).then_inc(weights_in, 16)
                    sp.dma_start(b[0:DB, :], src[DA:D, :]).then_inc(weights_in, 16)
                    sp.dma_start(b[DB:128, :], src[DA:D, :]).then_inc(weights_in, 16)
                sp.dma_start(raw_d[:, :, :], io["wdT"][bass.ds(e.n * FE, FE), :].rearrange("(c p) n -> p c n", p=128)).then_inc(weights_in, 16)

            load(FIRST)

            def step(e, g):
                if g == 0 and later(e, 1):
                    load(later(e, 1))

            over_experts(sp, step)

        @block.gpsimd
        def _(pool):
            def split_low(e, part):
                p = e.par
                wait(pool, high_ready, NHIGH, e, (2, NHIGH)[part])
                if part == 0:
                    for dst, src, hi in ((ga_l, raw_ga, ga_h), (ua_l, raw_ua, ua_h)):
                        nc.gpsimd.tensor_tensor(dst[p][:, :], src[:, :], hi[p][:, :].bitcast(F32), ALU.subtract)
                else:
                    for dst, src, hi in ((gb_l, raw_gb, gb_h), (ub_l, raw_ub, ub_h)):
                        nc.gpsimd.tensor_tensor(dst[p][:, :], src[:, :], hi[p][:, :].bitcast(F32), ALU.subtract)
                    nc.gpsimd.tensor_tensor(wd[p][:, :, D:2 * D], raw_d[:, :, :], wd[p][:, :, 0:D].bitcast(F32),
                                            ALU.subtract).then_inc(split_ready, 1)

            def gather(e, g):
                wait(pool, index_ready, 1, e, 1)
                wait(pool, tr_done, 2 * NG, e, 2 * (g - 1))
                wait(pool, score_ready, NG, e, g - 1)
                apart(pool)
                for j in range(GT):
                    n = g * GT + j
                    nc.gpsimd.indirect_dma_start(
                        out=xg[g % 2][:, j, :], out_offset=None, in_=io["rows"],
                        in_offset=bass.IndirectOffsetOnAxis(ap=index[e.par][:, n:n + 1], axis=0)).then_inc(gathered[g % 2], 16)

            def scatter(e, g):
                if g == 0:
                    for i in range(2):
                        wait(pool, added[i], 16 * GT * NG // 2, e)
                for j in range(GT):
                    n = g * GT + j
                    wait(pool, yo_ready, NG * GT, e, n + 1)
                    apart(pool)
                    nc.gpsimd.indirect_dma_start(
                        out=io["out"], out_offset=bass.IndirectOffsetOnAxis(ap=index[e.par][:, n:n + 1], axis=0),
                        in_=yo[g % 2][:, j, :], in_offset=None, compute_op=ALU.add).then_inc(added[g % 2], 16)

            split_low(FIRST, 0)
            split_low(FIRST, 1)
            gather(FIRST, 0)

            def step(e, g):
                ne, ng = following(e, g)
                if ne:
                    gather(ne, ng)
                after = later(e, 1)
                if after and g in (1, 2):
                    split_low(after, g - 1)
                pe_, pg = preceding(e, g)
                if pe_:
                    scatter(pe_, pg)

            over_experts(pool, step)
            scatter(LAST, NG - 1)
            for i in range(2):
                pool.wait_ge(added[i], EXPERTS * 16 * GT * NG // 2)

        @block.tensor
        def _(pe):
            def list_tokens(e, c):
                if c == 0:
                    wait(pe, rhs_ready, 1, e, 1)
                    wait(pe, index_ready, 1, e)
                wait(pe, isp_ready, NCH, e, c + 1)
                for t in range(OHT):
                    n = c * OHT + t
                    last = nc.tensor.matmul(bank[7][0:P, 0:2 * EXPERTS], is_p[c % 2][:, :, t], list_rhs[:, :, n],
                                            start=(n == 0), stop=(n == TILES - 1))
                last.then_inc(list_done, 1)

            def transpose(e, g, part):
                if part == 0:
                    wait(pe, gathered[g % 2], 16 * GT * NG // 2, e, 16 * GT * (g // 2 + 1))
                    wait(pe, xbl_ready, NG, e, g)
                else:
                    wait(pe, xal_ready, NG, e, g + 1)
                apart(pe)
                c0, m = ((0, DA), (DA, DB))[part]
                for j in range(GT):
                    last = nc.tensor.transpose(bank[6][0:m, j * P:(j + 1) * P], xg[g % 2][:, j, c0:c0 + m], ident[0:P, 0:P])
                last.then_inc(tr_done, 1)

            def up(e, g, f):
                if f == 0:
                    wait(pe, split_ready, 1, e, 1)
                    wait(pe, xal_ready, NG, e, g + 1)
                    wait(pe, xbl_ready, NG, e, g + 1)
                p, s, cols = e.par, g % 2, slice(f * 128, (f + 1) * 128)
                for w, (a_h, a_l, b_h, b_l) in enumerate(((ga_h, ga_l, gb_h, gb_l), (ua_h, ua_l, ub_h, ub_l))):
                    wait(pe, (silu_ready, hf_ready)[w], NG * NF, e, NF * g + f - 1)
                    to = bank[2 * (f % 2) + w][:, 0:G]
                    nc.tensor.matmul(to, a_h[p][:, cols], xa_h[s][:, :], start=True, stop=False)
                    nc.tensor.matmul(to, a_l[p][:, cols], xa_h[s][:, :], start=False, stop=False)
                    nc.tensor.matmul(to, a_h[p][:, cols], xa_l[s][:, :], start=False, stop=False)
                    nc.tensor.matmul(to, b_h[p][:, cols], xb[s][:, :], start=False, stop=False)
                    nc.tensor.matmul(to, b_l[p][:, cols], xb[s][:, :], start=False, stop=True).then_inc(gu_done, 1)

            def down(e, g):
                wait(pe, hl_ready, NG * NF, e, NF * (g + 1))
                for j in range(GT):
                    wait(pe, yo_ready, NG * GT, e, GT * g + j - 1)
                    cols = slice(j * P, (j + 1) * P)
                    to = bank[4 + j % 2]
                    for f in range(NF):
                        nc.tensor.matmul(to[0:P, 0:2 * D], h_h[g % 2][:, f, cols], wd[e.par][:, f, :], start=(f == 0), stop=False)
                        last = nc.tensor.matmul(to[0:P, 0:D], h_l[g % 2][:, f, cols], wd[e.par][:, f, 0:D],
                                                start=False, stop=(f == NF - 1))
                    last.then_inc(down_done, 1)

            for c in range(NCH):
                list_tokens(FIRST, c)
            transpose(FIRST, 0, 0)
            transpose(FIRST, 0, 1)

            def step(e, g):
                ne, ng = following(e, g)
                after = later(e, 1)
                for f in range(NF):
                    up(e, g, f)
                    if f == 1:
                        pe_, pg = preceding(e, g)
                        if pe_:
                            down(pe_, pg)
                    if f == 2 and ne:
                        transpose(ne, ng, 0)
                    if f == 4 and ne:
                        transpose(ne, ng, 1)
                    if after and (g, f - 1) in AT:
                        list_tokens(after, AT[g, f - 1])

            over_experts(pe, step)
            down(LAST, NG - 1)

        @block.scalar
        def _(act):
            def x_high(e, g, part):
                wait(act, tr_done, 2 * NG, e, 2 * g + part + 1)
                wait(act, gu_done, 2 * NF * NG, e, 2 * NF * (g - 1))
                if part == 0:
                    nc.scalar.copy(xa_h[g % 2][:, :], bank[6][:, 0:G]).then_inc(xah_ready, 1)
                else:
                    nc.scalar.copy(xb[g % 2][0:DB, :], bank[6][0:DB, 0:G]).then_inc(xbh_ready, 1)

            def gate(e, g, f):
                wait(act, gu_done, 2 * NF * NG, e, 2 * (NF * g + f) + 1)
                wait(act, hf_ready, NF * NG, e, NF * g + f - 1)
                nc.scalar.activation(silu[f % 2][:, :], bank[2 * (f % 2)][:, 0:G], ACT.Silu).then_inc(silu_ready, 1)

            def h_high(e, g, f):
                wait(act, hf_ready, NF * NG, e, NF * g + f + 1)
                wait(act, down_done, NG * GT, e, GT * (g - 1))
                nc.scalar.copy(h_h[g % 2][:, f, :], hf[f % 2][:, :]).then_inc(hh_ready, 1)

            def y_low(e, g):
                for j in range(GT):
                    wait(act, down_done, NG * GT, e, GT * g + j + 1)
                    wait(act, score_ready, NG, e, g + 1)
                    wait(act, yo_ready, NG * GT, e, GT * g + j - 1)
                    nc.scalar.mul(yb[j % 2][:, :], bank[4 + j % 2][0:P, D:2 * D], score[g % 2][:, j:j + 1]).then_inc(yb_ready, 1)

            def split_high(e, n):
                if n == 0:
                    wait(act, weights_in, 16 * NLOAD, e, 16 * NLOAD)
                    wait(act, down_done, NG * GT, e, less=1)
                if n < 4:
                    high, raw = ((ga_h, raw_ga), (ua_h, raw_ua), (gb_h, raw_gb), (ub_h, raw_ub))[n]
                    last = nc.scalar.copy(high[e.par][:, :], raw[:, :])
                else:
                    last = nc.scalar.copy(wd[e.par][:, :, 0:D], raw_d[:, :, :])
                last.then_inc(high_ready, 1)

            for n in range(NHIGH):
                split_high(FIRST, n)
            x_high(FIRST, 0, 0)
            x_high(FIRST, 0, 1)

            def step(e, g):
                ne, ng = following(e, g)
                gate(e, g, 0)
                gate(e, g, 1)
                h_high(e, g, 0)
                h_high(e, g, 1)
                pe_, pg = preceding(e, g)
                if pe_:
                    y_low(pe_, pg)
                for f in range(2, NF):
                    gate(e, g, f)
                    h_high(e, g, f)
                    if f in (2, 4) and ne:
                        x_high(ne, ng, f // 2 - 1)
                    if later(e, 1) and f > 2 and 3 * g + f - 3 < NHIGH:
                        split_high(later(e, 1), 3 * g + f - 3)

            over_experts(act, step)
            y_low(LAST, NG - 1)

        @block.vector
        def _(dve):
            def list_rhs_of(e):
                wait(dve, list_done, NCH, e)
                nc.vector.tensor_tensor(is_q[:, :, :], resident["slot_q"][:, bass.ds(e.n, 1), :].to_broadcast([P, EXPERTS, TILES]),
                                        iota_q[:, :, :], ALU.is_equal).then_inc(isq_ready, 1)
                wait(dve, isq_ready, 1, e, 1)
                nc.vector.tensor_scalar(list_rhs[:, 0:EXPERTS, :], is_q[:, :, :], iota_f[:, P:P + 1], None, ALU.mult)
                nc.vector.tensor_tensor(list_rhs[:, EXPERTS:2 * EXPERTS, :], is_q[:, :, :],
                                        tile_no[:, :].unsqueeze(1).to_broadcast([P, EXPERTS, TILES]), ALU.mult).then_inc(rhs_ready, 1)

            def list_lhs(e, c):
                wait(dve, list_done, NCH, e, c - 1)
                nc.vector.tensor_tensor(
                    is_p[c % 2][:, :, :],
                    resident["slot_p"][:, bass.ds(e.n, 1), c * OHT:(c + 1) * OHT].to_broadcast([P, P, OHT]),
                    iota_p[:, :, :], ALU.is_equal).then_inc(isp_ready, 1)

            def list_end(e):
                wait(dve, list_done, NCH, e, NCH)
                nc.vector.tensor_copy(place[:, :], bank[7][0:P, 0:EXPERTS]).then_inc(place_ready, 1)
                wait(dve, place_ready, 1, e, 1)
                for i in range(2):
                    wait(dve, added[i], 16 * GT * NG // 2, e, less=1)
                nc.vector.scalar_tensor_tensor(out=index[e.par][:, :], in0=bank[7][0:P, EXPERTS:2 * EXPERTS], scalar=float(P),
                                               in1=place[:, :], op0=ALU.mult, op1=ALU.add).then_inc(index_ready, 1)

            def scores(e, g):
                wait(dve, gathered[g % 2], 16 * GT * NG // 2, e, 16 * GT * (g // 2 + 1))
                apart(dve)
                nc.vector.tensor_copy(score[g % 2][:, :], xg[g % 2][:, :, bass.ds(e.n + D, 1)].rearrange("p j a -> p (j a)")).then_inc(score_ready, 1)

            def x_low(e, g, part):
                if part == 0:
                    wait(dve, xah_ready, NG, e, g + 1)
                    nc.vector.tensor_tensor(xa_l[g % 2][:, :], bank[6][:, 0:G], xa_h[g % 2][:, :].bitcast(F32), ALU.subtract).then_inc(xal_ready, 1)
                else:
                    wait(dve, xbh_ready, NG, e, g + 1)
                    nc.vector.tensor_tensor(xb[g % 2][DB:128, :], bank[6][0:DB, 0:G], xb[g % 2][0:DB, :].bitcast(F32), ALU.subtract).then_inc(xbl_ready, 1)

            def product(e, g, f):
                wait(dve, silu_ready, NF * NG, e, NF * g + f + 1)
                wait(dve, gu_done, 2 * NF * NG, e, 2 * (NF * g + f) + 2)
                wait(dve, hl_ready, NF * NG, e, NF * g + f - 1)
                nc.vector.tensor_tensor(hf[f % 2][:, :], silu[f % 2][:, :], bank[2 * (f % 2) + 1][:, 0:G], ALU.mult).then_inc(hf_ready, 1)

            def h_low(e, g, f):
                wait(dve, hh_ready, NF * NG, e, NF * g + f + 1)
                nc.vector.tensor_tensor(h_l[g % 2][:, f, :], hf[f % 2][:, :], h_h[g % 2][:, f, :].bitcast(F32), ALU.subtract).then_inc(hl_ready, 1)

            def y_sum(e, g):
                wait(dve, added[g % 2], 16 * GT * NG // 2, e, 16 * GT * (g // 2))
                for j in range(GT):
                    wait(dve, yb_ready, NG * GT, e, GT * g + j + 1)
                    nc.vector.scalar_tensor_tensor(out=yo[g % 2][:, j, :], in0=bank[4 + j % 2][0:P, 0:D], scalar=score[g % 2][:, j:j + 1],
                                                   in1=yb[j % 2][:, :], op0=ALU.mult, op1=ALU.add).then_inc(yo_ready, 1)

            list_rhs_of(FIRST)
            for c in range(NCH):
                list_lhs(FIRST, c)
            list_end(FIRST)
            scores(FIRST, 0)
            x_low(FIRST, 0, 0)
            x_low(FIRST, 0, 1)
            list_rhs_of(later(FIRST, 1))

            def step(e, g):
                ne, ng = following(e, g)
                after = later(e, 1)
                product(e, g, 0)
                product(e, g, 1)
                h_low(e, g, 0)
                h_low(e, g, 1)
                pe_, pg = preceding(e, g)
                if pe_:
                    y_sum(pe_, pg)
                for f in range(2, NF):
                    product(e, g, f)
                    if after and (g, f) in AT:
                        list_lhs(after, AT[g, f])
                    h_low(e, g, f)
                    if f == 2 and ne:
                        scores(ne, ng)
                    if f in (2, 4) and ne:
                        x_low(ne, ng, f // 2 - 1)
                if g == NG - 2 and after:
                    list_end(after)
                if g == NG - 1 and later(e, 2):
                    list_rhs_of(later(e, 2))

            over_experts(dve, step)
            y_sum(LAST, NG - 1)


def audio_tower(nc, io):
    with ExitStack() as ctx:
        def sb(name, shape, dt=F32):
            return ctx.enter_context(nc.sbuf_tensor(name, shape, dt))

        resident = {
            "ident": sb("ident", [128, 128]),
            "slot_p": sb("slot_p", [P, EXPERTS, TILES], BF16), "slot_q": sb("slot_q", [P, EXPERTS, TILES], BF16),
            "iota_f": sb("iota_f", [P, P + 1 + EXPERTS + TILES]),
            "iota_p": sb("iota_p", [P, P, OHT], BF16), "iota_q": sb("iota_q", [P, EXPERTS, TILES], BF16),
            "tile_no": sb("tile_no", [P, TILES], BF16),
        }
        with ExitStack() as early:
            def sb_early(name, shape, dt=F32):
                return early.enter_context(nc.sbuf_tensor(name, shape, dt))

            parts = ("ga_h", "ga_l", "gb_h", "gb_l", "ua_h", "ua_l", "ub_h", "ub_l")
            shared = {
                "scores_tm": sb_early("scores_tm", [P, TILES, EXPERTS]),
                "shared_raw": [sb_early(f"sh_raw_{n}", [128, FS]) for n in ("ga", "gb", "ua", "ub")] + [sb_early("sh_raw_d", [128, FS // 128, D])],
                "shared_parts": [sb_early(f"sh_{n}", [128, FS], F32R) for n in parts] + [sb_early("sh_wd", [128, FS // 128, 2 * D], F32R)],
            }
            tower_phase(nc, io, resident | shared)
            shared_phase(nc, io, resident | shared)
        experts_phase(nc, io, resident)


_IO = ["framesT", "dft", "mel", "dct", "w_proj", "b_proj", "wqkv", "wout", "b_out", "gateT", "wsgT", "wsuT", "wsdT",
       "wgT", "wuT", "wdT", "ident", "same_head", "head_of", "same_expert", "before", "iotas"]


def _constants():
    import numpy as np

    n = np.arange(FRAME)
    window = 0.54 - 0.46 * np.cos(2.0 * np.pi * n / (FRAME - 1))
    angle = 2.0 * np.pi * np.outer(n, np.arange(BINS // 2)) / FRAME
    dft = np.concatenate([np.cos(angle), -np.sin(angle)], axis=1) * window[:, None]
    d, r = np.arange(D), np.arange(128)
    iotas = np.concatenate([np.tile(np.arange(1, P + 1), (P, 1)), np.arange(P)[:, None],
                            np.tile(np.arange(EXPERTS), (P, 1)), np.tile(np.arange(TILES), (P, 1))], axis=1)
    f = np.float32
    same = r[:, None] % EXPERTS == r[None, :] % EXPERTS
    return {
        "dft": dft.astype(f),
        "ident": np.eye(128, dtype=f),
        "same_head": (d[:, None] // DH == d[None, :] // DH).astype(f),
        "head_of": (d[:, None] // DH == np.arange(HEADS)[None, :]).astype(f),
        "same_expert": same.astype(f),
        "before": (same & (r[:, None] < r[None, :])).astype(f),
        "iotas": iotas.astype(f),
    }


def _layout(a):
    import numpy as np

    step = (a["x"].shape[1] - FRAME) // (FRAMES - 1)
    at = np.arange(FRAMES)[:, None] * step + np.arange(FRAME)[None, :]
    return {
        "framesT": a["x"][:, at].reshape(TOKENS, FRAME).T,
        "mel": np.concatenate([a["L0_tok_mel_filters"].T] * 2, axis=0),
        "dct": a["L0_tok_dct"],
        "w_proj": a["L0_tok_w_proj"],
        "b_proj": a["L0_tok_b_proj"][None, :],
        "wqkv": a["L0_attn_W_qkv"],
        "wout": a["L0_attn_W_out"],
        "b_out": a["L0_attn_b_out"][None, :],
        "gateT": a["L0_ffn_gate_weight"].T,
        "wsgT": a["L0_ffn_Ws_g"].T,
        "wsuT": a["L0_ffn_Ws_u"].T,
        "wsdT": a["L0_ffn_Ws_d"].T,
        "wgT": a["L0_ffn_Wg"].transpose(0, 2, 1).reshape(EXPERTS * D, FE),
        "wuT": a["L0_ffn_Wu"].transpose(0, 2, 1).reshape(EXPERTS * D, FE),
        "wdT": a["L0_ffn_Wd"].transpose(0, 2, 1).reshape(EXPERTS * FE, D),
    }


def kernel(**inputs):
    import concourse.bacc as bacc
    import numpy as np
    from concourse.bass_utils import run_bass_kernel_spmd

    laid = _layout({name: np.asarray(a) for name, a in inputs.items()}) | _constants()
    nc = bacc.Bacc("TRN2", target_bir_lowering=False, num_devices=1)
    arrays, io = {}, {}
    for name in _IO:
        a = np.ascontiguousarray(laid[name])
        arrays[f"in_{name}"] = a
        io[name] = nc.dram_tensor(f"in_{name}", a.shape, mybir.dt.from_np(a.dtype), kind="ExternalInput").ap()
    io["x2T"] = nc.dram_tensor("x2T", (D, TOKENS), F32, kind="Internal").ap()
    io["rows"] = nc.dram_tensor("rows", (TOKENS, ROW), F32, kind="Internal").ap()
    io["out"] = nc.dram_tensor("out", (TOKENS, D), F32, kind="ExternalOutput").ap()
    audio_tower(nc, io)
    result = run_bass_kernel_spmd(nc, [arrays], core_ids=[0])
    return result.results[0]["out"].reshape(BATCH, FRAMES, D)
```
